# Optimizing a Trainium2 kernel written in Bass

```python
import numpy as np
import jax
import jax.numpy as jnp

def _softmax(x, axis=-1):
    return jax.nn.softmax(x, axis=axis)

def _gelu(x):
    return jax.nn.gelu(x, approximate=True)

def _silu(x):
    return jax.nn.silu(x)

def _sigmoid(x):
    return jax.nn.sigmoid(x)

def _layernorm(x, axis=-1, eps=1e-05):
    m = jnp.mean(x, axis=axis, keepdims=True)
    v = jnp.var(x, axis=axis, keepdims=True)
    return (x - m) / jnp.sqrt(v + eps)

def _scatter_add(tgt, idx, src, axis=0):
    return tgt.at[idx].add(src)

def _segment_sum(src, seg, n):
    return jax.ops.segment_sum(src, seg, n)
kernel_name = 'mk_cond_resid_d4_seqx_r4_e25184'

def setup_inputs(seed: int=0):
    np.random.seed(seed)
    _w = jnp.asarray

    def _rec_inputs():
        import jax
        import jax.numpy as jnp
        _rk = jax.random.key(seed)
        x = -0.000125 + 0.9999 * jax.random.normal(jax.random.fold_in(_rk, 1), (16, 256, 256), jnp.float32)
        _lenS = 256 - jax.random.randint(jax.random.fold_in(_rk, 7), (16,), 0, max(1, 256 // 4) + 1, jnp.int32)
        _lenS2 = 256 - jax.random.randint(jax.random.fold_in(_rk, 8), (16,), 0, max(1, 256 // 4) + 1, jnp.int32)
        cond_256 = -0.0209273 + 1.04763 * jax.random.normal(jax.random.fold_in(_rk, 11), (16, 64), jnp.float32)
        cond_64 = 0.0223021 + 1.01123 * jax.random.normal(jax.random.fold_in(_rk, 12), (16, 64), jnp.float32)
        _validS = jnp.arange(256)[None, :] < _lenS[:, None]
        _validS2 = jnp.arange(256)[None, :] < _lenS2[:, None]
        _causal = jnp.tril(jnp.ones((256, 256), dtype=bool))
        mask_SxS_bk1 = jnp.broadcast_to(_validS[0:1, :], (256, 256))
        return (x, cond_256, cond_64, mask_SxS_bk1)
    x, cond_256, cond_64, mask_SxS_bk1 = _rec_inputs()

    def _L0_cond_setup():
        import math
        import jax, jax.numpy as jnp
        import numpy as np
        from jax.scipy.linalg import cholesky, solve_triangular
        B, S, D, O, K, R = (4, 2048, 256, 256, 64, 64)

        def build_dct_basis(dim: int, num_bases: int) -> np.ndarray:
            num_bases = min(num_bases, dim)
            positions = np.arange(dim, dtype=np.float32)[None, :]
            modes = np.arange(num_bases, dtype=np.float32)[:, None]
            basis = np.cos(math.pi / float(dim) * (positions + 0.5) * modes)
            basis[0] = basis[0] / math.sqrt(2.0)
            basis = basis * math.sqrt(2.0 / float(dim))
            return basis.astype(np.float32)

        def _orthogonalize_mode_to_rank(raw: jnp.ndarray) -> jnp.ndarray:
            raw = raw.astype(jnp.float32)
            gram = raw.T @ raw
            eye = jnp.eye(raw.shape[1], dtype=jnp.float32)
            chol = cholesky(gram + 0.0001 * eye, lower=True)
            inv_chol = solve_triangular(chol, eye, lower=True)
            q = raw @ inv_chol.T
            signs = jnp.sign(jnp.sum(q * raw, axis=0, keepdims=True))
            signs = jnp.where(signs == 0, jnp.ones_like(signs), signs)
            return q * signs
        key = jax.random.key(seed)
        k1, k2, k3, k4, k5 = jax.random.split(key, 5)
        x = jax.random.normal(k1, (B, S, D), dtype=jnp.float32)
        spectral_coeff = jax.random.normal(k2, (B, K), dtype=jnp.float32)
        rank_coeff = jax.random.normal(k3, (B, R), dtype=jnp.float32)
        input_basis = jnp.asarray(build_dct_basis(D, K))
        diag = min(K, R)
        mode_to_rank = 0.02 * jax.random.normal(k4, (K, R), dtype=jnp.float32)
        mode_to_rank = mode_to_rank.at[:diag, :diag].add(jnp.eye(diag, dtype=jnp.float32))
        output_basis = 0.02 * jax.random.normal(k5, (R, O), dtype=jnp.float32)
        return {'x': x, 'spectral_coeff': spectral_coeff, 'rank_coeff': rank_coeff, 'input_basis': input_basis, 'mode_to_rank': mode_to_rank, 'output_basis': output_basis}
    _L0_cond_all = _L0_cond_setup()
    _L0_cond_in = {k: v for k, v in _L0_cond_all.items() if k in ('input_basis', 'mode_to_rank', 'output_basis')}
    del _L0_cond_all

    def _L1_cond_setup():
        import jax, jax.numpy as jnp
        import numpy as np
        D_MODEL = 256
        D_T = 64
        N_HEADS = 16
        HIDDEN = 4 * D_MODEL
        EPS = 1e-06

        def _tc_rmsnorm(x, t, gw, gb, bw, bb):
            g = (t @ gw.T + gb)[:, None, :]
            b = (t @ bw.T + bb)[:, None, :]
            inv_rms = jax.lax.rsqrt(jnp.mean(x * x, axis=-1, keepdims=True) + EPS)
            return g * x * inv_rms + b

        def _attention(x, Wq, Wk, Wv, Wo):
            B, L, D = x.shape
            H = N_HEADS
            dh = D // H
            scale = np.sqrt(dh).astype(np.float32)
            q = (x @ Wq.T).reshape(B, L, H, dh)
            k = (x @ Wk.T).reshape(B, L, H, dh)
            v = (x @ Wv.T).reshape(B, L, H, dh)
            attn = jnp.einsum('blhd,bmhd->bhlm', q, k) / scale
            p = jax.nn.softmax(attn, axis=-1)
            o = jnp.einsum('bhlm,bmhd->blhd', p, v).reshape(B, L, D)
            return o @ Wo.T

        def _swiglu(x, gate_w, hid_w, out_w):
            return jax.nn.silu(x @ gate_w.T) * (x @ hid_w.T) @ out_w.T
        key = jax.random.key(seed)
        ks = jax.random.split(key, 20)
        B, L = (8, 256)
        s_d = 1.0 / np.sqrt(D_MODEL)
        s_t = 1.0 / np.sqrt(D_T)
        s_h = 1.0 / np.sqrt(HIDDEN)
        return {'x': jax.random.normal(ks[0], (B, L, D_MODEL), jnp.float32), 't': jax.random.normal(ks[1], (B, D_T), jnp.float32), 'Wq': jax.random.normal(ks[2], (D_MODEL, D_MODEL), jnp.float32) * s_d, 'Wk': jax.random.normal(ks[3], (D_MODEL, D_MODEL), jnp.float32) * s_d, 'Wv': jax.random.normal(ks[4], (D_MODEL, D_MODEL), jnp.float32) * s_d, 'Wo': jax.random.normal(ks[5], (D_MODEL, D_MODEL), jnp.float32) * s_d, 'g1w': jax.random.normal(ks[6], (D_MODEL, D_T), jnp.float32) * s_t, 'g1b': jnp.ones((D_MODEL,), jnp.float32), 'b1w': jax.random.normal(ks[7], (D_MODEL, D_T), jnp.float32) * s_t, 'b1b': jnp.zeros((D_MODEL,), jnp.float32), 'g2w': jax.random.normal(ks[8], (D_MODEL, D_T), jnp.float32) * s_t, 'g2b': jnp.ones((D_MODEL,), jnp.float32), 'b2w': jax.random.normal(ks[9], (D_MODEL, D_T), jnp.float32) * s_t, 'b2b': jnp.zeros((D_MODEL,), jnp.float32), 'gate_w': jax.random.normal(ks[10], (HIDDEN, D_MODEL), jnp.float32) * s_d, 'hid_w': jax.random.normal(ks[11], (HIDDEN, D_MODEL), jnp.float32) * s_d, 'out_w': jax.random.normal(ks[12], (D_MODEL, HIDDEN), jnp.float32) * s_h}
    _L1_cond_all = _L1_cond_setup()
    _L1_cond_in = {k: v for k, v in _L1_cond_all.items() if k in ('Wq', 'Wk', 'Wv', 'Wo', 'g1w', 'g1b', 'b1w', 'b1b', 'g2w', 'g2b', 'b2w', 'b2b', 'gate_w', 'hid_w', 'out_w')}
    del _L1_cond_all

    def _L2_cond_setup():
        import jax, jax.numpy as jnp
        import numpy as np
        B, S, E, H, CD = (4, 256, 256, 16, 64)
        HD = E // H
        FIELD_COHERENCE = 0.7
        COH_THRESHOLD = 0.5
        FIELD_COUPLING = 0.3

        def _layernorm(x, g, b, eps=1e-05):
            mu = x.mean(-1, keepdims=True)
            var = ((x - mu) ** 2).mean(-1, keepdims=True)
            return (x - mu) * jax.lax.rsqrt(var + eps) * g + b
        key = jax.random.key(seed)
        ks = jax.random.split(key, 10)
        s = 0.02
        f32 = jnp.float32
        return {'x': jax.random.normal(ks[0], (B, S, E), f32), 'consciousness_state': jax.random.normal(ks[1], (B, CD), f32), 'Wqkv': jax.random.normal(ks[2], (3 * E, E), f32) * s, 'bqkv': jnp.zeros((3 * E,), f32), 'Wout': jax.random.normal(ks[3], (E, E), f32) * s, 'bout': jnp.zeros((E,), f32), 'Wc1': jax.random.normal(ks[4], (E, E + CD), f32) * s, 'bc1': jnp.zeros((E,), f32), 'Wc2': jax.random.normal(ks[5], (H, E), f32) * s, 'bc2': jnp.zeros((H,), f32), 'We1': jax.random.normal(ks[6], (E, CD), f32) * s, 'be1': jnp.zeros((E,), f32), 'We2': jax.random.normal(ks[7], (E, E), f32) * s, 'be2': jnp.zeros((E,), f32), 'ln_g': jnp.ones((E,), f32), 'ln_b': jnp.zeros((E,), f32)}
    _L2_cond_all = _L2_cond_setup()
    _L2_cond_in = {k: v for k, v in _L2_cond_all.items() if k in ('Wqkv', 'bqkv', 'Wout', 'bout', 'Wc1', 'bc1', 'Wc2', 'bc2', 'We1', 'be1', 'We2', 'be2', 'ln_g', 'ln_b')}
    del _L2_cond_all

    def _L3_cond_setup():
        import jax, jax.numpy as jnp
        import numpy as np
        EPS = 1e-06
        key = jax.random.key(seed)
        ks = jax.random.split(key, 8)
        B, S, E, C = (2, 512, 256, 64)
        x = jax.random.normal(ks[0], (B, S, E), dtype=jnp.float32)
        mask = jnp.triu(jnp.ones((S, S), dtype=bool), k=1)
        conditioning = jax.random.normal(ks[1], (B, C), dtype=jnp.float32)
        sc = 1.0 / np.sqrt(E)
        Wq = jax.random.normal(ks[2], (E, E), dtype=jnp.float32) * sc
        Wk = jax.random.normal(ks[3], (E, E), dtype=jnp.float32) * sc
        Wv = jax.random.normal(ks[4], (E, E), dtype=jnp.float32) * sc
        Wo = jax.random.normal(ks[5], (E, E), dtype=jnp.float32) * sc
        rms_scale = jnp.ones((E,), dtype=jnp.float32)
        Wc = jax.random.normal(ks[6], (2 * E, C), dtype=jnp.float32) * 0.02
        bc = jax.random.normal(ks[7], (2 * E,), dtype=jnp.float32) * 0.02
        return {'x': x, 'mask': mask, 'conditioning': conditioning, 'Wq': Wq, 'Wk': Wk, 'Wv': Wv, 'Wo': Wo, 'rms_scale': rms_scale, 'Wc': Wc, 'bc': bc}
    _L3_cond_all = _L3_cond_setup()
    _L3_cond_in = {k: v for k, v in _L3_cond_all.items() if k in ('Wq', 'Wk', 'Wv', 'Wo', 'rms_scale', 'Wc', 'bc')}
    del _L3_cond_all
    return {'x': x, 'cond_256': cond_256, 'cond_64': cond_64, 'mask_SxS_bk1': mask_SxS_bk1, 'L0_cond_input_basis': _L0_cond_in['input_basis'], 'L0_cond_mode_to_rank': _L0_cond_in['mode_to_rank'], 'L0_cond_output_basis': _L0_cond_in['output_basis'], 'L1_cond_Wq': _L1_cond_in['Wq'], 'L1_cond_Wk': _L1_cond_in['Wk'], 'L1_cond_Wv': _L1_cond_in['Wv'], 'L1_cond_Wo': _L1_cond_in['Wo'], 'L1_cond_g1w': _L1_cond_in['g1w'], 'L1_cond_g1b': _L1_cond_in['g1b'], 'L1_cond_b1w': _L1_cond_in['b1w'], 'L1_cond_b1b': _L1_cond_in['b1b'], 'L1_cond_g2w': _L1_cond_in['g2w'], 'L1_cond_g2b': _L1_cond_in['g2b'], 'L1_cond_b2w': _L1_cond_in['b2w'], 'L1_cond_b2b': _L1_cond_in['b2b'], 'L1_cond_gate_w': _L1_cond_in['gate_w'], 'L1_cond_hid_w': _L1_cond_in['hid_w'], 'L1_cond_out_w': _L1_cond_in['out_w'], 'L2_cond_Wqkv': _L2_cond_in['Wqkv'], 'L2_cond_bqkv': _L2_cond_in['bqkv'], 'L2_cond_Wout': _L2_cond_in['Wout'], 'L2_cond_bout': _L2_cond_in['bout'], 'L2_cond_Wc1': _L2_cond_in['Wc1'], 'L2_cond_bc1': _L2_cond_in['bc1'], 'L2_cond_Wc2': _L2_cond_in['Wc2'], 'L2_cond_bc2': _L2_cond_in['bc2'], 'L2_cond_We1': _L2_cond_in['We1'], 'L2_cond_be1': _L2_cond_in['be1'], 'L2_cond_We2': _L2_cond_in['We2'], 'L2_cond_be2': _L2_cond_in['be2'], 'L2_cond_ln_g': _L2_cond_in['ln_g'], 'L2_cond_ln_b': _L2_cond_in['ln_b'], 'L3_cond_Wq': _L3_cond_in['Wq'], 'L3_cond_Wk': _L3_cond_in['Wk'], 'L3_cond_Wv': _L3_cond_in['Wv'], 'L3_cond_Wo': _L3_cond_in['Wo'], 'L3_cond_rms_scale': _L3_cond_in['rms_scale'], 'L3_cond_Wc': _L3_cond_in['Wc'], 'L3_cond_bc': _L3_cond_in['bc']}

def reference(x, cond_256, cond_64, mask_SxS_bk1, L0_cond_input_basis, L0_cond_mode_to_rank, L0_cond_output_basis, L1_cond_Wq, L1_cond_Wk, L1_cond_Wv, L1_cond_Wo, L1_cond_g1w, L1_cond_g1b, L1_cond_b1w, L1_cond_b1b, L1_cond_g2w, L1_cond_g2b, L1_cond_b2w, L1_cond_b2b, L1_cond_gate_w, L1_cond_hid_w, L1_cond_out_w, L2_cond_Wqkv, L2_cond_bqkv, L2_cond_Wout, L2_cond_bout, L2_cond_Wc1, L2_cond_bc1, L2_cond_Wc2, L2_cond_bc2, L2_cond_We1, L2_cond_be1, L2_cond_We2, L2_cond_be2, L2_cond_ln_g, L2_cond_ln_b, L3_cond_Wq, L3_cond_Wk, L3_cond_Wv, L3_cond_Wo, L3_cond_rms_scale, L3_cond_Wc, L3_cond_bc):
    import jax
    import jax.numpy as jnp

    def _L0_cond_ref(x, spectral_coeff, rank_coeff, input_basis, mode_to_rank, output_basis):
        import math
        import jax, jax.numpy as jnp
        import numpy as np
        from jax.scipy.linalg import cholesky, solve_triangular
        B, S, D, O, K, R = (4, 2048, 256, 256, 64, 64)

        def build_dct_basis(dim: int, num_bases: int) -> np.ndarray:
            num_bases = min(num_bases, dim)
            positions = np.arange(dim, dtype=np.float32)[None, :]
            modes = np.arange(num_bases, dtype=np.float32)[:, None]
            basis = np.cos(math.pi / float(dim) * (positions + 0.5) * modes)
            basis[0] = basis[0] / math.sqrt(2.0)
            basis = basis * math.sqrt(2.0 / float(dim))
            return basis.astype(np.float32)

        def _orthogonalize_mode_to_rank(raw: jnp.ndarray) -> jnp.ndarray:
            raw = raw.astype(jnp.float32)
            gram = raw.T @ raw
            eye = jnp.eye(raw.shape[1], dtype=jnp.float32)
            chol = cholesky(gram + 0.0001 * eye, lower=True)
            inv_chol = solve_triangular(chol, eye, lower=True)
            q = raw @ inv_chol.T
            signs = jnp.sign(jnp.sum(q * raw, axis=0, keepdims=True))
            signs = jnp.where(signs == 0, jnp.ones_like(signs), signs)
            return q * signs
        mtr = _orthogonalize_mode_to_rank(mode_to_rank).astype(x.dtype)
        proj = jnp.einsum('bsd,kd->bsk', x, input_basis.astype(x.dtype))
        proj = proj * spectral_coeff[:, None, :]
        hidden = jnp.einsum('bsk,kr->bsr', proj, mtr)
        hidden = hidden * rank_coeff[:, None, :]
        out = jnp.einsum('bsr,ro->bso', hidden, output_basis.astype(x.dtype))
        return out

    def _L1_cond_ref(x, t, Wq, Wk, Wv, Wo, g1w, g1b, b1w, b1b, g2w, g2b, b2w, b2b, gate_w, hid_w, out_w):
        import jax, jax.numpy as jnp
        import numpy as np
        D_MODEL = 256
        D_T = 64
        N_HEADS = 16
        HIDDEN = 4 * D_MODEL
        EPS = 1e-06

        def _tc_rmsnorm(x, t, gw, gb, bw, bb):
            g = (t @ gw.T + gb)[:, None, :]
            b = (t @ bw.T + bb)[:, None, :]
            inv_rms = jax.lax.rsqrt(jnp.mean(x * x, axis=-1, keepdims=True) + EPS)
            return g * x * inv_rms + b

        def _attention(x, Wq, Wk, Wv, Wo):
            B, L, D = x.shape
            H = N_HEADS
            dh = D // H
            scale = np.sqrt(dh).astype(np.float32)
            q = (x @ Wq.T).reshape(B, L, H, dh)
            k = (x @ Wk.T).reshape(B, L, H, dh)
            v = (x @ Wv.T).reshape(B, L, H, dh)
            attn = jnp.einsum('blhd,bmhd->bhlm', q, k) / scale
            p = jax.nn.softmax(attn, axis=-1)
            o = jnp.einsum('bhlm,bmhd->blhd', p, v).reshape(B, L, D)
            return o @ Wo.T

        def _swiglu(x, gate_w, hid_w, out_w):
            return jax.nn.silu(x @ gate_w.T) * (x @ hid_w.T) @ out_w.T
        x = x + _attention(_tc_rmsnorm(x, t, g1w, g1b, b1w, b1b), Wq, Wk, Wv, Wo)
        return x + _swiglu(_tc_rmsnorm(x, t, g2w, g2b, b2w, b2b), gate_w, hid_w, out_w)

    def _L2_cond_ref(x, consciousness_state, Wqkv, bqkv, Wout, bout, Wc1, bc1, Wc2, bc2, We1, be1, We2, be2, ln_g, ln_b):
        import jax, jax.numpy as jnp
        import numpy as np
        B, S, E, H, CD = (4, 256, 256, 16, 64)
        HD = E // H
        FIELD_COHERENCE = 0.7
        COH_THRESHOLD = 0.5
        FIELD_COUPLING = 0.3

        def _layernorm(x, g, b, eps=1e-05):
            mu = x.mean(-1, keepdims=True)
            var = ((x - mu) ** 2).mean(-1, keepdims=True)
            return (x - mu) * jax.lax.rsqrt(var + eps) * g + b
        Bb, Ss, Ee = x.shape
        qkv = (x @ Wqkv.T + bqkv).reshape(Bb, Ss, 3, H, HD).transpose(2, 0, 3, 1, 4)
        q, k, v = (qkv[0], qkv[1], qkv[2])
        attn = jax.nn.softmax(jnp.einsum('bhid,bhjd->bhij', q, k) / jnp.sqrt(jnp.float32(HD)), axis=-1)
        cs_exp = jnp.broadcast_to(consciousness_state[:, None, :], (Bb, Ss, CD))
        comb = jnp.concatenate([x, cs_exp], axis=-1)
        coh = jax.nn.sigmoid(jnp.tanh(comb @ Wc1.T + bc1) @ Wc2.T + bc2).transpose(0, 2, 1)
        mod = attn * coh[..., None]
        mod = mod / (mod.sum(-1, keepdims=True) + 1e-08)
        fp = _layernorm(jax.nn.relu(consciousness_state @ We1.T + be1) @ We2.T + be2, ln_g, ln_b)
        pos = jnp.arange(Ss, dtype=jnp.float32)
        inv = 10000.0 ** jnp.repeat(jnp.arange(0, Ee, 2, dtype=jnp.float32) / Ee, 2)
        pe = jnp.sin(pos[:, None] / inv[None, :])
        fa = jax.nn.softmax(jnp.einsum('be,se->bs', fp, pe), axis=-1)
        fi = FIELD_COUPLING * FIELD_COHERENCE
        mod = (1.0 - fi) * mod + fi * fa[:, None, :, None]
        out = jnp.einsum('bhij,bhjd->bhid', mod, v).transpose(0, 2, 1, 3).reshape(Bb, Ss, Ee)
        return out @ Wout.T + bout

    def _L3_cond_ref(x, mask, conditioning, Wq, Wk, Wv, Wo, rms_scale, Wc, bc):
        import jax, jax.numpy as jnp
        import numpy as np
        EPS = 1e-06
        B, S, E = x.shape
        H = 16
        D = E // H
        scale = D ** (-0.5)

        def proj(W):
            return (x @ W.T).reshape(B, S, H, D).transpose(0, 2, 1, 3)
        q, k, v = (proj(Wq), proj(Wk), proj(Wv))
        scores = jnp.einsum('bhsd,bhtd->bhst', q, k) * scale
        scores = jnp.where(mask[None, None, :, :], -jnp.inf, scores)
        attn = jax.nn.softmax(scores, axis=-1)
        out = jnp.einsum('bhst,bhtd->bhsd', attn, v)
        out = out.transpose(0, 2, 1, 3).reshape(B, S, E)
        out = out @ Wo.T
        rms = jnp.sqrt(jnp.mean(out * out, axis=-1, keepdims=True) + EPS)
        xn = out / rms * rms_scale
        mod = jax.nn.silu(conditioning) @ Wc.T + bc
        shift, sc = jnp.split(mod, 2, axis=-1)
        xn = xn * (1.0 + sc[:, None, :]) + shift[:, None, :]
        return xn
    x = x + _L0_cond_ref(x, cond_256, cond_64, L0_cond_input_basis, L0_cond_mode_to_rank, L0_cond_output_basis)
    x = x + _L1_cond_ref(x, cond_256, L1_cond_Wq, L1_cond_Wk, L1_cond_Wv, L1_cond_Wo, L1_cond_g1w, L1_cond_g1b, L1_cond_b1w, L1_cond_b1b, L1_cond_g2w, L1_cond_g2b, L1_cond_b2w, L1_cond_b2b, L1_cond_gate_w, L1_cond_hid_w, L1_cond_out_w)
    x = x + _L2_cond_ref(x, cond_256, L2_cond_Wqkv, L2_cond_bqkv, L2_cond_Wout, L2_cond_bout, L2_cond_Wc1, L2_cond_bc1, L2_cond_Wc2, L2_cond_bc2, L2_cond_We1, L2_cond_be1, L2_cond_We2, L2_cond_be2, L2_cond_ln_g, L2_cond_ln_b)
    x = x + _L3_cond_ref(x, mask_SxS_bk1, cond_256, L3_cond_Wq, L3_cond_Wk, L3_cond_Wv, L3_cond_Wo, L3_cond_rms_scale, L3_cond_Wc, L3_cond_bc)
    return x

_drawn_inputs = setup_inputs


def setup_inputs(seed=0):
    import zlib

    import numpy as np

    out = dict(_drawn_inputs(seed))
    spreads = {'L1_cond_g1b': (1.0, 0.2),
     'L1_cond_b1b': (0.0, 0.1),
     'L1_cond_g2b': (1.0, 0.2),
     'L1_cond_b2b': (0.0, 0.1),
     'L2_cond_bqkv': (0.0, 0.351),
     'L2_cond_bout': (0.0, 0.1),
     'L2_cond_bc1': (0.0, 2.0),
     'L2_cond_bc2': (0.0, 2.0),
     'L2_cond_be1': (0.0, 0.275),
     'L2_cond_be2': (0.0, 0.1),
     'L2_cond_ln_g': (1.0, 0.6),
     'L2_cond_ln_b': (0.0, 0.267),
     'L3_cond_rms_scale': (1.0, 0.2)}
    factors = {'L2_cond_Wc1': 64.0, 'L2_cond_Wc2': 64.0, 'L3_cond_bc': 6.637}
    for name, (base, spread) in spreads.items():
        noise = np.random.default_rng([zlib.crc32(name.encode()), seed]).standard_normal(out[name].shape)
        drawn = base * np.exp(spread * noise) if base else spread * noise
        out[name] = jnp.asarray(drawn.astype(out[name].dtype))
    for name, factor in factors.items():
        out[name] = (out[name] * factor).astype(out[name].dtype)
    return out
```

```python
from contextlib import ExitStack

import numpy as np
import concourse.bass as bass
from concourse import mybir

F32 = mybir.dt.float32
F32R = mybir.dt.float32r
BF16 = mybir.dt.bfloat16
ALU = mybir.AluOpType
ACT = mybir.ActivationFunctionType
AX = mybir.AxisListType.X

P = 128
NBATCH, S, D = 16, 256, 256
H, HD = 16, 16
TC, DC = S // P, D // P
C = 64
CA = C + 1
FF = 1024
FC = FF // P
HG = 4
NG = H // HG
HW = 32
PBUF = 8
LAYERS = (1, 2, 3)
FI = 0.3 * 0.7
BIG = -1e30

SHIFT = 96
SCORE_ROWS, SHIFTED_ROWS = SHIFT, SHIFT + 2

G1, B1, G2, B2, C1, SPEC, RANK, FIELD, SILU = 0, 2, 4, 6, 8, 10, 11, 12, 14
NV = 15


class Event:

    def __init__(self, sem, per):
        self.sem, self.per = sem, per

    def at(self, b, k):
        return b * self.per + k


class Ring:

    def __init__(self, sem, banks, readers):
        self.banks, self.readers, self.uses = banks, readers, list(readers)
        self.full = Event(sem, len(readers))

    def bank(self, use):
        return self.banks[self.uses.index(use) % 3]

    def wait_filled(self, eng, b, use):
        eng.wait_ge(self.full.sem, self.full.at(b, self.uses.index(use) + 1))
        return self.bank(use)

    def wait_free(self, pe, b, use):
        u = self.uses.index(use)
        if u >= 3:
            event, k = self.readers[self.uses[u - 3]]
            pe.wait_ge(event.sem, event.at(b, k))
        else:
            event, _ = self.readers[self.uses[u::3][-1]]
            pe.wait_ge(event.sem, event.at(b, 0))
        return self.bank(use)


def order_of(layer):
    F, B = "front", "back"
    p = lambda a, b: [(B, "probs", h) for h in range(a, b)]
    out = [(F, "load", 0), (B, "vectors", 0)]
    if layer == 1:
        out += [(F, "spec", 0)] + p(0, 2) + [(F, "rank", 0)] + p(2, 4) + [(F, "cond", 0)] + p(4, 8)
    else:
        out += p(0, 4) + [(F, "stage", 0)] + p(4, 8)
    out += [(B, "pv", 0), (F, "xT", 0)] + p(8, 12) + [(F, "qk", 0), (B, "pv", 1), (F, "v", 0)]
    if layer == 2:
        out += [(F, "coh1", 0)]
    out += p(12, 16) + [(B, "pv", 2), (B, "pv", 3)]
    if layer == 2:
        out += [(F, "coh2", 0), (B, "sumv", 0)]
    out += [(B, "tok", 0), (F, "smax", 0), (F, "smax", 1), (B, "oT", 0), (F, "smax", 2), (F, "smax", 3), (B, "wo", 0)]
    if layer == 1:
        out += [(F, "smax", 4), (F, "smax", 5), (F, "smax", 6), (B, "yT", 0), (F, "smax", 7)]
        for f in range(FC):
            out += [(B, "ffn", f), (F, "smax", 8 + f)]
        out += [(F, "max", 0), (B, "down", 0)]
    elif layer == 2:
        out += [(F, "smax", h) for h in range(4, H)] + [(F, "max", 0)]
    else:
        out += [(F, "smax", h) for h in range(4, H)] + [(B, "mod", 0), (F, "max", 0)]
    return out


def cond_resid_kernel(nc, ins, out):
    with ExitStack() as ctx:
        def sb(name, shape, dt=F32):
            return ctx.enter_context(nc.sbuf_tensor(name, shape, dt))

        def sem(name):
            return ctx.enter_context(nc.semaphore(name))

        banks = [ctx.enter_context(nc.psum_tensor(f"bank{i}", [P, 512], F32)) for i in range(8)]
        o_bank = banks[6:8]

        probs = sb("probs", [P, PBUF, TC, S])
        probs_flat = probs[:, :, :, :].rearrange("p h t s -> p (h t s)")

        class Carver:

            def __init__(self, flat):
                self.flat, self.at = flat, 0

            def __call__(self, shape):
                size = int(np.prod(shape[1:]))
                piece = self.flat[0:shape[0], self.at:self.at + size]
                self.at += size
                if len(shape) == 2:
                    return piece
                names = [f"d{i}" for i in range(len(shape) - 1)]
                return piece.rearrange(f"p ({' '.join(names)}) -> p {' '.join(names)}", **dict(zip(names, shape[1:])))

        setup, ffn = Carver(probs_flat), Carver(probs_flat)
        ot_raw = sb("ot_raw", [P, NG, S])
        setup_more = Carver(ot_raw[:, :, :].rearrange("p g s -> p (g s)"))

        ident = sb("ident", [P, P])
        ident_bf = sb("ident_bf", [P, P], BF16)
        below = setup([C, C])
        ones = sb("ones", [P, P])
        raw, raw_t = setup([C, C]), setup([C, C])
        cond_a = sb("cond_a", [CA, NBATCH])
        cond_w = setup([CA, 10, P])
        we1 = setup([CA, D])
        we2 = setup([P, DC, D])
        be2 = setup([1, D])
        ln_gb = setup([NBATCH, 2, D])
        pe_t = setup([P, DC, S])
        w_basis = sb("w_basis", [P, DC, C])
        w_outb = sb("w_outb", [C, D])
        w_gate, w_hid = sb("w_gate", [P, DC, FF]), sb("w_hid", [P, DC, FF])
        wqkvo = {1: sb("wqkvo1", [P, 4, DC, D])}
        for n, over in ((2, w_gate), (3, w_hid)):
            wqkvo[n] = over[:, :, :].rearrange("p a (b d) -> p (a b) d", d=D).rearrange("p (m c) d -> p m c d", c=DC)
        w_down = sb("w_down", [P, FC, D])
        w_c1 = sb("w_c1", [P, DC, D])
        w_c2 = sb("w_c2", [P, DC, H])
        bqk = sb("bqk", [P, 4])
        bv_rows, bout_rows = sb("bv_rows", [P, D]), sb("bout_rows", [P, D])
        bc2_rows = sb("bc2_rows", [P, H])
        w_mod = sb("w_mod", [CA, 2 * D])
        rms_rows = sb("rms_rows", [P, D])
        mask_q, mask_k = sb("mask_q", [P, TC, S], mybir.dt.uint8), sb("mask_k", [P, TC, S], mybir.dt.uint8)
        big_q, big_k = sb("big_q", [P, TC, S], BF16), sb("big_k", [P, TC, S], BF16)
        some_key = sb("some_key", [P, TC])
        half = sb("half", [P, TC])

        xres = sb("xres", [P, NBATCH, TC, D])
        cvec = sb("cvec", [P, NV, NBATCH])

        qs = [sb(f"qs{i}", [P, H, S], F32R) for i in range(2)]
        ks = [sb(f"ks{i}", [P, H, S], F32R) for i in range(2)]
        vp = [sb(f"vp{i}", [P, TC, H, HW]) for i in range(2)]
        coh = [sb(f"coh{i}", [P, TC, H]) for i in range(2)]
        cur_f, cur_b = sb("cur_f", [P, NV]), sb("cur_b", [P, NV])
        x_in, xt_in = sb("x_in", [P, TC, D]), sb("xt_in", [P, DC, S])
        h_spec, h_rank = sb("h_spec", [C, S]), sb("h_rank", [C, S])
        xn = sb("xn", [P, TC, D])
        xt = sb("xt", [P, DC, S])
        qk = sb("qk", [P, 4, S])
        qk_hi, qk_lo = sb("qk_hi", [P, 4, S], F32R), sb("qk_lo", [P, 4, S], F32R)
        rowmax = sb("rowmax", [P, TC, H])
        nm_hi, nm_lo = sb("nm_hi", [H, S], F32R), sb("nm_lo", [H, S], F32R)
        rz = sb("rz", [P, TC, H])
        on = sb("on", [P, TC, D])
        ot = sb("ot", [P, DC, S])
        stat = sb("stat", [P, 3, TC])
        statb = sb("statb", [P, 3, TC])
        y = sb("y", [P, TC, D])
        yn = sb("yn", [P, TC, D])
        yt = sb("yt", [P, DC, S])
        th, act1 = ffn([P, 2, S]), ffn([P, 2, S])
        hm = ffn([P, FC, S])
        c1t = xt_in
        zz, ez = sb("zz", [P, TC, H]), sb("ez", [P, TC, H])
        mod_l = sb("mod_l", [CA, P])
        mod_a, mod_s = x_in[:, 0, :], x_in[:, 1, :]

        gj, gj_row = setup_more([C, 2 * C]), setup_more([C, 2 * C])
        gj_c = setup([C, 4])
        tinv, tinv_t, qmat, sgn = (setup([C, C]) for _ in range(4))
        mtr = sb("mtr", [C, P])
        keys_left = xn
        a1 = setup([P, DC, NBATCH])
        fld = setup_more([NBATCH, 3, D])
        fs = setup([NBATCH, 8])
        fld_t = setup([P, DC, NBATCH])
        th_c = setup([C, NBATCH])

        s_ld0, s_ld = sem("s_ld0"), {n: sem(f"s_ld{n}") for n in LAYERS}
        s_memset = sem("s_memset")
        s_vch, s_pe0, s_act0, s_pool0 = sem("s_vch"), sem("s_pe0"), sem("s_act0"), sem("s_pool0")
        s_gj_row, s_gj_bc, s_gj_up = sem("s_gj_row"), sem("s_gj_bc"), sem("s_gj_up")
        s_setup = sem("s_setup")

        def ev(name, per):
            return Event(sem(name), per)

        x_loaded, h_spec_ok, h_rank_ok, x1_ok = ev("x_loaded", 32), ev("h_spec_ok", 1), ev("h_rank_ok", 1), ev("x1_ok", 1)
        sq1, ms1, inv1, xn_ok = ev("sq1", TC), ev("ms1", 1), ev("inv1", 1), ev("xn_ok", TC)
        y_ok, sq2, ms2, inv2 = ev("y_ok", 1), ev("sq2", TC), ev("ms2", 1), ev("inv2", 1)
        yn_ok, yt_ok, xy_ok = ev("yn_ok", TC), ev("yt_ok", DC), ev("xy_ok", 1)
        th_ok, act1_ok, hm_ok = ev("th_ok", FC), ev("act1_ok", FC), ev("hm_ok", FC)
        c1_ok, zz_ok, ez_ok, coh_ok = ev("c1_ok", DC), ev("zz_ok", 1), ev("ez_ok", 1), ev("coh_ok", 3)
        rz_coh, on_field, attn2_ok = ev("rz_coh", TC), ev("on_field", TC), ev("attn2_ok", 1)
        rz_some, attn3_ok, sq3, ms3, inv3 = ev("rz_some", TC), ev("attn3_ok", 1), ev("sq3", TC), ev("ms3", 1), ev("inv3", 1)
        mod_l_ok, mod_ok, mod_sum, stored = ev("mod_l_ok", 1), ev("mod_ok", 2), ev("mod_sum", 4), ev("stored", 16)

        class Layer:

            def __init__(self, n):
                self.n = n
                self.cur_f, self.cur_b = ev(f"cur_f{n}", 1), ev(f"cur_b{n}", 1)
                self.staged, self.xt = ev(f"staged{n}", 1), ev(f"xt{n}", DC)
                self.q, self.k, self.vp = ev(f"q{n}", 1), ev(f"k{n}", 1), ev(f"vp{n}", 1)
                self.qk_hi, self.qk_lo, self.stacked = ev(f"qk_hi{n}", 1), ev(f"qk_lo{n}", 1), ev(f"stacked{n}", 16 * 12)
                self.rowmax, self.nm, self.shifted = ev(f"rowmax{n}", H), ev(f"nm{n}", 2), ev(f"shifted{n}", 32)
                self.probs, self.pv, self.o_raw = ev(f"probs{n}", H), ev(f"pv{n}", NG), ev(f"o_raw{n}", 2)
                self.rz, self.on, self.ot, self.x_new = ev(f"rz{n}", TC), ev(f"on{n}", TC), ev(f"ot{n}", 1), ev(f"x_new{n}", 1)

                front = {"spec": (h_spec_ok, 1), "rank": (h_rank_ok, 1), "cond": (x1_ok, 1)} if n == 1 else {}
                front |= {"xT": (self.xt, DC), "q": (self.q, 1), "k": (self.k, 1), "v": (self.vp, 1)}
                if n == 2:
                    front |= {"coh1": (c1_ok, DC), "coh2": (zz_ok, 1)}
                front |= {f"s{h}": (self.rowmax, h + 1) for h in range(H)} | {"max": (self.nm, 2)}
                self.front = Ring(sem(f"front_full{n}"), banks[0:3], front)

                back = {f"p{h}": (self.probs, h + 1) for h in range(H)}
                if n == 2:
                    back |= {"sumv": (on_field, TC)}
                back |= {"tok0": (self.on, 1), "tok1": (self.on, 2), "oT": (self.ot, 1)}
                back |= {"wo": ((y_ok, attn2_ok, attn3_ok)[n - 1], 1)}
                if n == 1:
                    back |= {"yT": (yt_ok, DC)} | {f"ffn{f}": (hm_ok, f + 1) for f in range(FC)} | {"down": (self.x_new, 1)}
                if n == 3:
                    back |= {"mod": (mod_ok, 2)}
                self.back = Ring(sem(f"back_full{n}"), banks[3:6], back)

        lay = {n: Layer(n) for n in LAYERS}
        L3 = lay[3]

        def run_layer(eng, L, step):
            order = order_of(L.n)

            def half_step(b, par, front, back):
                for side, what, n in order:
                    if side == "front" and front:
                        step(what, n, b + 1, 1 - par)
                    if side == "back" and back:
                        step(what, n, b, par)

            half_step(-1, 1, True, False)
            half_step(0, 0, True, True)
            half_step(1, 1, True, True)
            with eng.Fori(1, NBATCH // 2 - 1) as j:
                half_step(2 * j, 0, True, True)
                half_step(2 * j + 1, 1, True, True)
            half_step(NBATCH - 2, 0, True, True)
            half_step(NBATCH - 1, 1, False, True)

        def layer_gate(eng, n):
            if n == 1:
                eng.wait_ge(s_setup, 1)
            else:
                eng.wait_ge(lay[n - 1].x_new.sem, NBATCH)
            eng.wait_ge(s_ld[n], 16 * len(loads[n]))

        def rows(name, n):
            return ins[name].rearrange("(a d) -> a d", a=1).to_broadcast([n, ins[name].shape[0]])

        loads0 = [(ident, "ident"), (raw, "raw"), (raw_t, "raw_t"), (below, "below"), (cond_a, "cond_a"),
                  (cond_w, "cond_w"), (we1, "we1"), (we2, "we2"), (be2, "be2"), (ln_gb, "ln_gb"), (pe_t, "pe_t"),
                  (w_basis, "w_basis"), (w_outb, "w_outb"), (mask_q, "mask_q"), (mask_k, "mask_k"),
                  (bqk, "bqk")]
        loads = {
            1: [(wqkvo[1], "wqkvo1"), (w_gate, "w_gate"), (w_hid, "w_hid"), (w_down, "w_down")],
            2: [(wqkvo[2], "wqkvo2"), (w_c1, "w_c1"), (w_c2, "w_c2"), (bv_rows, "bv"), (bout_rows, "bout"), (bc2_rows, "bc2")],
            3: [(wqkvo[3], "wqkvo3"), (w_mod, "w_mod"), (rms_rows, "rms")],
        }

        mark = {}

        block = ctx.enter_context(nc.Block())

        @block.vector
        def _(dve):
            count = [0]

            def link(a):
                count[0] += 1
                a.then_inc(s_vch, 1)
                dve.wait_ge(s_vch, count[0])

            dve.wait_ge(s_ld0, 16 * (len(loads0) + 2))
            link(dve.tensor_copy(ident_bf[:], ident[:]))
            link(dve.tensor_scalar(bqk[:, 0:DC], bqk[:, 0:DC], HD ** -0.5, None, ALU.mult))
            link(dve.tensor_scalar(big_q[:], mask_q[:], BIG, None, ALU.mult))
            link(dve.tensor_scalar(big_k[:], mask_k[:], BIG, None, ALU.mult))
            link(dve.tensor_scalar(keys_left[:], mask_q[:], -1.0, 1.0, ALU.mult, ALU.add))
            link(dve.tensor_reduce(some_key[:], keys_left[:], AX, ALU.add))
            link(dve.reciprocal(stat[:, 0, :], some_key[:]))
            link(dve.tensor_tensor(some_key[:], some_key[:], stat[:, 0, :], ALU.mult))
            dve.wait_ge(s_pe0, 1)
            link(dve.tensor_copy(cvec[:, 0:10, :], banks[4][:, 0:10 * NBATCH].rearrange("p (v b) -> p v b", v=10)))
            dve.wait_ge(s_act0, 1)
            link(dve.scalar_tensor_tensor(th_c[:], th_c[:], 1.0, cond_a[0:C, :], ALU.add, ALU.mult))
            dve.wait_ge(s_memset, 4)
            link(dve.tensor_scalar(cvec[0:C, SILU, :], th_c[:], 0.5, None, ALU.mult))
            link(dve.tensor_scalar(a1[:], banks[5][:, 0:DC * NBATCH].rearrange("p (c b) -> p c b", c=DC), 0.0, None, ALU.max))
            mark["A1"] = count[0]
            dve.wait_ge(s_pe0, 2)
            link(dve.tensor_reduce(fs[:, 0:1], banks[6][0:NBATCH, 0:D], AX, ALU.add))
            link(dve.tensor_scalar(fs[:, 0:1], fs[:, 0:1], -1.0 / D, None, ALU.mult))
            link(dve.tensor_scalar(fld[:, 0, :], banks[6][0:NBATCH, 0:D], fs[:, 0:1], None, ALU.add))
            link(dve.tensor_tensor(fld[:, 1, :], fld[:, 0, :], fld[:, 0, :], ALU.mult))
            link(dve.tensor_reduce(fs[:, 1:2], fld[:, 1, :], AX, ALU.add))
            link(dve.tensor_scalar(fs[:, 2:3], fs[:, 1:2], 1.0 / D, 1e-5, ALU.mult, ALU.add))
            mark["var"] = count[0]
            dve.wait_ge(s_pe0, 3)
            link(dve.scalar_tensor_tensor(gj[:, 0:C], ident[0:C, 0:C], 1e-4, banks[7][0:C, 0:C], ALU.mult, ALU.add))
            link(dve.tensor_copy(gj[:, C:2 * C], ident[0:C, 0:C]))
            dve.tensor_copy(gj_c[:, 0:1], ident[0:C, 0:1]).then_inc(s_gj_up, 1)
            with dve.Fori(0, C) as j:
                dve.wait_ge(s_gj_up, j + 1)
                dve.tensor_scalar(gj_row[:], gj[:], ident[0:C, bass.ds(j, 1)], None, ALU.mult).then_inc(s_gj_row, 1)
                dve.wait_ge(s_gj_bc, j * 3 + 1)
                dve.reciprocal(gj_c[:, 0:1], banks[0][0:C, bass.ds(j, 1)]).then_inc(s_gj_bc, 1)
                dve.wait_ge(s_gj_bc, j * 3 + 2)
                dve.scalar_tensor_tensor(gj_c[:, 1:2], gj[:, bass.ds(j, 1)], gj_c[:, 0:1], below[:, bass.ds(j, 1)],
                                         ALU.mult, ALU.mult).then_inc(s_gj_bc, 1)
                dve.wait_ge(s_gj_bc, j * 3 + 3)
                dve.scalar_tensor_tensor(gj[:], banks[0][0:C, 0:2 * C], gj_c[:, 1:2], gj[:], ALU.mult, ALU.add)\
                    .then_inc(s_gj_up, 1)
            dve.wait_ge(s_gj_up, C + 1)
            link(dve.tensor_tensor(gj_row[:, 0:C], gj[:, 0:C], ident[0:C, 0:C], ALU.mult))
            link(dve.tensor_reduce(gj_c[:, 2:3], gj_row[:, 0:C], AX, ALU.add))
            mark["D"] = count[0]
            dve.wait_ge(s_pool0, 2)
            link(dve.tensor_scalar(tinv[:], gj[:, C:2 * C], gj_c[:, 3:4], None, ALU.mult))
            dve.wait_ge(s_pe0, 4)
            link(dve.tensor_copy(tinv_t[:], banks[1][0:C, 0:C]))
            dve.wait_ge(s_pe0, 5)
            link(dve.tensor_copy(qmat[:], banks[2][0:C, 0:C]))
            link(dve.tensor_tensor(sgn[:], qmat[:], raw[:], ALU.mult))
            mark["Q"] = count[0]
            dve.wait_ge(s_pe0, 6)
            link(dve.tensor_scalar(sgn[:], banks[3][0:C, 0:C], 0.0, 2.0, ALU.is_ge, ALU.mult))
            link(dve.memset(mtr[:, C:P], 0.0))
            link(dve.scalar_tensor_tensor(mtr[:, 0:C], sgn[:], -1.0, qmat[:], ALU.add, ALU.mult))
            dve.wait_ge(s_pool0, 1)
            link(dve.tensor_scalar(fld[:, 0, :], fld[:, 0, :], fs[:, 3:4], None, ALU.mult))
            link(dve.tensor_tensor(fld[:, 0, :], fld[:, 0, :], ln_gb[:, 0, :], ALU.mult))
            link(dve.tensor_tensor(fld[:, 0, :], fld[:, 0, :], ln_gb[:, 1, :], ALU.add))
            mark["F"] = count[0]
            dve.wait_ge(s_pe0, 7)
            link(dve.tensor_copy(fld_t[:], banks[7][:, 0:DC * NBATCH].rearrange("p (c b) -> p c b", c=DC)))
            mark["FT"] = count[0]
            dve.wait_ge(s_pe0, 8)
            link(dve.tensor_reduce(fs[:, 4:5], banks[6][0:NBATCH, 0:S], AX, ALU.max))
            link(dve.tensor_scalar(fs[:, 5:6], fs[:, 4:5], -1.0, None, ALU.mult))
            mark["E"] = count[0]
            dve.wait_ge(s_act0, 2)
            link(dve.reciprocal(fs[:, 7:8], fs[:, 6:7]))
            link(dve.tensor_scalar(fld[:, 1, :], fld[:, 2, :], fs[:, 7:8], FI, ALU.mult, ALU.mult))
            mark["FA"] = count[0]
            dve.wait_ge(s_pe0, 9)
            link(dve.tensor_copy(cvec[:, FIELD:FIELD + TC, :], banks[7][:, 0:TC * NBATCH].rearrange("p (t b) -> p t b", t=TC)))
            dve.wait_ge(s_memset, 18)
            dve.tensor_copy(fs[:, 0:1], fs[:, 1:2]).then_inc(s_setup, 1)

            for n in LAYERS:
                L = lay[n]
                fr, bk = L.front, L.back

                def step(what, k, b, par):
                    if what == "load":
                        dve.wait_ge(L.xt.sem, L.xt.at(b, 0))
                        if n == 2:
                            dve.wait_ge(c1_ok.sem, c1_ok.at(b, 0))
                        dve.tensor_scalar(cur_f[:], cvec[:, :, b], 1.0, None, ALU.mult).then_inc(L.cur_f.sem, 1)
                    if what == "vectors":
                        if n == 1:
                            dve.wait_ge(yt_ok.sem, yt_ok.at(b, 0))
                        dve.tensor_scalar(cur_b[:], cvec[:, :, b], 1.0, None, ALU.mult).then_inc(L.cur_b.sem, 1)
                    if what == "cond":
                        bank = fr.wait_filled(dve, b, "cond")
                        dve.wait_ge(x_loaded.sem, x_loaded.at(b, 32))
                        dve.tensor_tensor(xres[:, b, :, :], bank[:, :].rearrange("p (t d) -> p t d", t=TC), x_in[:], ALU.add)\
                            .then_inc(x1_ok.sem, 1)
                        mean_square(b, stat, sq1, ms1)
                    if what == "xT" and n == 1:
                        dve.wait_ge(inv1.sem, inv1.at(b, 1))
                        for t in range(TC):
                            dve.tensor_scalar(xn[:, t, :], xres[:, b, t, :], stat[:, 2, t:t + 1], None, ALU.mult).then_inc(xn_ok.sem, 1)
                    if what == "stage":
                        dve.wait_ge(L.xt.sem, L.xt.at(b, 0))
                        dve.tensor_scalar(xn[:], xres[:, b, :, :], 1.0, None, ALU.mult).then_inc(L.staged.sem, 1)
                    if what == "qk":
                        dve.wait_ge(L.qk_lo.sem, L.qk_lo.at(b, 0))
                        bank = fr.wait_filled(dve, b, "k")
                        if n == 2:
                            for c in range(DC):
                                a = dve.tensor_scalar(qk[:, DC + c, :], bank[:, c * S:(c + 1) * S], bqk[:, DC + c:DC + c + 1], None, ALU.add)
                        else:
                            a = dve.tensor_copy(qk[:, DC:2 * DC, :], bank[:, :].rearrange("p (c s) -> p c s", c=DC))
                        a.then_inc(L.k.sem, 1)
                        dve.wait_ge(L.q.sem, L.q.at(b, 1))
                        dve.wait_ge(L.k.sem, L.k.at(b, 1))
                        if not (isinstance(b, int) and b < 2):
                            dve.wait_ge(L.pv.sem, L.pv.at(b - 1, 0))
                        dve.wait_ge(L.stacked.sem, L.stacked.at(b, 0))
                        dve.tensor_copy(qk_hi[:], qk[:]).then_inc(L.qk_hi.sem, 1)
                    if what == "v" and n == 2:
                        if not (isinstance(b, int) and b < 2):
                            dve.wait_ge(L.pv.sem, L.pv.at(b - 1, 0))
                        bank = fr.wait_filled(dve, b, "v")
                        for t in range(TC):
                            a = dve.tensor_tensor(vp[par][:, t, :, 0:HD], bank[:, t * D:(t + 1) * D].rearrange("p (h d) -> p h d", h=H),
                                                  bv_rows[:, :].rearrange("p (h d) -> p h d", h=H), ALU.add)
                        a.then_inc(L.vp.sem, 1)
                    if what == "coh2":
                        bank = fr.wait_filled(dve, b, "coh2")
                        for t in range(TC):
                            a = dve.tensor_tensor(zz[:, t, :], bank[:, t * H:(t + 1) * H], bc2_rows[:], ALU.add)
                        a.then_inc(zz_ok.sem, 1)
                        dve.wait_ge(ez_ok.sem, ez_ok.at(b, 1))
                        dve.tensor_scalar(coh[par][:], ez[:], 1e-8, 1.0 + 1e-8, ALU.mult, ALU.add).then_inc(coh_ok.sem, 1)
                        dve.wait_ge(coh_ok.sem, coh_ok.at(b, 1))
                        dve.reciprocal(coh[par][:], coh[par][:]).then_inc(coh_ok.sem, 1)
                        dve.wait_ge(coh_ok.sem, coh_ok.at(b, 2))
                        dve.tensor_scalar(coh[par][:], coh[par][:], 1.0 - FI, None, ALU.mult).then_inc(coh_ok.sem, 1)
                    if what == "smax":
                        bank = fr.wait_filled(dve, b, f"s{k}")
                        dve.tensor_reduce(rowmax[:, :, k:k + 1], bank[:, :].rearrange("p (t s) -> p t s", t=TC), AX, ALU.max)\
                            .then_inc(L.rowmax.sem, 1)
                    if what == "max":
                        bank = fr.wait_filled(dve, b, "max")
                        dve.wait_ge(L.shifted.sem, L.shifted.at(b, 0))
                        dve.tensor_scalar(nm_hi[:], bank[0:H, 0:S], -1.0, None, ALU.mult).then_inc(L.nm.sem, 1)
                        dve.wait_ge(L.nm.sem, L.nm.at(b, 1))
                        dve.scalar_tensor_tensor(nm_lo[:], bank[0:H, 0:S], -1.0, nm_hi[:], ALU.mult, ALU.subtract).then_inc(L.nm.sem, 1)
                    if what == "pv" and k % 2 == 1:
                        dve.wait_ge(L.pv.sem, L.pv.at(b, k + 1))
                        dve.tensor_copy(ot_raw[:, k - 1:k + 1, :], o_bank[k // 2][:, :].rearrange("p (g s) -> p g s", g=2)).then_inc(L.o_raw.sem, 1)
                    if what == "tok":
                        for t in range(TC):
                            bank = bk.wait_filled(dve, b, f"tok{t}")
                            grid = bank[:, :].rearrange("p (h w) -> p h w", w=HW)
                            dve.reciprocal(rz[:, t, :], grid[:, :, HD]).then_inc(L.rz.sem, 1)
                            dve.wait_ge(L.rz.sem, L.rz.at(b, t + 1))
                            if n == 2:
                                dve.tensor_tensor(rz[:, t, :], rz[:, t, :], coh[par][:, t, :], ALU.mult).then_inc(rz_coh.sem, 1)
                                dve.wait_ge(rz_coh.sem, rz_coh.at(b, t + 1))
                            if n == 3:
                                dve.tensor_scalar(rz[:, t, :], rz[:, t, :], some_key[:, t:t + 1], None, ALU.mult).then_inc(rz_some.sem, 1)
                                dve.wait_ge(rz_some.sem, rz_some.at(b, t + 1))
                            dve.tensor_tensor(on[:, t, :].rearrange("p (h d) -> p h d", h=H), grid[:, :, 0:HD],
                                              rz[:, t, :].rearrange("p (h a) -> p h a", a=1).to_broadcast([P, H, HD]), ALU.mult)\
                                .then_inc(L.on.sem, 1)
                            if n == 2:
                                dve.wait_ge(L.on.sem, L.on.at(b, t + 1))
                                svb = bk.wait_filled(dve, b, "sumv")
                                dve.scalar_tensor_tensor(on[:, t, :], svb[:, 0:D], cur_b[:, FIELD + t:FIELD + t + 1], on[:, t, :],
                                                         ALU.mult, ALU.add).then_inc(on_field.sem, 1)
                    if what == "wo" and n == 1:
                        bank = bk.wait_filled(dve, b, "wo")
                        dve.wait_ge(xy_ok.sem, xy_ok.at(b, 0))
                        dve.tensor_tensor(y[:], bank[:, :].rearrange("p (t d) -> p t d", t=TC), xres[:, b, :, :], ALU.add).then_inc(y_ok.sem, 1)
                        mean_square(b, statb, sq2, ms2)
                    if what == "wo" and n == 3:
                        mean_square(b, statb, sq3, ms3)
                    if what == "wo" and n == 2:
                        bank = bk.wait_filled(dve, b, "wo")
                        dve.tensor_tensor(y[:], bank[:, :].rearrange("p (t d) -> p t d", t=TC),
                                          bout_rows[:, :].rearrange("p (a d) -> p a d", a=1).to_broadcast([P, TC, D]), ALU.add).then_inc(attn2_ok.sem, 1)
                        dve.wait_ge(attn2_ok.sem, attn2_ok.at(b, 1))
                        dve.tensor_tensor(xres[:, b, :, :], xres[:, b, :, :], y[:], ALU.add).then_inc(L.x_new.sem, 1)
                    if what == "yT":
                        dve.wait_ge(inv2.sem, inv2.at(b, 1))
                        for t in range(TC):
                            dve.tensor_scalar(yn[:, t, :], y[:, t, :], statb[:, 2, t:t + 1], None, ALU.mult).then_inc(yn_ok.sem, 1)
                    if what == "ffn":
                        bank = bk.bank(f"ffn{k}")
                        dve.wait_ge(th_ok.sem, th_ok.at(b, k + 1))
                        dve.scalar_tensor_tensor(act1[:, k % 2, :], th[:, k % 2, :], 1.0, bank[:, 0:S], ALU.add, ALU.mult).then_inc(act1_ok.sem, 1)
                        dve.wait_ge(act1_ok.sem, act1_ok.at(b, k + 1))
                        dve.scalar_tensor_tensor(hm[:, k, :], act1[:, k % 2, :], 0.5, bank[:, S:2 * S], ALU.mult, ALU.mult)\
                            .then_inc(hm_ok.sem, 1)
                    if what == "down":
                        bank = bk.wait_filled(dve, b, "down")
                        dve.wait_ge(xy_ok.sem, xy_ok.at(b, 1))
                        dve.tensor_tensor(xres[:, b, :, :], bank[:, :].rearrange("p (t d) -> p t d", t=TC), xres[:, b, :, :], ALU.add)\
                            .then_inc(L.x_new.sem, 1)
                    if what == "mod":
                        bank = bk.wait_filled(dve, b, "mod")
                        dve.scalar_tensor_tensor(mod_a[:], bank[:, D:2 * D], 1.0, rms_rows[:], ALU.add, ALU.mult).then_inc(mod_ok.sem, 1)
                        dve.tensor_copy(mod_s[:], bank[:, 0:D]).then_inc(mod_ok.sem, 1)
                        dve.wait_ge(mod_ok.sem, mod_ok.at(b, 2))
                        dve.wait_ge(inv3.sem, inv3.at(b, 1))
                        for t in range(TC):
                            dve.scalar_tensor_tensor(y[:, t, :], y[:, t, :], statb[:, 2, t:t + 1], mod_a[:], ALU.mult, ALU.mult).then_inc(mod_sum.sem, 1)
                        for t in range(TC):
                            dve.wait_ge(mod_sum.sem, mod_sum.at(b, t + 1))
                            dve.tensor_tensor(y[:, t, :], y[:, t, :], mod_s[:], ALU.add).then_inc(mod_sum.sem, 1)
                        dve.wait_ge(mod_sum.sem, mod_sum.at(b, 4))
                        dve.tensor_tensor(xres[:, b, :, :], xres[:, b, :, :], y[:], ALU.add).then_inc(L.x_new.sem, 1)

                def mean_square(b, st, sq, ms):
                    dve.wait_ge(sq.sem, sq.at(b, TC))
                    dve.tensor_scalar(st[:, 1, :], st[:, 0, :], 1.0 / D, 1e-6, ALU.mult, ALU.add).then_inc(ms.sem, 1)

                layer_gate(dve, n)
                run_layer(dve, L, step)

        @block.sync
        def _(sp):
            for tile, name in loads0:
                sp.dma_start(tile[:], ins[name]).then_inc(s_ld0, 16)
            sp.wait_ge(s_memset, 4)
            sp.dma_start(cvec[0:C, SPEC, :], ins["cond_a"][0:C, :]).then_inc(s_ld0, 16)
            sp.dma_start(cvec[0:C, RANK, :], ins["cond_64t"]).then_inc(s_ld0, 16)
            def load_layer(n):
                for tile, name in loads[n]:
                    src = ins[name]
                    if len(src.shape) == 1:
                        src = rows(name, P)
                    sp.dma_start(tile[:], src).then_inc(s_ld[n], 16)

            load_layer(1)
            for n in LAYERS:
                L = lay[n]
                if n == 2:
                    sp.wait_ge(lay[1].x_new.sem, NBATCH)
                    load_layer(2)
                    load_layer(3)

                def step(what, k, b, par):
                    if what == "load" and n == 1:
                        sp.wait_ge(x1_ok.sem, x1_ok.at(b, 0))
                        sp.wait_ge(s_setup, 1)
                        sp.dma_start(x_in[:], ins["x"][b].rearrange("(t p) d -> p t d", p=P)).then_inc(x_loaded.sem, 16)
                        sp.dma_start(xt_in[:], ins["x_t"][b]).then_inc(x_loaded.sem, 16)
                    if what == "qk":
                        sp.wait_ge(L.qk_hi.sem, L.qk_hi.at(b, 1))
                        for r, (q_part, k_part) in enumerate(((qk_hi, qk_hi), (qk_lo, qk_hi), (qk_hi, qk_lo))):
                            if r == 1:
                                sp.wait_ge(L.qk_lo.sem, L.qk_lo.at(b, 1))
                            for dst, src, c0 in ((qs[par], q_part, 0), (ks[par], k_part, DC)):
                                for c in range(DC):
                                    sp.dma_start(dst[HD * r:HD * (r + 1), 8 * c:8 * c + 8, :].bitcast(F32),
                                                 src[:, c0 + c, :].bitcast(F32)).then_inc(L.stacked.sem, 16)
                    if what == "max":
                        sp.wait_ge(L.nm.sem, L.nm.at(b, 2))
                        for r, part in enumerate((nm_hi, nm_lo)):
                            sp.dma_start(qs[par][SHIFT + r:SHIFT + r + 1, :, :].bitcast(F32),
                                         part[:, :].bitcast(F32)).then_inc(L.shifted.sem, 16)
                    if what == "mod":
                        sp.wait_ge(L3.x_new.sem, L3.x_new.at(b, 1))
                        sp.wait_ge(s_setup, 1)
                        sp.dma_start(out[b].rearrange("(t p) d -> p t d", p=P), xres[:, b, :, :]).then_inc(stored.sem, 16)

                layer_gate(sp, n)
                run_layer(sp, L, step)
            sp.wait_ge(stored.sem, 16 * NBATCH)

        @block.gpsimd
        def _(pool):
            clears = [(ones[:], 1.0), (half[:], -0.5), (cvec[:], 0.0), (cvec[C:CA, SILU, :], 1.0)]
            for i in range(2):
                clears += [(qs[i][32:64, :, :].bitcast(F32), 0.0), (qs[i][64:96, :, :].bitcast(F32), 0.0),
                           (ks[i][32:64, :, :].bitcast(F32), 0.0), (ks[i][64:96, :, :].bitcast(F32), 0.0),
                           (ks[i][96:98, :, :].bitcast(F32), 1.0), (vp[i][:, :, :, HD:HW], 0.0), (vp[i][:, :, :, HD:HD + 1], 1.0)]
            assert len(clears) == 18
            for k, (tile, value) in enumerate(clears):
                if k:
                    pool.wait_ge(s_memset, k)
                pool.memset(tile, value).then_inc(s_memset, 1)
            pool.wait_ge(s_memset, len(clears))

            pool.wait_ge(s_vch, mark["var"])
            pool.tensor_tensor(fs[:, 3:4], fs[:, 2:3], half[0:NBATCH, 0:1], ALU.pow).then_inc(s_pool0, 1)
            pool.wait_ge(s_vch, mark["D"])
            pool.tensor_tensor(gj_c[:, 3:4], gj_c[:, 2:3], half[0:C, 0:1], ALU.pow).then_inc(s_pool0, 1)

            for n in LAYERS:
                L = lay[n]

                def step(what, k, b, par):
                    if what == "cond":
                        rsqrt(b, stat, ms1, inv1)
                    if what == "qk":
                        pool.wait_ge(L.qk_hi.sem, L.qk_hi.at(b, 1))
                        pool.wait_ge(L.stacked.sem, L.stacked.at(b, 0))
                        pool.tensor_tensor(qk_lo[:], qk[:], qk_hi[:], ALU.subtract).then_inc(L.qk_lo.sem, 1)
                    if what == "yT":
                        rsqrt(b, statb, ms2, inv2)
                        pool.tensor_tensor(xres[:, b, :, :], xres[:, b, :, :], y[:], ALU.add).then_inc(xy_ok.sem, 1)
                    if what == "wo" and n == 3:
                        pool.wait_ge(mod_ok.sem, mod_ok.at(b, 0))
                        pool.wait_ge(L.cur_b.sem, L.cur_b.at(b, 1))
                        pool.tensor_tensor(mod_l[:], ones[0:CA, :], cur_b[0:CA, SILU:SILU + 1].to_broadcast([CA, P]), ALU.mult).then_inc(mod_l_ok.sem, 1)
                        rsqrt(b, statb, ms3, inv3)

                def rsqrt(b, st, ms, inv):
                    pool.wait_ge(ms.sem, ms.at(b, 1))
                    pool.tensor_tensor(st[:, 2, :], st[:, 1, :], half[:], ALU.pow).then_inc(inv.sem, 1)

                layer_gate(pool, n)
                run_layer(pool, L, step)

        @block.scalar
        def _(act):
            act.wait_ge(s_ld0, 16 * (len(loads0) + 2))
            act.activation(th_c[:], cond_a[0:C, :], ACT.Tanh, scale=0.5).then_inc(s_act0, 1)
            act.wait_ge(s_vch, mark["E"])
            act.activation(fld[:, 2, :], banks[6][0:NBATCH, 0:S], ACT.Exp, bias=fs[:, 5:6],
                           accum_out=fs[:, 6:7]).then_inc(s_act0, 1)

            for n in LAYERS:
                L = lay[n]
                fr, bk = L.front, L.back

                def step(what, k, b, par):
                    if what == "spec":
                        t = fr.wait_filled(act, b, "spec")
                        act.wait_ge(L.cur_f.sem, L.cur_f.at(b, 1))
                        act.activation(h_spec[:], t[0:C, 0:S], ACT.Identity, scale=cur_f[0:C, SPEC:SPEC + 1]).then_inc(h_spec_ok.sem, 1)
                    if what == "rank":
                        t = fr.wait_filled(act, b, "rank")
                        act.activation(h_rank[:], t[0:C, 0:S], ACT.Identity, scale=cur_f[0:C, RANK:RANK + 1]).then_inc(h_rank_ok.sem, 1)
                    if what == "cond":
                        act.wait_ge(x1_ok.sem, x1_ok.at(b, 1))
                        for t in range(TC):
                            act.activation(xn[:, t, :], xres[:, b, t, :], ACT.Square, accum_out=stat[:, 0, t:t + 1]).then_inc(sq1.sem, 1)
                    if what == "xT":
                        bank = fr.wait_filled(act, b, "xT")
                        for c in range(DC):
                            src = bank[:, c * S:(c + 1) * S]
                            if n == 1:
                                a = act.activation(xt[:, c, :], src, ACT.Identity, scale=cur_f[:, G1 + c:G1 + c + 1],
                                                   bias=cur_f[:, B1 + c:B1 + c + 1])
                            else:
                                a = act.copy(xt[:, c, :], src)
                            a.then_inc(L.xt.sem, 1)
                    if what == "qk":
                        act.wait_ge(L.qk_lo.sem, L.qk_lo.at(b, 0))
                        bank = fr.wait_filled(act, b, "q")
                        if n == 2:
                            for c in range(DC):
                                a = act.activation(qk[:, c, :], bank[:, c * S:(c + 1) * S], ACT.Identity,
                                                   scale=HD ** -0.5, bias=bqk[:, c:c + 1])
                        else:
                            a = act.activation(qk[:, 0:DC, :], bank[:, :].rearrange("p (c s) -> p c s", c=DC), ACT.Copy, scale=HD ** -0.5)
                        a.then_inc(L.q.sem, 1)
                    if what == "v" and n != 2:
                        if not (isinstance(b, int) and b < 2):
                            act.wait_ge(L.pv.sem, L.pv.at(b - 1, 0))
                        bank = fr.wait_filled(act, b, "v")
                        act.copy(vp[par][:, :, :, 0:HD], bank[:, :].rearrange("p (t h d) -> p t h d", t=TC, h=H)).then_inc(L.vp.sem, 1)
                    if what == "coh1":
                        bank = fr.wait_filled(act, b, "coh1")
                        for c in range(DC):
                            act.activation(c1t[:, c, :], bank[:, c * S:(c + 1) * S], ACT.Tanh,
                                           bias=cur_f[:, C1 + c:C1 + c + 1]).then_inc(c1_ok.sem, 1)
                    if what == "coh2":
                        act.wait_ge(zz_ok.sem, zz_ok.at(b, 1))
                        act.wait_ge(coh_ok.sem, coh_ok.at(b, 0))
                        act.activation(ez[:], zz[:], ACT.Exp, scale=-1.0).then_inc(ez_ok.sem, 1)
                    if what == "probs":
                        bank = bk.wait_filled(act, b, f"p{k}")
                        act.wait_ge(L.pv.sem, L.pv.at(b, 0 if k < PBUF else (k - PBUF) // HG + 1))
                        act.activation(probs[:, k % PBUF, :, :], bank[:, :].rearrange("p (c s) -> p c s", c=TC), ACT.Exp)\
                            .then_inc(L.probs.sem, 1)
                    if what == "oT":
                        bank = bk.wait_filled(act, b, "oT")
                        act.copy(ot[:], bank[:, :].rearrange("p (c s) -> p c s", c=DC)).then_inc(L.ot.sem, 1)
                    if what == "wo" and n == 1:
                        act.wait_ge(y_ok.sem, y_ok.at(b, 1))
                        for t in range(TC):
                            act.activation(yn[:, t, :], y[:, t, :], ACT.Square, accum_out=statb[:, 0, t:t + 1]).then_inc(sq2.sem, 1)
                    if what == "wo" and n == 3:
                        bank = bk.wait_filled(act, b, "wo")
                        act.wait_ge(L.x_new.sem, L.x_new.at(b, 0))
                        act.copy(y[:], bank[:, :].rearrange("p (t d) -> p t d", t=TC)).then_inc(attn3_ok.sem, 1)
                        act.wait_ge(attn3_ok.sem, attn3_ok.at(b, 1))
                        for t in range(TC):
                            act.activation(yn[:, t, :], y[:, t, :], ACT.Square, accum_out=statb[:, 0, t:t + 1]).then_inc(sq3.sem, 1)
                    if what == "yT":
                        bank = bk.wait_filled(act, b, "yT")
                        for c in range(DC):
                            act.activation(yt[:, c, :], bank[:, c * S:(c + 1) * S], ACT.Identity, scale=cur_b[:, G2 + c:G2 + c + 1],
                                           bias=cur_b[:, B2 + c:B2 + c + 1]).then_inc(yt_ok.sem, 1)
                    if what == "ffn":
                        bank = bk.wait_filled(act, b, f"ffn{k}")
                        act.wait_ge(act1_ok.sem, act1_ok.at(b, max(k - 1, 0)))
                        act.activation(th[:, k % 2, :], bank[:, 0:S], ACT.Tanh, scale=0.5).then_inc(th_ok.sem, 1)

                layer_gate(act, n)
                run_layer(act, L, step)

        @block.tensor
        def _(pe):
            pe.wait_ge(s_ld0, 16 * (len(loads0) + 2))
            for v in range(10):
                pe.matmul(banks[4][:, v * NBATCH:(v + 1) * NBATCH], cond_w[:, v, :], cond_a[:], start=True, stop=True)
            for c in range(DC):
                m = pe.matmul(banks[5][:, c * NBATCH:(c + 1) * NBATCH], we1[:, c * P:(c + 1) * P], cond_a[:], start=True, stop=True)
            m.then_inc(s_pe0, 1)
            pe.wait_ge(s_memset, 1)
            pe.wait_ge(s_vch, mark["A1"])
            for c in range(DC):
                pe.matmul(banks[6][0:NBATCH, 0:D], a1[:, c, :], we2[:, c, :], start=(c == 0), stop=False)
            pe.matmul(banks[6][0:NBATCH, 0:D], ones[0:1, 0:NBATCH], be2[:], start=False, stop=True).then_inc(s_pe0, 1)
            pe.matmul(banks[7][0:C, 0:C], raw[:], raw[:], start=True, stop=True).then_inc(s_pe0, 1)
            with pe.Fori(0, C) as j:
                pe.wait_ge(s_gj_row, j + 1)
                pe.matmul(banks[0][:, 0:2 * C], ones[0:C, :], gj_row[:], start=True, stop=True).then_inc(s_gj_bc, 1)
            pe.wait_ge(s_vch, mark["D"] + 1)
            pe.transpose(banks[1][0:C, 0:C], tinv[:], ident[0:C, 0:C]).then_inc(s_pe0, 1)
            pe.wait_ge(s_vch, mark["D"] + 2)
            pe.matmul(banks[2][0:C, 0:C], raw_t[:], tinv_t[:], start=True, stop=True).then_inc(s_pe0, 1)
            pe.wait_ge(s_vch, mark["Q"])
            pe.matmul(banks[3][0:C, 0:C], ones[0:C, 0:C], sgn[:], start=True, stop=True).then_inc(s_pe0, 1)
            pe.wait_ge(s_vch, mark["F"])
            for c in range(DC):
                m = pe.transpose(banks[7][:, c * NBATCH:(c + 1) * NBATCH], fld[:, 0, c * P:(c + 1) * P], ident[0:NBATCH, 0:NBATCH])
            m.then_inc(s_pe0, 1)
            pe.wait_ge(s_vch, mark["FT"])
            for c in range(DC):
                m = pe.matmul(banks[6][0:NBATCH, 0:S], fld_t[:, c, :], pe_t[:, c, :], start=(c == 0), stop=(c == DC - 1))
            m.then_inc(s_pe0, 1)
            pe.wait_ge(s_vch, mark["FA"])
            for t in range(TC):
                m = pe.transpose(banks[7][:, t * NBATCH:(t + 1) * NBATCH], fld[:, 1, t * P:(t + 1) * P], ident[0:NBATCH, 0:NBATCH])
            m.then_inc(s_pe0, 1)

            for n in LAYERS:
                L = lay[n]
                fr, bk = L.front, L.back
                w = wqkvo[n]

                def outputs_first(bank, weights, acts):
                    for c in range(DC):
                        for i in range(DC):
                            m = pe.matmul(bank[:, c * S:(c + 1) * S], weights[:, i, c * P:(c + 1) * P], acts[:, i, :],
                                          start=(i == 0), stop=(i == DC - 1))
                    return m

                def tokens_first(bank, acts, weights, n_in=DC, width=D):
                    for t in range(TC):
                        for i in range(n_in):
                            m = pe.matmul(bank[:, t * width:(t + 1) * width], acts[:, i, t * P:(t + 1) * P], weights[:, i, :],
                                          start=(i == 0), stop=(i == n_in - 1))
                    return m

                def transposes(bank, src):
                    for c in range(DC):
                        for t in range(TC):
                            m = pe.transpose(bank[:, c * S + t * P:c * S + (t + 1) * P], src[:, t, c * P:(c + 1) * P], ident[:])
                    return m

                def step(what, k, b, par):
                    if what == "spec":
                        pe.wait_ge(x_loaded.sem, x_loaded.at(b, 32))
                        fr.wait_free(pe, b, "spec")
                        for c in range(DC):
                            m = pe.matmul(fr.bank("spec")[0:C, 0:S], w_basis[:, c, :], xt_in[:, c, :], start=(c == 0), stop=(c == DC - 1))
                        m.then_inc(fr.full.sem, 1)
                    if what == "rank":
                        pe.wait_ge(h_spec_ok.sem, h_spec_ok.at(b, 1))
                        fr.wait_free(pe, b, "rank")
                        pe.matmul(fr.bank("rank")[:, 0:S], mtr[:], h_spec[:], start=True, stop=True).then_inc(fr.full.sem, 1)
                    if what == "cond":
                        pe.wait_ge(h_rank_ok.sem, h_rank_ok.at(b, 1))
                        fr.wait_free(pe, b, "cond")
                        for t in range(TC):
                            m = pe.matmul(fr.bank("cond")[:, t * D:(t + 1) * D], h_rank[:, t * P:(t + 1) * P], w_outb[:], start=True, stop=True)
                        m.then_inc(fr.full.sem, 1)
                    if what == "xT":
                        if n == 1:
                            pe.wait_ge(xn_ok.sem, xn_ok.at(b, 2))
                        else:
                            pe.wait_ge(L.staged.sem, L.staged.at(b, 1))
                        fr.wait_free(pe, b, "xT")
                        transposes(fr.bank("xT"), xn).then_inc(fr.full.sem, 1)
                    if what == "qk":
                        pe.wait_ge(L.xt.sem, L.xt.at(b, 2))
                        for i, use in enumerate("qk"):
                            fr.wait_free(pe, b, use)
                            outputs_first(fr.bank(use), w[:, i], xt).then_inc(fr.full.sem, 1)
                    if what == "v":
                        fr.wait_free(pe, b, "v")
                        tokens_first(fr.bank("v"), xt, w[:, 2]).then_inc(fr.full.sem, 1)
                    if what == "coh1":
                        fr.wait_free(pe, b, "coh1")
                        outputs_first(fr.bank("coh1"), w_c1, xt).then_inc(fr.full.sem, 1)
                    if what == "coh2":
                        pe.wait_ge(c1_ok.sem, c1_ok.at(b, 2))
                        fr.wait_free(pe, b, "coh2")
                        tokens_first(fr.bank("coh2"), c1t, w_c2, width=H).then_inc(fr.full.sem, 1)
                    if what == "smax":
                        if k == 0:
                            pe.wait_ge(L.stacked.sem, L.stacked.at(b, 16 * 12))
                        fr.wait_free(pe, b, f"s{k}")
                        bank = fr.bank(f"s{k}")
                        for t in range(TC):
                            m = pe.matmul(bank[:, t * S:(t + 1) * S], qs[par][0:SCORE_ROWS, k, t * P:(t + 1) * P], ks[par][0:SCORE_ROWS, k, :],
                                          start=True, stop=(n != 3))
                            if n == 3:
                                m = pe.matmul(bank[:, t * S:(t + 1) * S], ident_bf[:], big_q[:, t, :], start=False, stop=True)
                        m.then_inc(fr.full.sem, 1)
                    if what == "max":
                        pe.wait_ge(L.rowmax.sem, L.rowmax.at(b, H))
                        fr.wait_free(pe, b, "max")
                        for t in range(TC):
                            m = pe.transpose(fr.bank("max")[0:H, t * P:(t + 1) * P], rowmax[:, t, :], ident[:])
                        m.then_inc(fr.full.sem, 1)
                    if what == "probs":
                        if k == 0:
                            pe.wait_ge(L.shifted.sem, L.shifted.at(b, 32))
                        bk.wait_free(pe, b, f"p{k}")
                        bank = bk.bank(f"p{k}")
                        for c in range(TC):
                            m = pe.matmul(bank[:, c * S:(c + 1) * S], ks[par][0:SHIFTED_ROWS, k, c * P:(c + 1) * P], qs[par][0:SHIFTED_ROWS, k, :],
                                          start=True, stop=(n != 3))
                            if n == 3:
                                m = pe.matmul(bank[:, c * S:(c + 1) * S], ident_bf[:], big_k[:, c, :], start=False, stop=True)
                        m.then_inc(bk.full.sem, 1)
                    if what == "pv":
                        if k == 0:
                            pe.wait_ge(L.vp.sem, L.vp.at(b, 1))
                            pe.wait_ge(L.o_raw.sem, L.o_raw.at(b, 0))
                        pe.wait_ge(L.probs.sem, L.probs.at(b, HG * (k + 1)))
                        for c in range(TC):
                            for i in range(HG):
                                h = HG * k + i
                                m = pe.matmul(o_bank[k // 2][HW * i:HW * (i + 1), (k % 2) * S:(k % 2 + 1) * S], vp[par][:, c, h, :],
                                              probs[:, h % PBUF, c, :], start=(c == 0), stop=(c == TC - 1))
                        m.then_inc(L.pv.sem, 1)
                    if what == "sumv":
                        bk.wait_free(pe, b, "sumv")
                        for c in range(TC):
                            m = pe.matmul(bk.bank("sumv")[:, 0:D], ones[:], vp[par][:, c, :, 0:HD], start=(c == 0), stop=(c == TC - 1))
                        m.then_inc(bk.full.sem, 1)
                    if what == "tok":
                        pe.wait_ge(L.o_raw.sem, L.o_raw.at(b, 2))
                        for t in range(TC):
                            bk.wait_free(pe, b, f"tok{t}")
                            for g in range(NG):
                                m = pe.transpose(bk.bank(f"tok{t}")[:, g * P:(g + 1) * P], ot_raw[:, g, t * P:(t + 1) * P], ident[:])
                            m.then_inc(bk.full.sem, 1)
                    if what == "oT":
                        done = on_field if n == 2 else L.on
                        pe.wait_ge(done.sem, done.at(b, TC))
                        bk.wait_free(pe, b, "oT")
                        transposes(bk.bank("oT"), on).then_inc(bk.full.sem, 1)
                    if what == "wo":
                        pe.wait_ge(L.ot.sem, L.ot.at(b, 1))
                        bk.wait_free(pe, b, "wo")
                        tokens_first(bk.bank("wo"), ot, w[:, 3]).then_inc(bk.full.sem, 1)
                    if what == "yT":
                        pe.wait_ge(yn_ok.sem, yn_ok.at(b, 2))
                        bk.wait_free(pe, b, "yT")
                        transposes(bk.bank("yT"), yn).then_inc(bk.full.sem, 1)
                    if what == "ffn":
                        if k == 0:
                            pe.wait_ge(yt_ok.sem, yt_ok.at(b, 2))
                        bk.wait_free(pe, b, f"ffn{k}")
                        bank = bk.bank(f"ffn{k}")
                        for j, wt in enumerate((w_gate, w_hid)):
                            for c in range(DC):
                                m = pe.matmul(bank[:, j * S:(j + 1) * S], wt[:, c, k * P:(k + 1) * P], yt[:, c, :], start=(c == 0), stop=(c == DC - 1))
                        m.then_inc(bk.full.sem, 1)
                    if what == "down":
                        pe.wait_ge(hm_ok.sem, hm_ok.at(b, FC))
                        bk.wait_free(pe, b, "down")
                        tokens_first(bk.bank("down"), hm, w_down, n_in=FC).then_inc(bk.full.sem, 1)
                    if what == "mod":
                        pe.wait_ge(mod_l_ok.sem, mod_l_ok.at(b, 1))
                        bk.wait_free(pe, b, "mod")
                        pe.matmul(bk.bank("mod")[:, :], mod_l[:], w_mod[:], start=True, stop=True).then_inc(bk.full.sem, 1)

                layer_gate(pe, n)
                run_layer(pe, L, step)


def chunked(a):
    return np.ascontiguousarray(a.reshape(-1, P, a.shape[1]).transpose(1, 0, 2))


def by_dim(a):
    return a.reshape(*a.shape[:-1], 2, 8, HD).swapaxes(-1, -2).reshape(a.shape)


def position_table():
    pos = np.arange(S, dtype=np.float32)
    inv = np.float32(10000.0) ** np.repeat(np.arange(0, D, 2, dtype=np.float32) / np.float32(D), 2)
    return np.sin(pos[:, None] / inv[None, :]).astype(np.float32)


def layouts(v):
    one = np.ones((1, 1), np.float32)
    with_bias = lambda w, b: np.concatenate([w.T, b[None, :]], 0)
    cond_w = np.concatenate([
        with_bias(v["L1_cond_g1w"], v["L1_cond_g1b"]), with_bias(v["L1_cond_b1w"], v["L1_cond_b1b"]),
        with_bias(v["L1_cond_g2w"], v["L1_cond_g2b"]), with_bias(v["L1_cond_b2w"], v["L1_cond_b2b"]),
        with_bias(v["L2_cond_Wc1"][:, D:], v["L2_cond_bc1"])], 1).reshape(CA, 10, P)
    qkvo = lambda q, k, vv, o: np.stack([chunked(by_dim(q.T)), chunked(by_dim(k.T)), chunked(vv.T), chunked(o.T)], 1)
    w2 = v["L2_cond_Wqkv"].reshape(3, D, D)
    b2 = v["L2_cond_bqkv"].reshape(3, D)
    mask = v["mask_SxS_bk1"]
    return {
        "x": v["x"], "x_t": v["x"].transpose(0, 2, 1).reshape(NBATCH, DC, P, S).transpose(0, 2, 1, 3),
        "ident": np.eye(P, dtype=np.float32), "below": -np.tril(np.ones((C, C), np.float32), -1),
        "raw": v["L0_cond_mode_to_rank"], "raw_t": v["L0_cond_mode_to_rank"].T,
        "cond_a": np.concatenate([v["cond_256"].T, np.repeat(one, NBATCH, 1)], 0), "cond_64t": v["cond_64"].T,
        "cond_w": cond_w, "we1": with_bias(v["L2_cond_We1"], v["L2_cond_be1"]), "we2": chunked(v["L2_cond_We2"].T),
        "be2": v["L2_cond_be2"][None, :],
        "ln_gb": np.broadcast_to(np.stack([v["L2_cond_ln_g"], v["L2_cond_ln_b"]])[None], (NBATCH, 2, D)),
        "pe_t": chunked(position_table().T),
        "w_basis": chunked(v["L0_cond_input_basis"].T), "w_outb": v["L0_cond_output_basis"],
        "mask_q": chunked(mask), "mask_k": chunked(mask.T),
        "bqk": np.concatenate([by_dim(b2[0]).reshape(DC, P), by_dim(b2[1]).reshape(DC, P)]).T,
        "wqkvo1": qkvo(v["L1_cond_Wq"], v["L1_cond_Wk"], v["L1_cond_Wv"], v["L1_cond_Wo"]),
        "w_gate": chunked(v["L1_cond_gate_w"].T), "w_hid": chunked(v["L1_cond_hid_w"].T), "w_down": chunked(v["L1_cond_out_w"].T),
        "wqkvo2": qkvo(w2[0], w2[1], w2[2], v["L2_cond_Wout"]),
        "w_c1": chunked(v["L2_cond_Wc1"][:, :D].T), "w_c2": chunked(v["L2_cond_Wc2"].T),
        "bv": b2[2], "bout": v["L2_cond_bout"], "bc2": v["L2_cond_bc2"],
        "wqkvo3": qkvo(v["L3_cond_Wq"], v["L3_cond_Wk"], v["L3_cond_Wv"], v["L3_cond_Wo"]),
        "w_mod": with_bias(v["L3_cond_Wc"], v["L3_cond_bc"]), "rms": v["L3_cond_rms_scale"],
    }


def kernel(**inputs):
    import concourse.bacc as bacc
    from concourse.bass_utils import run_bass_kernel_spmd

    nc = bacc.Bacc("TRN2", target_bir_lowering=False, num_devices=1)
    arrays, ins = {}, {}
    for name, a in layouts({k: np.asarray(a) for k, a in inputs.items()}).items():
        a = np.ascontiguousarray(a)
        arrays[f"in_{name}"] = a
        ins[name] = nc.dram_tensor(f"in_{name}", a.shape, mybir.dt.from_np(a.dtype), kind="ExternalInput").ap()
    out = nc.dram_tensor("out", (NBATCH, S, D), F32, kind="ExternalOutput").ap()
    cond_resid_kernel(nc, ins, out)
    r = run_bass_kernel_spmd(nc, [arrays], core_ids=[0])
    return r.results[0]["out"]
```

```python
from contextlib import ExitStack

import numpy as np
import concourse.bass as bass
from concourse import mybir

F32 = mybir.dt.float32
F32R = mybir.dt.float32r
BF16 = mybir.dt.bfloat16
ALU = mybir.AluOpType
ACT = mybir.ActivationFunctionType
AX = mybir.AxisListType.X

P = 128
NBATCH, S, D = 16, 256, 256
H, HD = 16, 16
TC, DC = S // P, D // P
C = 64
CA = C + 1
FF = 1024
FC = FF // P
HG = 4
NG = H // HG
HW = 32
PBUF = 8
LAYERS = (1, 2, 3)
FI = 0.3 * 0.7
BIG = -1e30

SHIFT = 96
SCORE_ROWS, SHIFTED_ROWS = SHIFT, SHIFT + 2

G1, B1, G2, B2, C1, SPEC, RANK, FIELD, SILU = 0, 2, 4, 6, 8, 10, 11, 12, 14
NV = 15


class Event:

    def __init__(self, sem, per):
        self.sem, self.per = sem, per

    def at(self, b, k):
        return b * self.per + k


class Ring:

    def __init__(self, sem, banks, readers):
        self.banks, self.readers, self.uses = banks, readers, list(readers)
        self.full = Event(sem, len(readers))

    def bank(self, use):
        return self.banks[self.uses.index(use) % len(self.banks)]

    def wait_filled(self, eng, b, use):
        eng.wait_ge(self.full.sem, self.full.at(b, self.uses.index(use) + 1))
        return self.bank(use)

    def wait_free(self, pe, b, use):
        u, n = self.uses.index(use), len(self.banks)
        if u >= n:
            event, k = self.readers[self.uses[u - n]]
            pe.wait_ge(event.sem, event.at(b, k))
        else:
            event, _ = self.readers[self.uses[u::n][-1]]
            pe.wait_ge(event.sem, event.at(b, 0))
        return self.bank(use)


def order_of(layer):
    out = []

    def add(side, what, first=0, end=None):
        out.extend((side, what, n) for n in range(first, first + 1 if end is None else end))

    maxima_here = 11 if layer == 1 else 12
    between = {2: ("cond",), 6: ("xn",), 8: ("xT",)} if layer == 1 else {1: ("stage",), 6: ("xT",)}
    add("back", "vectors")
    for h in range(H):
        add("back", "probs", h)
        for what in between.get(h, ()):
            add("head", what)
        if h == 11 and layer == 1:
            add("next", "load")
        if h >= H - maxima_here:
            add("middle", "smax", h - (H - maxima_here))
        if h % HG == 1 and h > HG:
            add("back", "pv", h // HG - 1)
    add("back", "pv", NG - 1)
    if layer == 1:
        add("head", "q")
        add("back", "tok")
        add("head", "k")
        add("head", "split")
        add("back", "oT")
        add("head", "v")
        add("back", "wo")
        add("middle", "smax", maxima_here, H - 2)
        add("next", "spec")
        add("back", "yn")
        add("middle", "smax", H - 2, H)
        add("back", "yT")
        add("next", "rank")
        add("middle", "max")
        add("back", "ffn", 0, FC)
        add("back", "down")
    else:
        add("middle", "smax", maxima_here, H)
        if layer == 2:
            add("back", "sumv")
        add("back", "tok")
        add("middle", "max")
        add("head", "q")
        add("head", "k")
        add("head", "split")
        add("back", "oT")
        add("head", "v")
        if layer == 2:
            add("head", "coh1")
        add("back", "wo")
        if layer == 2:
            add("head", "coh2")
        else:
            add("back", "mod")
        add("next", "load")
    return out


def cond_resid_kernel(nc, ins, out):
    with ExitStack() as ctx:
        def sb(name, shape, dt=F32):
            return ctx.enter_context(nc.sbuf_tensor(name, shape, dt))

        def sem(name):
            return ctx.enter_context(nc.semaphore(name))

        banks = [ctx.enter_context(nc.psum_tensor(f"bank{i}", [P, 512], F32)) for i in range(8)]
        o_bank = banks[6:8]

        probs = sb("probs", [P, PBUF, TC, S])
        probs_flat = probs[:, :, :, :].rearrange("p h t s -> p (h t s)")

        class Carver:

            def __init__(self, flat):
                self.flat, self.at = flat, 0

            def __call__(self, shape):
                size = int(np.prod(shape[1:]))
                piece = self.flat[0:shape[0], self.at:self.at + size]
                self.at += size
                if len(shape) == 2:
                    return piece
                names = [f"d{i}" for i in range(len(shape) - 1)]
                return piece.rearrange(f"p ({' '.join(names)}) -> p {' '.join(names)}", **dict(zip(names, shape[1:])))

        setup, ffn = Carver(probs_flat), Carver(probs_flat)
        ot_raw = sb("ot_raw", [P, NG, S])
        setup_more = Carver(ot_raw[:, :, :].rearrange("p g s -> p (g s)"))

        ident = sb("ident", [P, P])
        ident_bf = sb("ident_bf", [P, P], BF16)
        below = setup([C, C])
        ones = sb("ones", [P, P])
        raw, raw_t = setup([C, C]), setup([C, C])
        cond_a = sb("cond_a", [CA, NBATCH])
        cond_w = setup([CA, 10, P])
        we1 = setup([CA, D])
        we2 = setup([P, DC, D])
        be2 = setup([1, D])
        ln_gb = setup([NBATCH, 2, D])
        pe_t = setup([P, DC, S])
        w_basis = sb("w_basis", [P, DC, C])
        w_outb = sb("w_outb", [C, D])
        w_gate, w_hid = sb("w_gate", [P, DC, FF]), sb("w_hid", [P, DC, FF])
        wqkvo = {1: sb("wqkvo1", [P, 4, DC, D])}
        for n, over in ((2, w_gate), (3, w_hid)):
            wqkvo[n] = over[:, :, :].rearrange("p a (b d) -> p (a b) d", d=D).rearrange("p (m c) d -> p m c d", c=DC)
        w_down = sb("w_down", [P, FC, D])
        w_c1 = sb("w_c1", [P, DC, D])
        w_c2 = sb("w_c2", [P, DC, H])
        bqk = sb("bqk", [P, 4])
        bv_rows, bout_rows = sb("bv_rows", [P, D]), sb("bout_rows", [P, D])
        bc2_rows = sb("bc2_rows", [P, H])
        w_mod = sb("w_mod", [CA, 2 * D])
        rms_rows = sb("rms_rows", [P, D])
        mask_q, mask_k = sb("mask_q", [P, TC, S], mybir.dt.uint8), sb("mask_k", [P, TC, S], mybir.dt.uint8)
        big_q, big_k = sb("big_q", [P, TC, S], BF16), sb("big_k", [P, TC, S], BF16)
        some_key = sb("some_key", [P, TC])
        half = sb("half", [P, TC])
        guard = sb("guard", [P, TC])

        xres = sb("xres", [P, NBATCH, TC, D])
        cvec = sb("cvec", [P, NV, NBATCH])

        qs = [sb(f"qs{i}", [P, H, S], F32R) for i in range(2)]
        ks = [sb(f"ks{i}", [P, H, S], F32R) for i in range(2)]
        vp = [sb(f"vp{i}", [P, TC, H, HW]) for i in range(2)]
        coh = [sb(f"coh{i}", [P, TC, H]) for i in range(2)]
        cur_f, cur_b = sb("cur_f", [P, NV]), sb("cur_b", [P, NV])
        x_in, xt_in = sb("x_in", [P, TC, D]), sb("xt_in", [P, DC, S])
        h_spec, h_rank = sb("h_spec", [C, S]), sb("h_rank", [C, S])
        xn = sb("xn", [P, TC, D])
        xt = sb("xt", [P, DC, S])
        qk = sb("qk", [P, 4, S])
        qk_hi, qk_lo = sb("qk_hi", [P, 4, S], F32R), sb("qk_lo", [P, 4, S], F32R)
        rowmax = sb("rowmax", [P, TC, H])
        nm_hi, nm_lo = sb("nm_hi", [H, S], F32R), sb("nm_lo", [H, S], F32R)
        rz = sb("rz", [P, TC, H])
        on = sb("on", [P, TC, D])
        ot = sb("ot", [P, DC, S])
        stat = sb("stat", [P, 3, TC])
        statb = sb("statb", [P, 3, TC])
        y = sb("y", [P, TC, D])
        yn = sb("yn", [P, TC, D])
        yt = sb("yt", [P, DC, S])
        th, act1 = ffn([P, 2, S]), ffn([P, 2, S])
        hm = ffn([P, FC, S])
        c1t = xt_in
        zz, ez = sb("zz", [P, TC, H]), sb("ez", [P, TC, H])
        mod_l = sb("mod_l", [CA, P])
        mod_a, mod_s = x_in[:, 0, :], x_in[:, 1, :]

        gj, gj_row = setup_more([C, 2 * C]), setup_more([C, 2 * C])
        gj_c = setup([C, 4])
        tinv, tinv_t, qmat, sgn = (setup([C, C]) for _ in range(4))
        mtr = sb("mtr", [C, P])
        keys_left = xn
        a1 = setup([P, DC, NBATCH])
        fld = setup_more([NBATCH, 3, D])
        fs = setup([NBATCH, 8])
        fld_t = setup([P, DC, NBATCH])
        th_c = setup([C, NBATCH])

        s_ld0, s_ld = sem("s_ld0"), {n: sem(f"s_ld{n}") for n in LAYERS}
        s_memset = sem("s_memset")
        s_vch, s_pe0, s_act0, s_pool0 = sem("s_vch"), sem("s_pe0"), sem("s_act0"), sem("s_pool0")
        s_gj_row, s_gj_bc, s_gj_up = sem("s_gj_row"), sem("s_gj_bc"), sem("s_gj_up")
        s_setup = sem("s_setup")

        def ev(name, per):
            return Event(sem(name), per)

        x_loaded, h_spec_ok, h_rank_ok, x1_ok = ev("x_loaded", 32), ev("h_spec_ok", 1), ev("h_rank_ok", 1), ev("x1_ok", 1)
        sq1, ms1, inv1, xn_ok = ev("sq1", TC), ev("ms1", 1), ev("inv1", 1), ev("xn_ok", TC)
        y_ok, sq2, ms2, inv2 = ev("y_ok", 1), ev("sq2", TC), ev("ms2", 1), ev("inv2", 1)
        yn_ok, yt_ok, xy_ok = ev("yn_ok", TC), ev("yt_ok", DC), ev("xy_ok", 1)
        th_ok, act1_ok, hm_ok = ev("th_ok", FC), ev("act1_ok", FC), ev("hm_ok", FC)
        c1_ok, zz_ok, ez_ok, coh_ok = ev("c1_ok", DC), ev("zz_ok", 1), ev("ez_ok", 1), ev("coh_ok", 3)
        sumv_ok = ev("sumv_ok", 1)
        rz_coh, on_field, attn2_ok = ev("rz_coh", TC), ev("on_field", TC), ev("attn2_ok", 1)
        rz_some, attn3_ok, sq3, ms3, inv3 = ev("rz_some", TC), ev("attn3_ok", 1), ev("sq3", TC), ev("ms3", 1), ev("inv3", 1)
        mod_l_ok, mod_ok, mod_sum, stored = ev("mod_l_ok", 1), ev("mod_ok", 2), ev("mod_sum", 4), ev("stored", 16)

        class Layer:

            def __init__(self, n):
                self.n = n
                self.cur_f, self.cur_b = ev(f"cur_f{n}", 1), ev(f"cur_b{n}", 1)
                self.staged, self.xt = ev(f"staged{n}", 1), ev(f"xt{n}", DC)
                self.q, self.k, self.vp = ev(f"q{n}", 1), ev(f"k{n}", 1), ev(f"vp{n}", 1)
                self.qk_hi, self.qk_lo, self.stacked = ev(f"qk_hi{n}", 1), ev(f"qk_lo{n}", 1), ev(f"stacked{n}", 16 * 12)
                self.rowmax, self.nm, self.shifted = ev(f"rowmax{n}", H), ev(f"nm{n}", 2), ev(f"shifted{n}", 32)
                self.probs, self.pv, self.o_raw = ev(f"probs{n}", H), ev(f"pv{n}", NG), ev(f"o_raw{n}", 2)
                self.rz, self.on, self.ot, self.x_new = ev(f"rz{n}", TC), ev(f"on{n}", TC), ev(f"ot{n}", 1), ev(f"x_new{n}", 1)

                head = {"spec": (h_spec_ok, 1), "rank": (h_rank_ok, 1), "cond": (x1_ok, 1)} if n == 1 else {}
                head |= {"xT": (self.xt, DC), "q": (self.q, 1), "k": (self.k, 1), "v": (self.vp, 1)}
                if n == 2:
                    head |= {"coh1": (c1_ok, DC), "coh2": (zz_ok, 1)}
                self.head = Ring(sem(f"head_full{n}"), banks[0:2], head)

                middle = {f"s{h}": (self.rowmax, h + 1) for h in range(H)} | {"max": (self.nm, 2)}
                self.middle = Ring(sem(f"middle_full{n}"), banks[2:4], middle)

                back = {f"p{h}": (self.probs, h + 1) for h in range(H)}
                back |= {"tok0": (self.on, 1), "tok1": (self.on, 2), "oT": (self.ot, 1)}
                back |= {"wo": ((y_ok, attn2_ok, attn3_ok)[n - 1], 1)}
                if n == 1:
                    back |= {"yT": (yt_ok, DC)} | {f"ffn{f}": (hm_ok, f + 1) for f in range(FC)} | {"down": (self.x_new, 1)}
                if n == 3:
                    back |= {"mod": (mod_ok, 2)}
                self.back = Ring(sem(f"back_full{n}"), banks[4:6], back)

        lay = {n: Layer(n) for n in LAYERS}
        L3 = lay[3]

        def run_layer(eng, L, step):
            order = order_of(L.n)

            def phase(b, par, *sides):
                for side, what, n in order:
                    if side in sides:
                        ahead = ("back", "middle", "head", "next").index(side)
                        step(what, n, b + ahead, (par + ahead) % 2)

            phase(-3, 1, "next")
            phase(-2, 0, "head", "next")
            phase(-1, 1, "middle", "head", "next")
            phase(0, 0, "back", "middle", "head", "next")
            phase(1, 1, "back", "middle", "head", "next")
            with eng.Fori(1, NBATCH // 2 - 2) as j:
                phase(2 * j, 0, "back", "middle", "head", "next")
                phase(2 * j + 1, 1, "back", "middle", "head", "next")
            phase(NBATCH - 4, 0, "back", "middle", "head", "next")
            phase(NBATCH - 3, 1, "back", "middle", "head")
            phase(NBATCH - 2, 0, "back", "middle")
            phase(NBATCH - 1, 1, "back")

        def layer_gate(eng, n):
            if n == 1:
                eng.wait_ge(s_setup, 1)
            else:
                eng.wait_ge(lay[n - 1].x_new.sem, NBATCH)
            eng.wait_ge(s_ld[n], 16 * len(loads[n]))

        def rows(name, n):
            return ins[name].rearrange("(a d) -> a d", a=1).to_broadcast([n, ins[name].shape[0]])

        loads0 = [(ident, "ident"), (raw, "raw"), (raw_t, "raw_t"), (below, "below"), (cond_a, "cond_a"),
                  (cond_w, "cond_w"), (we1, "we1"), (we2, "we2"), (be2, "be2"), (ln_gb, "ln_gb"), (pe_t, "pe_t"),
                  (w_basis, "w_basis"), (w_outb, "w_outb"), (mask_q, "mask_q"), (mask_k, "mask_k"),
                  (bqk, "bqk")]
        loads = {
            1: [(wqkvo[1], "wqkvo1"), (w_gate, "w_gate"), (w_hid, "w_hid"), (w_down, "w_down")],
            2: [(wqkvo[2], "wqkvo2"), (w_c1, "w_c1"), (w_c2, "w_c2"), (bv_rows, "bv"), (bout_rows, "bout"), (bc2_rows, "bc2")],
            3: [(wqkvo[3], "wqkvo3"), (w_mod, "w_mod"), (rms_rows, "rms")],
        }

        mark = {}

        block = ctx.enter_context(nc.Block())

        @block.vector
        def _(dve):
            count = [0]

            def link(a):
                count[0] += 1
                a.then_inc(s_vch, 1)
                dve.wait_ge(s_vch, count[0])

            dve.wait_ge(s_ld0, 16 * (len(loads0) + 2))
            link(dve.tensor_copy(ident_bf[:], ident[:]))
            link(dve.tensor_scalar(bqk[:, 0:DC], bqk[:, 0:DC], HD ** -0.5, None, ALU.mult))
            link(dve.tensor_scalar(big_q[:], mask_q[:], BIG, None, ALU.mult))
            link(dve.tensor_scalar(big_k[:], mask_k[:], BIG, None, ALU.mult))
            link(dve.tensor_scalar(keys_left[:], mask_q[:], -1.0, 1.0, ALU.mult, ALU.add))
            link(dve.tensor_reduce(some_key[:], keys_left[:], AX, ALU.add))
            link(dve.reciprocal(stat[:, 0, :], some_key[:]))
            link(dve.tensor_tensor(some_key[:], some_key[:], stat[:, 0, :], ALU.mult))
            dve.wait_ge(s_pe0, 1)
            link(dve.tensor_copy(cvec[:, 0:10, :], banks[4][:, 0:10 * NBATCH].rearrange("p (v b) -> p v b", v=10)))
            dve.wait_ge(s_act0, 1)
            link(dve.scalar_tensor_tensor(th_c[:], th_c[:], 1.0, cond_a[0:C, :], ALU.add, ALU.mult))
            dve.wait_ge(s_memset, 5)
            link(dve.tensor_scalar(cvec[0:C, SILU, :], th_c[:], 0.5, None, ALU.mult))
            link(dve.tensor_scalar(a1[:], banks[5][:, 0:DC * NBATCH].rearrange("p (c b) -> p c b", c=DC), 0.0, None, ALU.max))
            mark["A1"] = count[0]
            dve.wait_ge(s_pe0, 2)
            link(dve.tensor_reduce(fs[:, 0:1], banks[6][0:NBATCH, 0:D], AX, ALU.add))
            link(dve.tensor_scalar(fs[:, 0:1], fs[:, 0:1], -1.0 / D, None, ALU.mult))
            link(dve.tensor_scalar(fld[:, 0, :], banks[6][0:NBATCH, 0:D], fs[:, 0:1], None, ALU.add))
            link(dve.tensor_tensor(fld[:, 1, :], fld[:, 0, :], fld[:, 0, :], ALU.mult))
            link(dve.tensor_reduce(fs[:, 1:2], fld[:, 1, :], AX, ALU.add))
            link(dve.tensor_scalar(fs[:, 2:3], fs[:, 1:2], 1.0 / D, 1e-5, ALU.mult, ALU.add))
            mark["var"] = count[0]
            dve.wait_ge(s_pe0, 3)
            link(dve.scalar_tensor_tensor(gj[:, 0:C], ident[0:C, 0:C], 1e-4, banks[7][0:C, 0:C], ALU.mult, ALU.add))
            link(dve.tensor_copy(gj[:, C:2 * C], ident[0:C, 0:C]))
            dve.tensor_copy(gj_c[:, 0:1], ident[0:C, 0:1]).then_inc(s_gj_up, 1)
            with dve.Fori(0, C) as j:
                dve.wait_ge(s_gj_up, j + 1)
                dve.tensor_scalar(gj_row[:], gj[:], ident[0:C, bass.ds(j, 1)], None, ALU.mult).then_inc(s_gj_row, 1)
                dve.wait_ge(s_gj_bc, j * 3 + 1)
                dve.reciprocal(gj_c[:, 0:1], banks[0][0:C, bass.ds(j, 1)]).then_inc(s_gj_bc, 1)
                dve.wait_ge(s_gj_bc, j * 3 + 2)
                dve.scalar_tensor_tensor(gj_c[:, 1:2], gj[:, bass.ds(j, 1)], gj_c[:, 0:1], below[:, bass.ds(j, 1)],
                                         ALU.mult, ALU.mult).then_inc(s_gj_bc, 1)
                dve.wait_ge(s_gj_bc, j * 3 + 3)
                dve.scalar_tensor_tensor(gj[:], banks[0][0:C, 0:2 * C], gj_c[:, 1:2], gj[:], ALU.mult, ALU.add)\
                    .then_inc(s_gj_up, 1)
            dve.wait_ge(s_gj_up, C + 1)
            link(dve.tensor_tensor(gj_row[:, 0:C], gj[:, 0:C], ident[0:C, 0:C], ALU.mult))
            link(dve.tensor_reduce(gj_c[:, 2:3], gj_row[:, 0:C], AX, ALU.add))
            mark["D"] = count[0]
            dve.wait_ge(s_pool0, 2)
            link(dve.tensor_scalar(tinv[:], gj[:, C:2 * C], gj_c[:, 3:4], None, ALU.mult))
            dve.wait_ge(s_pe0, 4)
            link(dve.tensor_copy(tinv_t[:], banks[1][0:C, 0:C]))
            dve.wait_ge(s_pe0, 5)
            link(dve.tensor_copy(qmat[:], banks[2][0:C, 0:C]))
            link(dve.tensor_tensor(sgn[:], qmat[:], raw[:], ALU.mult))
            mark["Q"] = count[0]
            dve.wait_ge(s_pe0, 6)
            link(dve.tensor_scalar(sgn[:], banks[3][0:C, 0:C], 0.0, 2.0, ALU.is_ge, ALU.mult))
            link(dve.memset(mtr[:, C:P], 0.0))
            link(dve.scalar_tensor_tensor(mtr[:, 0:C], sgn[:], -1.0, qmat[:], ALU.add, ALU.mult))
            dve.wait_ge(s_pool0, 1)
            link(dve.tensor_scalar(fld[:, 0, :], fld[:, 0, :], fs[:, 3:4], None, ALU.mult))
            link(dve.tensor_tensor(fld[:, 0, :], fld[:, 0, :], ln_gb[:, 0, :], ALU.mult))
            link(dve.tensor_tensor(fld[:, 0, :], fld[:, 0, :], ln_gb[:, 1, :], ALU.add))
            mark["F"] = count[0]
            dve.wait_ge(s_pe0, 7)
            link(dve.tensor_copy(fld_t[:], banks[7][:, 0:DC * NBATCH].rearrange("p (c b) -> p c b", c=DC)))
            mark["FT"] = count[0]
            dve.wait_ge(s_pe0, 8)
            link(dve.tensor_reduce(fs[:, 4:5], banks[6][0:NBATCH, 0:S], AX, ALU.max))
            link(dve.tensor_scalar(fs[:, 5:6], fs[:, 4:5], -1.0, None, ALU.mult))
            mark["E"] = count[0]
            dve.wait_ge(s_act0, 2)
            link(dve.reciprocal(fs[:, 7:8], fs[:, 6:7]))
            link(dve.tensor_scalar(fld[:, 1, :], fld[:, 2, :], fs[:, 7:8], FI, ALU.mult, ALU.mult))
            mark["FA"] = count[0]
            dve.wait_ge(s_pe0, 9)
            link(dve.tensor_copy(cvec[:, FIELD:FIELD + TC, :], banks[7][:, 0:TC * NBATCH].rearrange("p (t b) -> p t b", t=TC)))
            dve.wait_ge(s_memset, 19)
            dve.tensor_copy(fs[:, 0:1], fs[:, 1:2]).then_inc(s_setup, 1)

            for n in LAYERS:
                L = lay[n]
                hd, md, bk = L.head, L.middle, L.back

                def step(what, k, b, par):
                    if what == "load":
                        dve.wait_ge(L.xt.sem, L.xt.at(b, 0))
                        if n == 2:
                            dve.wait_ge(c1_ok.sem, c1_ok.at(b, 0))
                        dve.tensor_scalar(cur_f[:], cvec[:, :, b], 1.0, None, ALU.mult).then_inc(L.cur_f.sem, 1)
                    if what == "vectors":
                        if n == 1:
                            dve.wait_ge(yt_ok.sem, yt_ok.at(b, 0))
                        dve.tensor_scalar(cur_b[:], cvec[:, :, b], 1.0, None, ALU.mult).then_inc(L.cur_b.sem, 1)
                    if what == "cond":
                        bank = hd.wait_filled(dve, b, "cond")
                        dve.wait_ge(x_loaded.sem, x_loaded.at(b, 32))
                        dve.tensor_tensor(xres[:, b, :, :], bank[:, :].rearrange("p (t d) -> p t d", t=TC), x_in[:], ALU.add)\
                            .then_inc(x1_ok.sem, 1)
                    if what == "xn":
                        dve.wait_ge(inv1.sem, inv1.at(b, 1))
                        for t in range(TC):
                            dve.tensor_scalar(xn[:, t, :], xres[:, b, t, :], stat[:, 2, t:t + 1], None, ALU.mult).then_inc(xn_ok.sem, 1)
                    if what == "stage":
                        dve.wait_ge(L.xt.sem, L.xt.at(b, 0))
                        dve.tensor_scalar(xn[:], xres[:, b, :, :], 1.0, None, ALU.mult).then_inc(L.staged.sem, 1)
                    if what == "k":
                        dve.wait_ge(L.qk_lo.sem, L.qk_lo.at(b, 0))
                        bank = hd.wait_filled(dve, b, "k")
                        if n == 2:
                            for c in range(DC):
                                a = dve.tensor_scalar(qk[:, DC + c, :], bank[:, c * S:(c + 1) * S], bqk[:, DC + c:DC + c + 1], None, ALU.add)
                        else:
                            a = dve.tensor_copy(qk[:, DC:2 * DC, :], bank[:, :].rearrange("p (c s) -> p c s", c=DC))
                        a.then_inc(L.k.sem, 1)
                    if what == "split":
                        dve.wait_ge(L.q.sem, L.q.at(b, 1))
                        dve.wait_ge(L.k.sem, L.k.at(b, 1))
                        if not (isinstance(b, int) and b < 2):
                            dve.wait_ge(L.pv.sem, L.pv.at(b - 1, 0))
                        dve.wait_ge(L.stacked.sem, L.stacked.at(b, 0))
                        dve.tensor_copy(qk_hi[:], qk[:]).then_inc(L.qk_hi.sem, 1)
                    if what == "v" and n == 2:
                        if not (isinstance(b, int) and b < 2):
                            dve.wait_ge(L.pv.sem, L.pv.at(b - 1, 0))
                        bank = hd.wait_filled(dve, b, "v")
                        for t in range(TC):
                            a = dve.tensor_tensor(vp[par][:, t, :, 0:HD], bank[:, t * D:(t + 1) * D].rearrange("p (h d) -> p h d", h=H),
                                                  bv_rows[:, :].rearrange("p (h d) -> p h d", h=H), ALU.add)
                        a.then_inc(L.vp.sem, 1)
                    if what == "coh2":
                        bank = hd.wait_filled(dve, b, "coh2")
                        for t in range(TC):
                            a = dve.tensor_tensor(zz[:, t, :], bank[:, t * H:(t + 1) * H], bc2_rows[:], ALU.add)
                        a.then_inc(zz_ok.sem, 1)
                        dve.wait_ge(ez_ok.sem, ez_ok.at(b, 1))
                        dve.tensor_scalar(coh[par][:], ez[:], 1e-8, 1.0 + 1e-8, ALU.mult, ALU.add).then_inc(coh_ok.sem, 1)
                        dve.wait_ge(coh_ok.sem, coh_ok.at(b, 1))
                        dve.reciprocal(coh[par][:], coh[par][:]).then_inc(coh_ok.sem, 1)
                        dve.wait_ge(coh_ok.sem, coh_ok.at(b, 2))
                        dve.tensor_scalar(coh[par][:], coh[par][:], 1.0 - FI, None, ALU.mult).then_inc(coh_ok.sem, 1)
                    if what == "smax":
                        bank = md.wait_filled(dve, b, f"s{k}")
                        dve.tensor_reduce(rowmax[:, :, k:k + 1], bank[:, :].rearrange("p (t s) -> p t s", t=TC), AX, ALU.max)\
                            .then_inc(L.rowmax.sem, 1)
                    if what == "max":
                        bank = md.wait_filled(dve, b, "max")
                        dve.wait_ge(L.shifted.sem, L.shifted.at(b, 0))
                        dve.tensor_scalar(nm_hi[:], bank[0:H, 0:S], -1.0, None, ALU.mult).then_inc(L.nm.sem, 1)
                        dve.wait_ge(L.nm.sem, L.nm.at(b, 1))
                        dve.scalar_tensor_tensor(nm_lo[:], bank[0:H, 0:S], -1.0, nm_hi[:], ALU.mult, ALU.subtract).then_inc(L.nm.sem, 1)
                    if what == "pv" and k % 2 == 1:
                        dve.wait_ge(L.pv.sem, L.pv.at(b, k + 1))
                        dve.tensor_copy(ot_raw[:, k - 1:k + 1, :], o_bank[k // 2][:, :].rearrange("p (g s) -> p g s", g=2)).then_inc(L.o_raw.sem, 1)
                    if what == "tok":
                        for t in range(TC):
                            bank = bk.wait_filled(dve, b, f"tok{t}")
                            grid = bank[:, :].rearrange("p (h w) -> p h w", w=HW)
                            dve.reciprocal(rz[:, t, :], grid[:, :, HD]).then_inc(L.rz.sem, 1)
                            dve.wait_ge(L.rz.sem, L.rz.at(b, t + 1))
                            if n == 2:
                                dve.tensor_tensor(rz[:, t, :], rz[:, t, :], coh[par][:, t, :], ALU.mult).then_inc(rz_coh.sem, 1)
                                dve.wait_ge(rz_coh.sem, rz_coh.at(b, t + 1))
                            if n == 3:
                                dve.tensor_scalar(rz[:, t, :], rz[:, t, :], some_key[:, t:t + 1], None, ALU.mult).then_inc(rz_some.sem, 1)
                                dve.wait_ge(rz_some.sem, rz_some.at(b, t + 1))
                            dve.tensor_tensor(on[:, t, :].rearrange("p (h d) -> p h d", h=H), grid[:, :, 0:HD],
                                              rz[:, t, :].rearrange("p (h a) -> p h a", a=1).to_broadcast([P, H, HD]), ALU.mult)\
                                .then_inc(L.on.sem, 1)
                            if n == 2:
                                dve.wait_ge(L.on.sem, L.on.at(b, t + 1))
                                dve.wait_ge(sumv_ok.sem, sumv_ok.at(b, 1))
                                dve.scalar_tensor_tensor(on[:, t, :], o_bank[0][:, 0:D], cur_b[:, FIELD + t:FIELD + t + 1], on[:, t, :],
                                                         ALU.mult, ALU.add).then_inc(on_field.sem, 1)
                    if what == "wo" and n == 1:
                        bank = bk.wait_filled(dve, b, "wo")
                        dve.wait_ge(xy_ok.sem, xy_ok.at(b, 0))
                        dve.tensor_tensor(y[:], bank[:, :].rearrange("p (t d) -> p t d", t=TC), xres[:, b, :, :], ALU.add).then_inc(y_ok.sem, 1)
                    if what == "wo" and n == 2:
                        bank = bk.wait_filled(dve, b, "wo")
                        dve.tensor_tensor(y[:], bank[:, :].rearrange("p (t d) -> p t d", t=TC),
                                          bout_rows[:, :].rearrange("p (a d) -> p a d", a=1).to_broadcast([P, TC, D]), ALU.add).then_inc(attn2_ok.sem, 1)
                        dve.wait_ge(attn2_ok.sem, attn2_ok.at(b, 1))
                        dve.tensor_tensor(xres[:, b, :, :], xres[:, b, :, :], y[:], ALU.add).then_inc(L.x_new.sem, 1)
                    if what == "yn":
                        dve.wait_ge(inv2.sem, inv2.at(b, 1))
                        for t in range(TC):
                            dve.tensor_scalar(yn[:, t, :], y[:, t, :], statb[:, 2, t:t + 1], None, ALU.mult).then_inc(yn_ok.sem, 1)
                    if what == "ffn":
                        bank = bk.bank(f"ffn{k}")
                        dve.wait_ge(th_ok.sem, th_ok.at(b, k + 1))
                        dve.scalar_tensor_tensor(act1[:, k % 2, :], th[:, k % 2, :], 1.0, bank[:, 0:S], ALU.add, ALU.mult).then_inc(act1_ok.sem, 1)
                        dve.wait_ge(act1_ok.sem, act1_ok.at(b, k + 1))
                        dve.scalar_tensor_tensor(hm[:, k, :], act1[:, k % 2, :], 0.5, bank[:, S:2 * S], ALU.mult, ALU.mult)\
                            .then_inc(hm_ok.sem, 1)
                    if what == "down":
                        bank = bk.wait_filled(dve, b, "down")
                        dve.wait_ge(xy_ok.sem, xy_ok.at(b, 1))
                        dve.tensor_tensor(xres[:, b, :, :], bank[:, :].rearrange("p (t d) -> p t d", t=TC), xres[:, b, :, :], ALU.add)\
                            .then_inc(L.x_new.sem, 1)
                    if what == "mod":
                        bank = bk.wait_filled(dve, b, "mod")
                        dve.scalar_tensor_tensor(mod_a[:], bank[:, D:2 * D], 1.0, rms_rows[:], ALU.add, ALU.mult).then_inc(mod_ok.sem, 1)
                        dve.tensor_copy(mod_s[:], bank[:, 0:D]).then_inc(mod_ok.sem, 1)
                        dve.wait_ge(mod_ok.sem, mod_ok.at(b, 2))
                        dve.wait_ge(inv3.sem, inv3.at(b, 1))
                        for t in range(TC):
                            dve.scalar_tensor_tensor(y[:, t, :], y[:, t, :], statb[:, 2, t:t + 1], mod_a[:], ALU.mult, ALU.mult).then_inc(mod_sum.sem, 1)
                        for t in range(TC):
                            dve.wait_ge(mod_sum.sem, mod_sum.at(b, t + 1))
                            dve.tensor_tensor(y[:, t, :], y[:, t, :], mod_s[:], ALU.add).then_inc(mod_sum.sem, 1)
                        dve.wait_ge(mod_sum.sem, mod_sum.at(b, 4))
                        dve.tensor_tensor(xres[:, b, :, :], xres[:, b, :, :], y[:], ALU.add).then_inc(L.x_new.sem, 1)

                layer_gate(dve, n)
                run_layer(dve, L, step)

        @block.sync
        def _(sp):
            for tile, name in loads0:
                sp.dma_start(tile[:], ins[name]).then_inc(s_ld0, 16)
            sp.wait_ge(s_memset, 5)
            sp.dma_start(cvec[0:C, SPEC, :], ins["cond_a"][0:C, :]).then_inc(s_ld0, 16)
            sp.dma_start(cvec[0:C, RANK, :], ins["cond_64t"]).then_inc(s_ld0, 16)
            def load_layer(n):
                for tile, name in loads[n]:
                    src = ins[name]
                    if len(src.shape) == 1:
                        src = rows(name, P)
                    sp.dma_start(tile[:], src).then_inc(s_ld[n], 16)

            load_layer(1)
            for n in LAYERS:
                L = lay[n]
                if n == 2:
                    sp.wait_ge(lay[1].x_new.sem, NBATCH)
                    load_layer(2)
                    load_layer(3)

                def step(what, k, b, par):
                    if what == "load" and n == 1:
                        sp.wait_ge(x1_ok.sem, x1_ok.at(b, 0))
                        sp.wait_ge(s_setup, 1)
                        sp.dma_start(x_in[:], ins["x"][b].rearrange("(t p) d -> p t d", p=P)).then_inc(x_loaded.sem, 16)
                        sp.dma_start(xt_in[:], ins["x_t"][b]).then_inc(x_loaded.sem, 16)
                    if what == "split":
                        sp.wait_ge(L.qk_hi.sem, L.qk_hi.at(b, 1))
                        for r, (q_part, k_part) in enumerate(((qk_hi, qk_hi), (qk_lo, qk_hi), (qk_hi, qk_lo))):
                            if r == 1:
                                sp.wait_ge(L.qk_lo.sem, L.qk_lo.at(b, 1))
                            for dst, src, c0 in ((qs[par], q_part, 0), (ks[par], k_part, DC)):
                                for c in range(DC):
                                    sp.dma_start(dst[HD * r:HD * (r + 1), 8 * c:8 * c + 8, :].bitcast(F32),
                                                 src[:, c0 + c, :].bitcast(F32)).then_inc(L.stacked.sem, 16)
                    if what == "max":
                        sp.wait_ge(L.nm.sem, L.nm.at(b, 2))
                        for r, part in enumerate((nm_hi, nm_lo)):
                            sp.dma_start(qs[par][SHIFT + r:SHIFT + r + 1, :, :].bitcast(F32),
                                         part[:, :].bitcast(F32)).then_inc(L.shifted.sem, 16)
                    if what == "mod":
                        sp.wait_ge(L3.x_new.sem, L3.x_new.at(b, 1))
                        sp.wait_ge(s_setup, 1)
                        sp.dma_start(out[b].rearrange("(t p) d -> p t d", p=P), xres[:, b, :, :]).then_inc(stored.sem, 16)

                layer_gate(sp, n)
                run_layer(sp, L, step)
            sp.wait_ge(stored.sem, 16 * NBATCH)

        @block.gpsimd
        def _(pool):
            clears = [(ones[:], 1.0), (half[:], -0.5), (guard[:], 1e-6), (cvec[:], 0.0), (cvec[C:CA, SILU, :], 1.0)]
            for i in range(2):
                clears += [(qs[i][32:64, :, :].bitcast(F32), 0.0), (qs[i][64:96, :, :].bitcast(F32), 0.0),
                           (ks[i][32:64, :, :].bitcast(F32), 0.0), (ks[i][64:96, :, :].bitcast(F32), 0.0),
                           (ks[i][96:98, :, :].bitcast(F32), 1.0), (vp[i][:, :, :, HD:HW], 0.0), (vp[i][:, :, :, HD:HD + 1], 1.0)]
            assert len(clears) == 19
            for k, (tile, value) in enumerate(clears):
                if k:
                    pool.wait_ge(s_memset, k)
                pool.memset(tile, value).then_inc(s_memset, 1)
            pool.wait_ge(s_memset, len(clears))

            pool.wait_ge(s_vch, mark["var"])
            pool.tensor_tensor(fs[:, 3:4], fs[:, 2:3], half[0:NBATCH, 0:1], ALU.pow).then_inc(s_pool0, 1)
            pool.wait_ge(s_vch, mark["D"])
            pool.tensor_tensor(gj_c[:, 3:4], gj_c[:, 2:3], half[0:C, 0:1], ALU.pow).then_inc(s_pool0, 1)

            for n in LAYERS:
                L = lay[n]

                def step(what, k, b, par):
                    if what == "cond":
                        rsqrt(b, stat, sq1, ms1, inv1)
                    if what == "split":
                        pool.wait_ge(L.qk_hi.sem, L.qk_hi.at(b, 1))
                        pool.wait_ge(L.stacked.sem, L.stacked.at(b, 0))
                        pool.tensor_tensor(qk_lo[:], qk[:], qk_hi[:], ALU.subtract).then_inc(L.qk_lo.sem, 1)
                    if what == "yn":
                        rsqrt(b, statb, sq2, ms2, inv2)
                        pool.tensor_tensor(xres[:, b, :, :], xres[:, b, :, :], y[:], ALU.add).then_inc(xy_ok.sem, 1)
                    if what == "wo" and n == 3:
                        pool.wait_ge(mod_ok.sem, mod_ok.at(b, 0))
                        pool.wait_ge(L.cur_b.sem, L.cur_b.at(b, 1))
                        pool.tensor_tensor(mod_l[:], ones[0:CA, :], cur_b[0:CA, SILU:SILU + 1].to_broadcast([CA, P]), ALU.mult).then_inc(mod_l_ok.sem, 1)
                        rsqrt(b, statb, sq3, ms3, inv3)

                def rsqrt(b, st, sq, ms, inv):
                    pool.wait_ge(sq.sem, sq.at(b, TC))
                    pool.tensor_tensor(st[:, 1, :], st[:, 0, :], guard[:], ALU.add).then_inc(ms.sem, 1)
                    pool.wait_ge(ms.sem, ms.at(b, 1))
                    pool.tensor_tensor(st[:, 2, :], st[:, 1, :], half[:], ALU.pow).then_inc(inv.sem, 1)

                layer_gate(pool, n)
                run_layer(pool, L, step)

        @block.scalar
        def _(act):
            act.wait_ge(s_ld0, 16 * (len(loads0) + 2))
            act.activation(th_c[:], cond_a[0:C, :], ACT.Tanh, scale=0.5).then_inc(s_act0, 1)
            act.wait_ge(s_vch, mark["E"])
            act.activation(fld[:, 2, :], banks[6][0:NBATCH, 0:S], ACT.Exp, bias=fs[:, 5:6],
                           accum_out=fs[:, 6:7]).then_inc(s_act0, 1)

            for n in LAYERS:
                L = lay[n]
                hd, md, bk = L.head, L.middle, L.back

                def step(what, k, b, par):
                    if what == "spec":
                        t = hd.wait_filled(act, b, "spec")
                        act.wait_ge(L.cur_f.sem, L.cur_f.at(b, 1))
                        act.activation(h_spec[:], t[0:C, 0:S], ACT.Identity, scale=cur_f[0:C, SPEC:SPEC + 1]).then_inc(h_spec_ok.sem, 1)
                    if what == "rank":
                        t = hd.wait_filled(act, b, "rank")
                        act.activation(h_rank[:], t[0:C, 0:S], ACT.Identity, scale=cur_f[0:C, RANK:RANK + 1]).then_inc(h_rank_ok.sem, 1)
                    if what == "cond":
                        act.wait_ge(x1_ok.sem, x1_ok.at(b, 1))
                        for t in range(TC):
                            act.activation(xn[:, t, :], xres[:, b, t, :], ACT.Square, scale=D ** -0.5, accum_out=stat[:, 0, t:t + 1]).then_inc(sq1.sem, 1)
                    if what == "xT":
                        bank = hd.wait_filled(act, b, "xT")
                        for c in range(DC):
                            src = bank[:, c * S:(c + 1) * S]
                            if n == 1:
                                a = act.activation(xt[:, c, :], src, ACT.Identity, scale=cur_f[:, G1 + c:G1 + c + 1],
                                                   bias=cur_f[:, B1 + c:B1 + c + 1])
                            else:
                                a = act.copy(xt[:, c, :], src)
                            a.then_inc(L.xt.sem, 1)
                    if what == "q":
                        act.wait_ge(L.qk_lo.sem, L.qk_lo.at(b, 0))
                        bank = hd.wait_filled(act, b, "q")
                        if n == 2:
                            for c in range(DC):
                                a = act.activation(qk[:, c, :], bank[:, c * S:(c + 1) * S], ACT.Identity,
                                                   scale=HD ** -0.5, bias=bqk[:, c:c + 1])
                        else:
                            a = act.activation(qk[:, 0:DC, :], bank[:, :].rearrange("p (c s) -> p c s", c=DC), ACT.Copy, scale=HD ** -0.5)
                        a.then_inc(L.q.sem, 1)
                    if what == "v" and n != 2:
                        if not (isinstance(b, int) and b < 2):
                            act.wait_ge(L.pv.sem, L.pv.at(b - 1, 0))
                        bank = hd.wait_filled(act, b, "v")
                        act.copy(vp[par][:, :, :, 0:HD], bank[:, :].rearrange("p (t h d) -> p t h d", t=TC, h=H)).then_inc(L.vp.sem, 1)
                    if what == "coh1":
                        bank = hd.wait_filled(act, b, "coh1")
                        for c in range(DC):
                            act.activation(c1t[:, c, :], bank[:, c * S:(c + 1) * S], ACT.Tanh,
                                           bias=cur_f[:, C1 + c:C1 + c + 1]).then_inc(c1_ok.sem, 1)
                    if what == "coh2":
                        act.wait_ge(zz_ok.sem, zz_ok.at(b, 1))
                        act.wait_ge(coh_ok.sem, coh_ok.at(b, 0))
                        act.activation(ez[:], zz[:], ACT.Exp, scale=-1.0).then_inc(ez_ok.sem, 1)
                    if what == "probs":
                        bank = bk.wait_filled(act, b, f"p{k}")
                        act.wait_ge(L.pv.sem, L.pv.at(b, 0 if k < PBUF else (k - PBUF) // HG + 1))
                        act.activation(probs[:, k % PBUF, :, :], bank[:, :].rearrange("p (c s) -> p c s", c=TC), ACT.Exp)\
                            .then_inc(L.probs.sem, 1)
                    if what == "oT":
                        bank = bk.wait_filled(act, b, "oT")
                        act.copy(ot[:], bank[:, :].rearrange("p (c s) -> p c s", c=DC)).then_inc(L.ot.sem, 1)
                    if what == "wo" and n == 1:
                        act.wait_ge(y_ok.sem, y_ok.at(b, 1))
                        for t in range(TC):
                            act.activation(yn[:, t, :], y[:, t, :], ACT.Square, scale=D ** -0.5, accum_out=statb[:, 0, t:t + 1]).then_inc(sq2.sem, 1)
                    if what == "wo" and n == 3:
                        bank = bk.wait_filled(act, b, "wo")
                        act.wait_ge(L.x_new.sem, L.x_new.at(b, 0))
                        act.copy(y[:], bank[:, :].rearrange("p (t d) -> p t d", t=TC)).then_inc(attn3_ok.sem, 1)
                        act.wait_ge(attn3_ok.sem, attn3_ok.at(b, 1))
                        for t in range(TC):
                            act.activation(yn[:, t, :], y[:, t, :], ACT.Square, scale=D ** -0.5, accum_out=statb[:, 0, t:t + 1]).then_inc(sq3.sem, 1)
                    if what == "yT":
                        bank = bk.wait_filled(act, b, "yT")
                        for c in range(DC):
                            act.activation(yt[:, c, :], bank[:, c * S:(c + 1) * S], ACT.Identity, scale=cur_b[:, G2 + c:G2 + c + 1],
                                           bias=cur_b[:, B2 + c:B2 + c + 1]).then_inc(yt_ok.sem, 1)
                    if what == "ffn":
                        bank = bk.wait_filled(act, b, f"ffn{k}")
                        act.wait_ge(act1_ok.sem, act1_ok.at(b, max(k - 1, 0)))
                        act.activation(th[:, k % 2, :], bank[:, 0:S], ACT.Tanh, scale=0.5).then_inc(th_ok.sem, 1)

                layer_gate(act, n)
                run_layer(act, L, step)

        @block.tensor
        def _(pe):
            pe.wait_ge(s_ld0, 16 * (len(loads0) + 2))
            for v in range(10):
                pe.matmul(banks[4][:, v * NBATCH:(v + 1) * NBATCH], cond_w[:, v, :], cond_a[:], start=True, stop=True)
            for c in range(DC):
                m = pe.matmul(banks[5][:, c * NBATCH:(c + 1) * NBATCH], we1[:, c * P:(c + 1) * P], cond_a[:], start=True, stop=True)
            m.then_inc(s_pe0, 1)
            pe.wait_ge(s_memset, 1)
            pe.wait_ge(s_vch, mark["A1"])
            for c in range(DC):
                pe.matmul(banks[6][0:NBATCH, 0:D], a1[:, c, :], we2[:, c, :], start=(c == 0), stop=False)
            pe.matmul(banks[6][0:NBATCH, 0:D], ones[0:1, 0:NBATCH], be2[:], start=False, stop=True).then_inc(s_pe0, 1)
            pe.matmul(banks[7][0:C, 0:C], raw[:], raw[:], start=True, stop=True).then_inc(s_pe0, 1)
            with pe.Fori(0, C) as j:
                pe.wait_ge(s_gj_row, j + 1)
                pe.matmul(banks[0][:, 0:2 * C], ones[0:C, :], gj_row[:], start=True, stop=True).then_inc(s_gj_bc, 1)
            pe.wait_ge(s_vch, mark["D"] + 1)
            pe.transpose(banks[1][0:C, 0:C], tinv[:], ident[0:C, 0:C]).then_inc(s_pe0, 1)
            pe.wait_ge(s_vch, mark["D"] + 2)
            pe.matmul(banks[2][0:C, 0:C], raw_t[:], tinv_t[:], start=True, stop=True).then_inc(s_pe0, 1)
            pe.wait_ge(s_vch, mark["Q"])
            pe.matmul(banks[3][0:C, 0:C], ones[0:C, 0:C], sgn[:], start=True, stop=True).then_inc(s_pe0, 1)
            pe.wait_ge(s_vch, mark["F"])
            for c in range(DC):
                m = pe.transpose(banks[7][:, c * NBATCH:(c + 1) * NBATCH], fld[:, 0, c * P:(c + 1) * P], ident[0:NBATCH, 0:NBATCH])
            m.then_inc(s_pe0, 1)
            pe.wait_ge(s_vch, mark["FT"])
            for c in range(DC):
                m = pe.matmul(banks[6][0:NBATCH, 0:S], fld_t[:, c, :], pe_t[:, c, :], start=(c == 0), stop=(c == DC - 1))
            m.then_inc(s_pe0, 1)
            pe.wait_ge(s_vch, mark["FA"])
            for t in range(TC):
                m = pe.transpose(banks[7][:, t * NBATCH:(t + 1) * NBATCH], fld[:, 1, t * P:(t + 1) * P], ident[0:NBATCH, 0:NBATCH])
            m.then_inc(s_pe0, 1)

            for n in LAYERS:
                L = lay[n]
                hd, md, bk = L.head, L.middle, L.back
                w = wqkvo[n]

                def outputs_first(bank, weights, acts):
                    for c in range(DC):
                        for i in range(DC):
                            m = pe.matmul(bank[:, c * S:(c + 1) * S], weights[:, i, c * P:(c + 1) * P], acts[:, i, :],
                                          start=(i == 0), stop=(i == DC - 1))
                    return m

                def tokens_first(bank, acts, weights, n_in=DC, width=D):
                    for t in range(TC):
                        for i in range(n_in):
                            m = pe.matmul(bank[:, t * width:(t + 1) * width], acts[:, i, t * P:(t + 1) * P], weights[:, i, :],
                                          start=(i == 0), stop=(i == n_in - 1))
                    return m

                def transposes(bank, src):
                    for c in range(DC):
                        for t in range(TC):
                            m = pe.transpose(bank[:, c * S + t * P:c * S + (t + 1) * P], src[:, t, c * P:(c + 1) * P], ident[:])
                    return m

                def step(what, k, b, par):
                    if what == "spec":
                        pe.wait_ge(x_loaded.sem, x_loaded.at(b, 32))
                        hd.wait_free(pe, b, "spec")
                        for c in range(DC):
                            m = pe.matmul(hd.bank("spec")[0:C, 0:S], w_basis[:, c, :], xt_in[:, c, :], start=(c == 0), stop=(c == DC - 1))
                        m.then_inc(hd.full.sem, 1)
                    if what == "rank":
                        pe.wait_ge(h_spec_ok.sem, h_spec_ok.at(b, 1))
                        hd.wait_free(pe, b, "rank")
                        pe.matmul(hd.bank("rank")[:, 0:S], mtr[:], h_spec[:], start=True, stop=True).then_inc(hd.full.sem, 1)
                    if what == "cond":
                        pe.wait_ge(h_rank_ok.sem, h_rank_ok.at(b, 1))
                        hd.wait_free(pe, b, "cond")
                        for t in range(TC):
                            m = pe.matmul(hd.bank("cond")[:, t * D:(t + 1) * D], h_rank[:, t * P:(t + 1) * P], w_outb[:], start=True, stop=True)
                        m.then_inc(hd.full.sem, 1)
                    if what == "xT":
                        if n == 1:
                            pe.wait_ge(xn_ok.sem, xn_ok.at(b, 2))
                        else:
                            pe.wait_ge(L.staged.sem, L.staged.at(b, 1))
                        hd.wait_free(pe, b, "xT")
                        transposes(hd.bank("xT"), xn).then_inc(hd.full.sem, 1)
                    if what in ("q", "k"):
                        pe.wait_ge(L.xt.sem, L.xt.at(b, 2))
                        hd.wait_free(pe, b, what)
                        outputs_first(hd.bank(what), w[:, "qk".index(what)], xt).then_inc(hd.full.sem, 1)
                    if what == "v":
                        hd.wait_free(pe, b, "v")
                        tokens_first(hd.bank("v"), xt, w[:, 2]).then_inc(hd.full.sem, 1)
                    if what == "coh1":
                        hd.wait_free(pe, b, "coh1")
                        outputs_first(hd.bank("coh1"), w_c1, xt).then_inc(hd.full.sem, 1)
                    if what == "coh2":
                        pe.wait_ge(c1_ok.sem, c1_ok.at(b, 2))
                        hd.wait_free(pe, b, "coh2")
                        tokens_first(hd.bank("coh2"), c1t, w_c2, width=H).then_inc(hd.full.sem, 1)
                    if what == "smax":
                        if k == 0:
                            pe.wait_ge(L.stacked.sem, L.stacked.at(b, 16 * 12))
                        md.wait_free(pe, b, f"s{k}")
                        bank = md.bank(f"s{k}")
                        for t in range(TC):
                            m = pe.matmul(bank[:, t * S:(t + 1) * S], qs[par][0:SCORE_ROWS, k, t * P:(t + 1) * P], ks[par][0:SCORE_ROWS, k, :],
                                          start=True, stop=(n != 3))
                            if n == 3:
                                m = pe.matmul(bank[:, t * S:(t + 1) * S], ident_bf[:], big_q[:, t, :], start=False, stop=True)
                        m.then_inc(md.full.sem, 1)
                    if what == "max":
                        pe.wait_ge(L.rowmax.sem, L.rowmax.at(b, H))
                        md.wait_free(pe, b, "max")
                        for t in range(TC):
                            m = pe.transpose(md.bank("max")[0:H, t * P:(t + 1) * P], rowmax[:, t, :], ident[:])
                        m.then_inc(md.full.sem, 1)
                    if what == "probs":
                        if k == 0:
                            pe.wait_ge(L.shifted.sem, L.shifted.at(b, 32))
                        bk.wait_free(pe, b, f"p{k}")
                        bank = bk.bank(f"p{k}")
                        for c in range(TC):
                            m = pe.matmul(bank[:, c * S:(c + 1) * S], ks[par][0:SHIFTED_ROWS, k, c * P:(c + 1) * P], qs[par][0:SHIFTED_ROWS, k, :],
                                          start=True, stop=(n != 3))
                            if n == 3:
                                m = pe.matmul(bank[:, c * S:(c + 1) * S], ident_bf[:], big_k[:, c, :], start=False, stop=True)
                        m.then_inc(bk.full.sem, 1)
                    if what == "pv":
                        if k == 0:
                            pe.wait_ge(L.vp.sem, L.vp.at(b, 1))
                            pe.wait_ge(L.o_raw.sem, L.o_raw.at(b, 0))
                        pe.wait_ge(L.probs.sem, L.probs.at(b, HG * (k + 1)))
                        for c in range(TC):
                            for i in range(HG):
                                h = HG * k + i
                                m = pe.matmul(o_bank[k // 2][HW * i:HW * (i + 1), (k % 2) * S:(k % 2 + 1) * S], vp[par][:, c, h, :],
                                              probs[:, h % PBUF, c, :], start=(c == 0), stop=(c == TC - 1))
                        m.then_inc(L.pv.sem, 1)
                    if what == "sumv":
                        pe.wait_ge(L.o_raw.sem, L.o_raw.at(b, 1))
                        for c in range(TC):
                            m = pe.matmul(o_bank[0][:, 0:D], ones[:], vp[par][:, c, :, 0:HD], start=(c == 0), stop=(c == TC - 1))
                        m.then_inc(sumv_ok.sem, 1)
                    if what == "tok":
                        pe.wait_ge(L.o_raw.sem, L.o_raw.at(b, 2))
                        for t in range(TC):
                            bk.wait_free(pe, b, f"tok{t}")
                            for g in range(NG):
                                m = pe.transpose(bk.bank(f"tok{t}")[:, g * P:(g + 1) * P], ot_raw[:, g, t * P:(t + 1) * P], ident[:])
                            m.then_inc(bk.full.sem, 1)
                    if what == "oT":
                        done = on_field if n == 2 else L.on
                        pe.wait_ge(done.sem, done.at(b, TC))
                        bk.wait_free(pe, b, "oT")
                        transposes(bk.bank("oT"), on).then_inc(bk.full.sem, 1)
                    if what == "wo":
                        pe.wait_ge(L.ot.sem, L.ot.at(b, 1))
                        bk.wait_free(pe, b, "wo")
                        tokens_first(bk.bank("wo"), ot, w[:, 3]).then_inc(bk.full.sem, 1)
                    if what == "yT":
                        pe.wait_ge(yn_ok.sem, yn_ok.at(b, 2))
                        bk.wait_free(pe, b, "yT")
                        transposes(bk.bank("yT"), yn).then_inc(bk.full.sem, 1)
                    if what == "ffn":
                        if k == 0:
                            pe.wait_ge(yt_ok.sem, yt_ok.at(b, 2))
                        bk.wait_free(pe, b, f"ffn{k}")
                        bank = bk.bank(f"ffn{k}")
                        for j, wt in enumerate((w_gate, w_hid)):
                            for c in range(DC):
                                m = pe.matmul(bank[:, j * S:(j + 1) * S], wt[:, c, k * P:(k + 1) * P], yt[:, c, :], start=(c == 0), stop=(c == DC - 1))
                        m.then_inc(bk.full.sem, 1)
                    if what == "down":
                        bk.wait_free(pe, b, "down")
                        for f in range(FC):
                            if f == FC - 1:
                                pe.wait_ge(hm_ok.sem, hm_ok.at(b, FC))
                            for t in range(TC):
                                m = pe.matmul(bk.bank("down")[:, t * D:(t + 1) * D], hm[:, f, t * P:(t + 1) * P], w_down[:, f, :],
                                              start=(f == 0 and t == 0), stop=(f == FC - 1 and t == TC - 1))
                        m.then_inc(bk.full.sem, 1)
                    if what == "mod":
                        pe.wait_ge(mod_l_ok.sem, mod_l_ok.at(b, 1))
                        bk.wait_free(pe, b, "mod")
                        pe.matmul(bk.bank("mod")[:, :], mod_l[:], w_mod[:], start=True, stop=True).then_inc(bk.full.sem, 1)

                layer_gate(pe, n)
                run_layer(pe, L, step)


def chunked(a):
    return np.ascontiguousarray(a.reshape(-1, P, a.shape[1]).transpose(1, 0, 2))


def by_dim(a):
    return a.reshape(*a.shape[:-1], 2, 8, HD).swapaxes(-1, -2).reshape(a.shape)


def position_table():
    pos = np.arange(S, dtype=np.float32)
    inv = np.float32(10000.0) ** np.repeat(np.arange(0, D, 2, dtype=np.float32) / np.float32(D), 2)
    return np.sin(pos[:, None] / inv[None, :]).astype(np.float32)


def layouts(v):
    one = np.ones((1, 1), np.float32)
    with_bias = lambda w, b: np.concatenate([w.T, b[None, :]], 0)
    cond_w = np.concatenate([
        with_bias(v["L1_cond_g1w"], v["L1_cond_g1b"]), with_bias(v["L1_cond_b1w"], v["L1_cond_b1b"]),
        with_bias(v["L1_cond_g2w"], v["L1_cond_g2b"]), with_bias(v["L1_cond_b2w"], v["L1_cond_b2b"]),
        with_bias(v["L2_cond_Wc1"][:, D:], v["L2_cond_bc1"])], 1).reshape(CA, 10, P)
    qkvo = lambda q, k, vv, o: np.stack([chunked(by_dim(q.T)), chunked(by_dim(k.T)), chunked(vv.T), chunked(o.T)], 1)
    w2 = v["L2_cond_Wqkv"].reshape(3, D, D)
    b2 = v["L2_cond_bqkv"].reshape(3, D)
    mask = v["mask_SxS_bk1"]
    return {
        "x": v["x"], "x_t": v["x"].transpose(0, 2, 1).reshape(NBATCH, DC, P, S).transpose(0, 2, 1, 3),
        "ident": np.eye(P, dtype=np.float32), "below": -np.tril(np.ones((C, C), np.float32), -1),
        "raw": v["L0_cond_mode_to_rank"], "raw_t": v["L0_cond_mode_to_rank"].T,
        "cond_a": np.concatenate([v["cond_256"].T, np.repeat(one, NBATCH, 1)], 0), "cond_64t": v["cond_64"].T,
        "cond_w": cond_w, "we1": with_bias(v["L2_cond_We1"], v["L2_cond_be1"]), "we2": chunked(v["L2_cond_We2"].T),
        "be2": v["L2_cond_be2"][None, :],
        "ln_gb": np.broadcast_to(np.stack([v["L2_cond_ln_g"], v["L2_cond_ln_b"]])[None], (NBATCH, 2, D)),
        "pe_t": chunked(position_table().T),
        "w_basis": chunked(v["L0_cond_input_basis"].T), "w_outb": v["L0_cond_output_basis"],
        "mask_q": chunked(mask), "mask_k": chunked(mask.T),
        "bqk": np.concatenate([by_dim(b2[0]).reshape(DC, P), by_dim(b2[1]).reshape(DC, P)]).T,
        "wqkvo1": qkvo(v["L1_cond_Wq"], v["L1_cond_Wk"], v["L1_cond_Wv"], v["L1_cond_Wo"]),
        "w_gate": chunked(v["L1_cond_gate_w"].T), "w_hid": chunked(v["L1_cond_hid_w"].T), "w_down": chunked(v["L1_cond_out_w"].T),
        "wqkvo2": qkvo(w2[0], w2[1], w2[2], v["L2_cond_Wout"]),
        "w_c1": chunked(v["L2_cond_Wc1"][:, :D].T), "w_c2": chunked(v["L2_cond_Wc2"].T),
        "bv": b2[2], "bout": v["L2_cond_bout"], "bc2": v["L2_cond_bc2"],
        "wqkvo3": qkvo(v["L3_cond_Wq"], v["L3_cond_Wk"], v["L3_cond_Wv"], v["L3_cond_Wo"]),
        "w_mod": with_bias(v["L3_cond_Wc"], v["L3_cond_bc"]), "rms": v["L3_cond_rms_scale"],
    }


def kernel(**inputs):
    import concourse.bacc as bacc
    from concourse.bass_utils import run_bass_kernel_spmd

    nc = bacc.Bacc("TRN2", target_bir_lowering=False, num_devices=1)
    arrays, ins = {}, {}
    for name, a in layouts({k: np.asarray(a) for k, a in inputs.items()}).items():
        a = np.ascontiguousarray(a)
        arrays[f"in_{name}"] = a
        ins[name] = nc.dram_tensor(f"in_{name}", a.shape, mybir.dt.from_np(a.dtype), kind="ExternalInput").ap()
    out = nc.dram_tensor("out", (NBATCH, S, D), F32, kind="ExternalOutput").ap()
    cond_resid_kernel(nc, ins, out)
    r = run_bass_kernel_spmd(nc, [arrays], core_ids=[0])
    return r.results[0]["out"]
```

```python
from contextlib import ExitStack

import numpy as np
import concourse.bass as bass
from concourse import mybir

F32 = mybir.dt.float32
F32R = mybir.dt.float32r
BF16 = mybir.dt.bfloat16
ALU = mybir.AluOpType
ACT = mybir.ActivationFunctionType
AX = mybir.AxisListType.X

P = 128
NBATCH, S, D = 16, 256, 256
H, HD = 16, 16
TC, DC = S // P, D // P
C = 64
HC = C // 2
CA = C + 1
FF = 1024
FC = FF // P
HG = 4
NG = H // HG
HW = 32
PBUF = 8
LAYERS = (1, 2, 3)
AHEAD = {"tail": -1, "back": 0, "middle": 1, "head": 2, "next": 3}
FIRST_ALONE, LAST_ALONE = 2, NBATCH - 4
FI = 0.3 * 0.7
BIG = -1e30

SHIFT = 96
SCORE_ROWS, SHIFTED_ROWS = SHIFT, SHIFT + 2

G1, B1, G2, B2, C1, SPEC, RANK, FIELD, SILU = 0, 2, 4, 6, 8, 10, 11, 12, 14
NV = 15


class Event:

    def __init__(self, sem, per, base=0):
        self.sem, self.per, self.base = sem, per, base

    def at(self, b, k):
        return b * self.per + (k + self.base)

    def after(self, batches):
        return Event(self.sem, self.per, self.base + batches * self.per)


class Ring:

    def __init__(self, sem, banks, readers):
        self.banks, self.readers, self.uses = banks, readers, list(readers)
        self.full = Event(sem, len(readers))

    def bank(self, use):
        return self.banks[self.uses.index(use) % len(self.banks)]

    def wait_filled(self, eng, b, use):
        eng.wait_ge(self.full.sem, self.full.at(b, self.uses.index(use) + 1))
        return self.bank(use)

    def wait_free(self, pe, b, use):
        u, n = self.uses.index(use), len(self.banks)
        if u >= n:
            event, k = self.readers[self.uses[u - n]]
            pe.wait_ge(event.sem, event.at(b, k))
        else:
            event, _ = self.readers[self.uses[u::n][-1]]
            pe.wait_ge(event.sem, event.at(b, 0))
        return self.bank(use)


def order_of(layer):
    out = []

    def add(side, what, first=0, end=None):
        out.extend((side, what, n) for n in range(first, first + 1 if end is None else end))

    maxima_here = 11 if layer == 1 else H
    maxima_after = {h: 1 for h in range(H - maxima_here, H)} if layer == 1 else {h: 1 + (h == 9) for h in range(1, H)}
    head = lambda *steps: [("head", *step) for step in steps]
    between = {1: {1: head(["cond"]), 4: head(["squares"]), 7: head(["xn"]), 9: head(["xT"]), 11: [("next", "load")]},
               2: {0: head(["stage"]), 3: [("middle", "coh2")], 5: [("middle", "coh3")], 6: head(["xT"]), 10: head(["q"]),
                   12: head(["split", 0])},
               3: {0: head(["stage"]), 1: [("tail", "squares")], 4: [("tail", "resid")], 6: head(["xT"]), 9: [("back", "mod")],
                   10: head(["q"]), 12: head(["split", 0])}}[layer]
    add("back", "vectors")
    maxima = 0
    for h in range(H):
        add("back", "probs", h)
        for step in between.get(h, ()):
            add(*step)
        if h % HG == 1 and h > HG:
            add("back", "pv", h // HG - 1)
        add("middle", "smax", maxima, maxima + maxima_after.get(h, 0))
        maxima += maxima_after.get(h, 0)
    assert maxima == maxima_here
    add("back", "pv", NG - 1)
    if layer == 1:
        add("head", "q")
        add("head", "split", 0)
        add("back", "tok")
        add("head", "k")
        add("head", "split", 1)
        add("back", "oT")
        add("head", "v")
        add("back", "wo")
    else:
        add("middle", "max")
        add("head", "k")
        add("head", "split", 1)
        add("back", "tok")
        if layer == 2:
            add("back", "sumv")
        add("head", "v")
        add("back", "oT")
        if layer == 2:
            add("head", "coh1")
        add("back", "wo")
    if layer == 1:
        add("middle", "smax", maxima_here, H - 3)
        add("next", "spec")
        add("middle", "smax", H - 3)
        add("back", "yn")
        add("middle", "smax", H - 2)
        add("next", "rank")
        add("back", "yT")
        add("middle", "smax", H - 1)
        add("back", "ffn", 0)
        add("middle", "max")
        add("back", "ffn", 1, FC)
        add("back", "down")
    else:
        add("next", "load")
    return out


def merged(ending, starting):
    whole = order_of(starting[0][0]) if starting else []
    anchors = [("probs", h) for h in range(H)] + [("pv", g) for g in range(NG)] + [("tok", 0), ("oT", 0), ("wo", 0)]
    have = [(what, k) for _, what, k, _ in ending]
    if not all(a in have for a in anchors):
        return ending + starting
    after, rest = {}, list(starting)
    last = None
    for side, what, k in whole:
        if side == "back" and (what, k) in anchors:
            last = (what, k)
        elif rest and rest[0][1:3] == (what, k):
            after.setdefault(last, []).append(rest.pop(0))
    assert not rest
    out = after.get(None, [])
    for step in ending:
        out = out + [step] + after.get(step[1:3], [])
    return out


def cond_resid_kernel(nc, ins, out):
    with ExitStack() as ctx:
        def sb(name, shape, dt=F32):
            return ctx.enter_context(nc.sbuf_tensor(name, shape, dt))

        def sem(name):
            return ctx.enter_context(nc.semaphore(name))

        banks = [ctx.enter_context(nc.psum_tensor(f"bank{i}", [P, 512], F32)) for i in range(8)]
        o_bank = banks[6:8]

        probs = sb("probs", [P, PBUF, TC, S])
        probs_flat = probs[:, :, :, :].rearrange("p h t s -> p (h t s)")

        class Carver:

            def __init__(self, flat):
                self.flat, self.at = flat, 0

            def __call__(self, shape):
                size = int(np.prod(shape[1:]))
                piece = self.flat[0:shape[0], self.at:self.at + size]
                self.at += size
                if len(shape) == 2:
                    return piece
                names = [f"d{i}" for i in range(len(shape) - 1)]
                return piece.rearrange(f"p ({' '.join(names)}) -> p {' '.join(names)}", **dict(zip(names, shape[1:])))

        setup, ffn = Carver(probs_flat), Carver(probs_flat)
        ot_raw = sb("ot_raw", [P, NG, S])
        setup_more = Carver(ot_raw[:, :, :].rearrange("p g s -> p (g s)"))

        ident = sb("ident", [P, P])
        ident_bf = sb("ident_bf", [P, P], BF16)
        below = setup([HC, HC])
        ones = sb("ones", [P, P])
        raw, raw_t, raw_t2 = setup([C, C]), setup([HC, C]), setup([HC, C])
        cond_a = sb("cond_a", [CA, NBATCH])
        cond_w = setup([CA, 10, P])
        we1 = setup([CA, D])
        we2 = setup([P, DC, D])
        be2 = setup([1, D])
        ln_gb = setup([NBATCH, 2, D])
        pe_t = setup([P, DC, S])
        w_basis = sb("w_basis", [P, DC, C])
        w_outb = sb("w_outb", [C, D])
        w_gate, w_hid = sb("w_gate", [P, DC, FF]), sb("w_hid", [P, DC, FF])
        wqkvo1 = sb("wqkvo1", [P, 4, DC, D])
        wqkvo3 = w_hid[:, :, :].rearrange("p a (b d) -> p (a b) d", d=D).rearrange("p (m c) d -> p m c d", c=DC)
        wqkv = {1: wqkvo1, 2: wqkvo1, 3: wqkvo3}
        w_out = {1: wqkvo1[:, 3], 2: w_gate[:, :, 0:D], 3: wqkvo3[:, 3]}
        w_down = sb("w_down", [P, FC, D])
        w_c1 = sb("w_c1", [P, DC, D])
        w_c2 = sb("w_c2", [P, DC, H])
        bqk = sb("bqk", [P, 4])
        bv_rows, bout_rows = sb("bv_rows", [P, D]), sb("bout_rows", [P, D])
        bc2_rows = sb("bc2_rows", [P, H])
        w_mod = sb("w_mod", [CA, 2 * D])
        rms_rows = sb("rms_rows", [P, D])
        mask_q, mask_k = sb("mask_q", [P, TC, S], mybir.dt.uint8), sb("mask_k", [P, TC, S], mybir.dt.uint8)
        big_q, big_k = sb("big_q", [P, TC, S], BF16), sb("big_k", [P, TC, S], BF16)
        some_key = sb("some_key", [P, TC])
        half = sb("half", [P, TC])
        guard = sb("guard", [P, TC])

        xres = sb("xres", [P, NBATCH, TC, D])
        cvec = sb("cvec", [P, NV, NBATCH])

        qs = [sb(f"qs{i}", [P, H, S], F32R) for i in range(2)]
        ks = [sb(f"ks{i}", [P, H, S], F32R) for i in range(2)]
        vp = [sb(f"vp{i}", [P, TC, H, HW]) for i in range(2)]
        coh = [sb(f"coh{i}", [P, TC, H]) for i in range(2)]
        cur_f, cur_b = sb("cur_f", [P, NV]), sb("cur_b", [P, NV])
        x_in, xt_in = sb("x_in", [P, TC, D]), sb("xt_in", [P, DC, S])
        h_spec, h_rank = sb("h_spec", [C, S]), sb("h_rank", [C, S])
        xn = sb("xn", [P, TC, D])
        xt = sb("xt", [P, DC, S])
        qk = sb("qk", [P, 4, S])
        qk_hi, qk_lo = sb("qk_hi", [P, 4, S], F32R), sb("qk_lo", [P, 4, S], F32R)
        rowmax = sb("rowmax", [P, TC, H])
        nm_hi, nm_lo = sb("nm_hi", [H, S], F32R), sb("nm_lo", [H, S], F32R)
        rz = sb("rz", [P, TC, H])
        on = sb("on", [P, TC, D])
        ot = sb("ot", [P, DC, S])
        stat = sb("stat", [P, 3, TC])
        statb = sb("statb", [P, 3, TC])
        y = sb("y", [P, TC, D])
        yn = sb("yn", [P, TC, D])
        yt = sb("yt", [P, DC, S])
        th, act1 = ffn([P, 2, S]), ffn([P, 2, S])
        hm = ffn([P, FC, S])
        c1t = xt_in
        masked = xt_in[:, :, :].bitcast(BF16).rearrange("p a (t s) -> p a t s", t=TC)
        tick = sb("tick", [1, 2])
        zz, ez = sb("zz", [P, TC, H]), sb("ez", [P, TC, H])
        mod_l = sb("mod_l", [CA, P])
        mod_a, mod_s = x_in[:, 0, :], x_in[:, 1, :]

        gj, gj_row = setup_more([HC, C]), setup_more([HC, C])
        gj_c = setup([HC, 4])
        cross, z, m1, inv_a, inv_a_t, inv_c, inv_c_t, inv_b_t = (setup([HC, HC]) for _ in range(8))
        qmat, sgn = setup([C, C]), setup([C, C])
        mtr = sb("mtr", [C, P])
        keys_left = xn
        a1 = setup([P, DC, NBATCH])
        fld = setup_more([NBATCH, 3, D])
        fs = setup([NBATCH, 8])
        fld_t = setup([P, DC, NBATCH])
        th_c = setup([C, NBATCH])

        s_first, s_ld0, s_ld = sem("s_first"), sem("s_ld0"), {n: sem(f"s_ld{n}") for n in LAYERS}
        s_memset = sem("s_memset")
        s_vch, s_pe0, s_act0, s_pool0 = sem("s_vch"), sem("s_pe0"), sem("s_act0"), sem("s_pool0")
        s_setup = sem("s_setup")

        def ev(name, per):
            return Event(sem(name), per)

        x_loaded, h_spec_ok, h_rank_ok, x1_ok = ev("x_loaded", 32), ev("h_spec_ok", 1), ev("h_rank_ok", 1), ev("x1_ok", 1)
        sq1, ms1, inv1, xn_ok = ev("sq1", TC), ev("ms1", 1), ev("inv1", 1), ev("xn_ok", TC)
        y_ok, sq2, ms2, inv2 = ev("y_ok", 1), ev("sq2", TC), ev("ms2", 1), ev("inv2", 1)
        yn_ok, yt_ok, xy_ok = ev("yn_ok", TC), ev("yt_ok", DC), ev("xy_ok", 1)
        th_ok, act1_ok, hm_ok = ev("th_ok", FC), ev("act1_ok", FC), ev("hm_ok", FC)
        c1_ok, zz_ok, ez_ok, coh_ok = ev("c1_ok", DC), ev("zz_ok", 1), ev("ez_ok", 1), ev("coh_ok", 3)
        sumv_ok = ev("sumv_ok", 1)
        rz_coh, on_field, attn2_ok = ev("rz_coh", 1), ev("on_field", TC), ev("attn2_ok", 1)
        rz_some, attn3_ok, sq3, ms3, inv3 = ev("rz_some", 1), ev("attn3_ok", 1), ev("sq3", TC), ev("ms3", 1), ev("inv3", 1)
        mod_full, down_full = ev("mod_full", 1), ev("down_full", 1)
        mod_l_ok, mod_ok, mod_sum, stored = ev("mod_l_ok", 1), ev("mod_ok", 2), ev("mod_sum", 3), ev("stored", 16)

        class Layer:

            def __init__(self, n, before):
                self.n, self.events = n, {}

                def shared(name, per):
                    known = before.events.get(name) if before else None
                    self.events[name] = known.after(NBATCH) if known else ev(name, per)
                    return self.events[name]

                self.cur_f, self.cur_b, self.xt = shared("cur_f", 1), shared("cur_b", 1), shared("xt", DC)
                if n > 1:
                    self.staged = shared("staged", 1)
                self.q, self.k, self.vp = shared("q", 1), shared("k", 1), shared("vp", 1)
                self.qk_hi, self.qk_lo, self.stacked = shared("qk_hi", 2), shared("qk_lo", 2), shared("stacked", 16 * 6)
                self.rowmax, self.nm, self.shifted = shared("rowmax", H), shared("nm", 2), shared("shifted", 32)
                self.probs, self.pv, self.o_raw = shared("probs", H), shared("pv", NG), shared("o_raw", 2)
                self.wo = shared("wo", 1)
                self.rz, self.on, self.ot, self.x_new = shared("rz", TC), shared("on", TC), shared("ot", DC), shared("x_new", 1)

                head = {"spec": (h_spec_ok, 1), "rank": (h_rank_ok, 1), "cond": (x1_ok, 1)} if n == 1 else {}
                head |= {"xT": (self.xt, DC), "q": (self.q, 1), "k": (self.k, 1), "v": (self.vp, 1)}
                if n == 2:
                    head |= {"coh1": (c1_ok, DC), "coh2": (zz_ok, 1)}
                self.head = Ring(sem(f"head_full{n}"), banks[0:2], head)

                middle = {f"s{h}": (self.rowmax, h + 1) for h in range(H)} | {"max": (self.nm, 2)}
                self.middle = Ring(sem(f"middle_full{n}"), banks[2:4], middle)

                back = {f"p{h}": (self.probs, h + 1) for h in range(H)}
                back |= {"tok0": (self.on, 1), "tok1": (self.on, 2), "oT": (self.ot, DC)}
                if n == 1:
                    back |= {"yT": (yt_ok, DC)} | {f"ffn{f}": (hm_ok, f + 1) for f in range(FC)}
                self.back = Ring(sem(f"back_full{n}"), banks[4:6], back)

        lay = {}
        for n in LAYERS:
            lay[n] = Layer(n, lay.get(n - 1))
        L3 = lay[3]

        def run_layers(eng, steps_of):
            steps = {n: steps_of(n) for n in LAYERS}

            def phase(n, b):
                return [(n, what, k, b + AHEAD[side]) for side, what, k in order_of(n) if 0 <= b + AHEAD[side] < NBATCH]

            def run(phase_steps):
                for n, what, k, b in phase_steps:
                    steps[n](what, k, b, b % 2)

            for n in LAYERS:
                for b in range(-3 if n == 1 else LAST_ALONE - NBATCH, FIRST_ALONE):
                    run(merged(phase(n - 1, b + NBATCH), phase(n, b)) if n > 1 and b <= 1 else phase(n, b))
                with eng.Fori(FIRST_ALONE // 2, LAST_ALONE // 2) as j:
                    for par in range(2):
                        for side, what, k in order_of(n):
                            steps[n](what, k, 2 * j + (par + AHEAD[side]), (par + AHEAD[side]) % 2)
                if n == LAYERS[-1]:
                    for b in range(LAST_ALONE, NBATCH + 2):
                        run(phase(n, b))

        def rows(name, n):
            return ins[name].rearrange("(a d) -> a d", a=1).to_broadcast([n, ins[name].shape[0]])

        loads_first = [(raw, "raw"), (ident, "ident"), (below, "below")]
        loads0 = [(raw_t, "raw_t"), (raw_t2, "raw_t2"), (cond_a, "cond_a"),
                  (cond_w, "cond_w"), (we1, "we1"), (we2, "we2"), (be2, "be2"), (ln_gb, "ln_gb"), (pe_t, "pe_t"),
                  (w_basis, "w_basis"), (w_outb, "w_outb"), (mask_q, "mask_q"), (mask_k, "mask_k"),
                  (bqk, "bqk")]
        loads1 = [(wqkvo1, "wqkvo1"), (w_gate, "w_gate"), (w_hid, "w_hid"), (w_down, "w_down"),
                  (w_c1, "w_c1"), (w_c2, "w_c2"), (bv_rows, "bv"), (bout_rows, "bout"), (bc2_rows, "bc2"),
                  (w_mod, "w_mod"), (rms_rows, "rms")]

        def start_layers(eng):
            eng.wait_ge(s_setup, 1)
            eng.wait_ge(s_ld[1], 16 * len(loads1))

        mark = {}

        block = ctx.enter_context(nc.Block())

        @block.vector
        def _(dve):
            count = [0]

            def link(a):
                count[0] += 1
                a.then_inc(s_vch, 1)
                dve.wait_ge(s_vch, count[0])

            def eliminate(name, meanwhile):
                link(dve.tensor_copy(gj[:, HC:C], ident[0:HC, 0:HC]))
                for j in range(HC - 1):
                    part = slice(j, HC + j + 1)
                    link(dve.stream_shuffle(gj_row[:, part], gj[:, part], mask=[j] * 32))
                    link(dve.reciprocal(gj_c[:, 0:1], gj_row[:, j:j + 1]))
                    link(dve.scalar_tensor_tensor(gj_c[:, 1:2], gj[:, j:j + 1], gj_c[:, 0:1], below[:, j:j + 1], ALU.mult, ALU.mult))
                    link(dve.scalar_tensor_tensor(gj[:, part], gj_row[:, part], gj_c[:, 1:2], gj[:, part], ALU.mult, ALU.add))
                    if j in meanwhile:
                        meanwhile[j]()
                link(dve.tensor_tensor(gj_row[:, 0:HC], gj[:, 0:HC], ident[0:HC, 0:HC], ALU.mult))
                link(dve.tensor_reduce(gj_c[:, 2:3], gj_row[:, 0:HC], AX, ALU.add))
                mark[name] = count[0]

            dve.wait_ge(s_first, 16 * len(loads_first))
            dve.wait_ge(s_pe0, 1)
            link(dve.scalar_tensor_tensor(gj[:, 0:HC], ident[0:HC, 0:HC], 1e-4, banks[7][0:HC, 0:HC], ALU.mult, ALU.add))
            link(dve.tensor_copy(cross[:], banks[7][0:HC, HC:C]))
            eliminate("A", {})
            dve.wait_ge(s_pool0, 1)
            link(dve.tensor_scalar(inv_a[:], gj[:, HC:C], gj_c[:, 3:4], None, ALU.mult))
            link(dve.transpose(inv_a_t[:], inv_a[:]))
            mark["inv_a"] = count[0]

            dve.wait_ge(s_ld0, 16 * (len(loads0) + 2))
            dve.wait_ge(s_pe0, 2)
            link(dve.tensor_copy(cvec[:, 0:10, :], banks[4][:, 0:10 * NBATCH].rearrange("p (v b) -> p v b", v=10)))
            dve.wait_ge(s_act0, 1)
            link(dve.scalar_tensor_tensor(th_c[:], th_c[:], 1.0, cond_a[0:C, :], ALU.add, ALU.mult))
            dve.wait_ge(s_memset, 5)
            link(dve.tensor_scalar(cvec[0:C, SILU, :], th_c[:], 0.5, None, ALU.mult))
            link(dve.tensor_scalar(a1[:], banks[5][:, 0:DC * NBATCH].rearrange("p (c b) -> p c b", c=DC), 0.0, None, ALU.max))
            mark["A1"] = count[0]

            dve.wait_ge(s_pe0, 3)
            link(dve.tensor_copy(z[:], banks[1][0:HC, 0:HC]))
            mark["Z"] = count[0]

            link(dve.tensor_copy(ident_bf[:], ident[:]))
            link(dve.tensor_scalar(bqk[:, 0:DC], bqk[:, 0:DC], HD ** -0.5, None, ALU.mult))
            link(dve.tensor_scalar(big_q[:], mask_q[:], BIG, None, ALU.mult))
            link(dve.tensor_scalar(big_k[:], mask_k[:], BIG, None, ALU.mult))
            link(dve.tensor_scalar(keys_left[:], mask_q[:], -1.0, 1.0, ALU.mult, ALU.add))
            link(dve.tensor_reduce(some_key[:], keys_left[:], AX, ALU.add))
            link(dve.reciprocal(stat[:, 0, :], some_key[:]))
            link(dve.tensor_tensor(some_key[:], some_key[:], stat[:, 0, :], ALU.mult))

            dve.wait_ge(s_pe0, 4)
            link(dve.tensor_reduce(fs[:, 0:1], banks[6][0:NBATCH, 0:D], AX, ALU.add))
            link(dve.tensor_scalar(fs[:, 0:1], fs[:, 0:1], -1.0 / D, None, ALU.mult))
            link(dve.tensor_scalar(fld[:, 0, :], banks[6][0:NBATCH, 0:D], fs[:, 0:1], None, ALU.add))
            link(dve.tensor_tensor(fld[:, 1, :], fld[:, 0, :], fld[:, 0, :], ALU.mult))
            link(dve.tensor_reduce(fs[:, 1:2], fld[:, 1, :], AX, ALU.add))
            link(dve.tensor_scalar(fs[:, 2:3], fs[:, 1:2], 1.0 / D, 1e-5, ALU.mult, ALU.add))
            mark["var"] = count[0]

            def field_normed():
                dve.wait_ge(s_pool0, 2)
                link(dve.tensor_scalar(fld[:, 0, :], fld[:, 0, :], fs[:, 3:4], None, ALU.mult))
                link(dve.tensor_tensor(fld[:, 0, :], fld[:, 0, :], ln_gb[:, 0, :], ALU.mult))
                link(dve.tensor_tensor(fld[:, 0, :], fld[:, 0, :], ln_gb[:, 1, :], ALU.add))
                mark["F"] = count[0]

            def field_turned():
                dve.wait_ge(s_pe0, 6)
                link(dve.tensor_copy(fld_t[:], banks[7][:, 0:DC * NBATCH].rearrange("p (c b) -> p c b", c=DC)))
                mark["FT"] = count[0]

            def field_maximum():
                dve.wait_ge(s_pe0, 7)
                link(dve.tensor_reduce(fs[:, 4:5], banks[6][0:NBATCH, 0:S], AX, ALU.max))
                link(dve.tensor_scalar(fs[:, 5:6], fs[:, 4:5], -1.0, None, ALU.mult))
                mark["E"] = count[0]

            def field_shares():
                dve.wait_ge(s_act0, 2)
                link(dve.reciprocal(fs[:, 7:8], fs[:, 6:7]))
                link(dve.tensor_scalar(fld[:, 1, :], fld[:, 2, :], fs[:, 7:8], FI, ALU.mult, ALU.mult))
                mark["FA"] = count[0]

            def field_vectors():
                dve.wait_ge(s_pe0, 8)
                link(dve.tensor_copy(cvec[:, FIELD:FIELD + TC, :], banks[7][:, 0:TC * NBATCH].rearrange("p (t b) -> p t b", t=TC)))

            dve.wait_ge(s_pe0, 5)
            link(dve.scalar_tensor_tensor(gj[:, 0:HC], ident[0:HC, 0:HC], 1e-4, banks[7][0:HC, C:C + HC], ALU.mult, ALU.add))
            link(dve.scalar_tensor_tensor(gj[:, 0:HC], banks[2][0:HC, 0:HC], -1.0, gj[:, 0:HC], ALU.mult, ALU.add))
            link(dve.tensor_scalar(m1[:], banks[3][0:HC, 0:HC], -1.0, None, ALU.mult))
            eliminate("C", {3: field_normed, 8: field_turned, 14: field_maximum, 20: field_shares, 26: field_vectors})
            dve.wait_ge(s_pool0, 3)
            link(dve.tensor_scalar(inv_c[:], gj[:, HC:C], gj_c[:, 3:4], None, ALU.mult))
            link(dve.transpose(inv_c_t[:], inv_c[:]))
            mark["inv_c"] = count[0]
            dve.wait_ge(s_pe0, 9)
            link(dve.tensor_copy(inv_b_t[:], banks[1][0:HC, 0:HC]))
            mark["inv_b"] = count[0]
            dve.wait_ge(s_pe0, 10)
            link(dve.tensor_copy(qmat[:], banks[2][0:C, 0:C]))
            link(dve.tensor_tensor(sgn[:], qmat[:], raw[:], ALU.mult))
            mark["Q"] = count[0]
            link(dve.memset(mtr[:, C:P], 0.0))
            dve.wait_ge(s_pe0, 11)
            link(dve.tensor_scalar(sgn[:], banks[3][0:C, 0:C], 0.0, 2.0, ALU.is_ge, ALU.mult))
            dve.wait_ge(s_memset, 19)
            dve.scalar_tensor_tensor(mtr[:, 0:C], sgn[:], -1.0, qmat[:], ALU.add, ALU.mult).then_inc(s_setup, 1)

            def steps_of(n):
                L = lay[n]
                hd, md, bk = L.head, L.middle, L.back

                def step(what, k, b, par):
                    if what == "load" and n != 3:
                        dve.wait_ge(L.xt.sem, L.xt.at(b, 0))
                        if n == 2:
                            dve.wait_ge(c1_ok.sem, c1_ok.at(b, 0))
                        dve.tensor_scalar(cur_f[:], cvec[:, :, b], 1.0, None, ALU.mult).then_inc(L.cur_f.sem, 1)
                    if what == "vectors":
                        if n == 1:
                            dve.wait_ge(yt_ok.sem, yt_ok.at(b, 0))
                        dve.tensor_scalar(cur_b[:], cvec[:, :, b], 1.0, None, ALU.mult).then_inc(L.cur_b.sem, 1)
                    if what == "cond":
                        bank = hd.wait_filled(dve, b, "cond")
                        dve.wait_ge(x_loaded.sem, x_loaded.at(b, 32))
                        dve.tensor_tensor(xres[:, b, :, :], bank[:, :].rearrange("p (t d) -> p t d", t=TC), x_in[:], ALU.add)\
                            .then_inc(x1_ok.sem, 1)
                    if what == "xn":
                        dve.wait_ge(inv1.sem, inv1.at(b, 1))
                        for t in range(TC):
                            dve.tensor_scalar(xn[:, t, :], xres[:, b, t, :], stat[:, 2, t:t + 1], None, ALU.mult).then_inc(xn_ok.sem, 1)
                    if what == "stage":
                        dve.wait_ge(L.xt.sem, L.xt.at(b, 0))
                        dve.wait_ge(L.x_new.sem, lay[n - 1].x_new.at(b, 1))
                        dve.tensor_scalar(xn[:], xres[:, b, :, :], 1.0, None, ALU.mult).then_inc(L.staged.sem, 1)
                    if what == "k":
                        dve.wait_ge(L.qk_lo.sem, L.qk_lo.at(b, 0))
                        bank = hd.wait_filled(dve, b, "k")
                        if n == 2:
                            for c in range(DC):
                                a = dve.tensor_scalar(qk[:, DC + c, :], bank[:, c * S:(c + 1) * S], bqk[:, DC + c:DC + c + 1], None, ALU.add)
                        else:
                            a = dve.tensor_copy(qk[:, DC:2 * DC, :], bank[:, :].rearrange("p (c s) -> p c s", c=DC))
                        a.then_inc(L.k.sem, 1)
                    if what == "split":
                        part = slice(DC * k, DC * (k + 1))
                        stands = (L.q, L.k)[k]
                        dve.wait_ge(stands.sem, stands.at(b, 1))
                        if k == 0:
                            dve.wait_ge(L.stacked.sem, L.stacked.at(b, 0))
                        if k == 0 and n == 1 and not (isinstance(b, int) and b < 2):
                            dve.wait_ge(L.pv.sem, L.pv.at(b - 1, 0))
                        dve.tensor_copy(qk_hi[:, part, :], qk[:, part, :]).then_inc(L.qk_hi.sem, 1)
                    if what == "v" and n == 2:
                        if not (isinstance(b, int) and b < 2 and n == 1):
                            dve.wait_ge(L.pv.sem, L.pv.at(b - 1, 0))
                        bank = hd.wait_filled(dve, b, "v")
                        for t in range(TC):
                            a = dve.tensor_tensor(vp[par][:, t, :, 0:HD], bank[:, t * D:(t + 1) * D].rearrange("p (h d) -> p h d", h=H),
                                                  bv_rows[:, :].rearrange("p (h d) -> p h d", h=H), ALU.add)
                        a.then_inc(L.vp.sem, 1)
                    if what == "coh2":
                        bank = hd.wait_filled(dve, b, "coh2")
                        for t in range(TC):
                            a = dve.tensor_tensor(zz[:, t, :], bank[:, t * H:(t + 1) * H], bc2_rows[:], ALU.add)
                        a.then_inc(zz_ok.sem, 1)
                    if what == "coh3":
                        dve.wait_ge(ez_ok.sem, ez_ok.at(b, 1))
                        dve.tensor_scalar(coh[par][:], ez[:], 1e-8, 1.0 + 1e-8, ALU.mult, ALU.add).then_inc(coh_ok.sem, 1)
                        dve.wait_ge(coh_ok.sem, coh_ok.at(b, 1))
                        dve.reciprocal(coh[par][:], coh[par][:]).then_inc(coh_ok.sem, 1)
                        dve.wait_ge(coh_ok.sem, coh_ok.at(b, 2))
                        dve.tensor_scalar(coh[par][:], coh[par][:], 1.0 - FI, None, ALU.mult).then_inc(coh_ok.sem, 1)
                    if what == "smax":
                        if n == 3:
                            dve.wait_ge(L.rowmax.sem, L.rowmax.at(b, max(k - 1, 0)))
                        bank = md.wait_filled(dve, b, f"s{k}")
                        if n == 3:
                            dve.memset(tick[:, k % 2:k % 2 + 1], 0.0)
                            for t in range(TC):
                                a = dve.tensor_tensor_reduce(masked[:, k % 2, t, :], bank[:, t * S:(t + 1) * S], big_q[:, t, :], 1.0, 2 * BIG,
                                                             ALU.add, ALU.max, rowmax[:, t, k:k + 1])
                        else:
                            a = dve.tensor_reduce(rowmax[:, :, k:k + 1], bank[:, :].rearrange("p (t s) -> p t s", t=TC), AX, ALU.max)
                        a.then_inc(L.rowmax.sem, 1)
                    if what == "max":
                        bank = md.wait_filled(dve, b, "max")
                        dve.wait_ge(L.shifted.sem, L.shifted.at(b, 0))
                        dve.tensor_scalar(nm_hi[:], bank[0:H, 0:S], -1.0, None, ALU.mult).then_inc(L.nm.sem, 1)
                        dve.wait_ge(L.nm.sem, L.nm.at(b, 1))
                        dve.scalar_tensor_tensor(nm_lo[:], bank[0:H, 0:S], -1.0, nm_hi[:], ALU.mult, ALU.subtract).then_inc(L.nm.sem, 1)
                    if what == "pv" and k % 2 == 1:
                        dve.wait_ge(L.pv.sem, L.pv.at(b, k + 1))
                        dve.tensor_copy(ot_raw[:, k - 1:k + 1, :], o_bank[k // 2][:, :].rearrange("p (g s) -> p g s", g=2)).then_inc(L.o_raw.sem, 1)
                    if what == "tok":
                        grids = []
                        for t in range(TC):
                            grids.append(bk.wait_filled(dve, b, f"tok{t}")[:, :].rearrange("p (h w) -> p h w", w=HW))
                            dve.reciprocal(rz[:, t, :], grids[t][:, :, HD]).then_inc(L.rz.sem, 1)
                        dve.wait_ge(L.rz.sem, L.rz.at(b, TC))
                        if n == 2:
                            dve.tensor_tensor(rz[:], rz[:], coh[par][:], ALU.mult).then_inc(rz_coh.sem, 1)
                            dve.wait_ge(rz_coh.sem, rz_coh.at(b, 1))
                        if n == 3:
                            dve.tensor_tensor(rz[:], rz[:], some_key[:, :].rearrange("p (t a) -> p t a", a=1).to_broadcast([P, TC, H]),
                                              ALU.mult).then_inc(rz_some.sem, 1)
                            dve.wait_ge(rz_some.sem, rz_some.at(b, 1))
                        for t in range(TC):
                            dve.tensor_tensor(on[:, t, :].rearrange("p (h d) -> p h d", h=H), grids[t][:, :, 0:HD],
                                              rz[:, t, :].rearrange("p (h a) -> p h a", a=1).to_broadcast([P, H, HD]), ALU.mult)\
                                .then_inc(L.on.sem, 1)
                        if n == 2:
                            dve.wait_ge(sumv_ok.sem, sumv_ok.at(b, 1))
                            for t in range(TC):
                                dve.wait_ge(L.on.sem, L.on.at(b, t + 1))
                                dve.scalar_tensor_tensor(on[:, t, :], o_bank[0][:, 0:D], cur_b[:, FIELD + t:FIELD + t + 1], on[:, t, :],
                                                         ALU.mult, ALU.add).then_inc(on_field.sem, 1)
                    if what == "wo" and n == 1:
                        bank = o_bank[1]
                        dve.wait_ge(L.wo.sem, L.wo.at(b, 1))
                        dve.wait_ge(xy_ok.sem, xy_ok.at(b, 0))
                        dve.tensor_tensor(y[:], bank[:, :].rearrange("p (t d) -> p t d", t=TC), xres[:, b, :, :], ALU.add).then_inc(y_ok.sem, 1)
                    if what == "wo" and n == 3:
                        dve.wait_ge(L.x_new.sem, L.x_new.at(b, 0))
                        bank = o_bank[1]
                        dve.wait_ge(L.wo.sem, L.wo.at(b, 1))
                        dve.tensor_copy(y[:], bank[:, :].rearrange("p (t d) -> p t d", t=TC)).then_inc(attn3_ok.sem, 1)
                    if what == "wo" and n == 2:
                        dve.wait_ge(L.x_new.sem, L.x_new.at(b, 0))
                        bank = o_bank[1]
                        dve.wait_ge(L.wo.sem, L.wo.at(b, 1))
                        dve.tensor_tensor(y[:], bank[:, :].rearrange("p (t d) -> p t d", t=TC),
                                          bout_rows[:, :].rearrange("p (a d) -> p a d", a=1).to_broadcast([P, TC, D]), ALU.add).then_inc(attn2_ok.sem, 1)
                    if what == "yn":
                        dve.wait_ge(inv2.sem, inv2.at(b, 1))
                        for t in range(TC):
                            dve.tensor_scalar(yn[:, t, :], y[:, t, :], statb[:, 2, t:t + 1], None, ALU.mult).then_inc(yn_ok.sem, 1)
                    if what == "ffn":
                        bank = bk.bank(f"ffn{k}")
                        dve.wait_ge(th_ok.sem, th_ok.at(b, k + 1))
                        dve.scalar_tensor_tensor(act1[:, k % 2, :], th[:, k % 2, :], 1.0, bank[:, 0:S], ALU.add, ALU.mult).then_inc(act1_ok.sem, 1)
                        dve.wait_ge(act1_ok.sem, act1_ok.at(b, k + 1))
                        dve.scalar_tensor_tensor(hm[:, k, :], act1[:, k % 2, :], 0.5, bank[:, S:2 * S], ALU.mult, ALU.mult)\
                            .then_inc(hm_ok.sem, 1)
                    if what == "down":
                        bank = o_bank[1]
                        dve.wait_ge(down_full.sem, down_full.at(b, 1))
                        dve.wait_ge(xy_ok.sem, xy_ok.at(b, 1))
                        dve.tensor_tensor(xres[:, b, :, :], bank[:, :].rearrange("p (t d) -> p t d", t=TC), xres[:, b, :, :], ALU.add)\
                            .then_inc(L.x_new.sem, 1)
                    if what == "mod":
                        dve.wait_ge(L.x_new.sem, L.x_new.at(b, 0))
                        bank = o_bank[1]
                        dve.wait_ge(mod_full.sem, mod_full.at(b, 1))
                        dve.scalar_tensor_tensor(mod_a[:], bank[:, D:2 * D], 1.0, rms_rows[:], ALU.add, ALU.mult).then_inc(mod_ok.sem, 1)
                        dve.tensor_copy(mod_s[:], bank[:, 0:D]).then_inc(mod_ok.sem, 1)
                    if what == "resid":
                        dve.wait_ge(mod_ok.sem, mod_ok.at(b, 2))
                        dve.wait_ge(inv3.sem, inv3.at(b, 1))
                        for t in range(TC):
                            dve.scalar_tensor_tensor(y[:, t, :], y[:, t, :], statb[:, 2, t:t + 1], mod_a[:], ALU.mult, ALU.mult).then_inc(mod_sum.sem, 1)

                return step

            start_layers(dve)
            run_layers(dve, steps_of)

        @block.sync
        def _(sp):
            for tile, name in loads_first:
                sp.dma_start(tile[:], ins[name]).then_inc(s_first, 16)
            for tile, name in loads0:
                sp.dma_start(tile[:], ins[name]).then_inc(s_ld0, 16)
            sp.wait_ge(s_memset, 5)
            sp.dma_start(cvec[0:C, SPEC, :], ins["cond_a"][0:C, :]).then_inc(s_ld0, 16)
            sp.dma_start(cvec[0:C, RANK, :], ins["cond_64t"]).then_inc(s_ld0, 16)
            for tile, name in loads1:
                src = ins[name]
                if len(src.shape) == 1:
                    src = rows(name, P)
                sp.dma_start(tile[:], src).then_inc(s_ld[1], 16)

            def steps_of(n):
                L = lay[n]

                def step(what, k, b, par):
                    if what == "load" and n == 2 and isinstance(b, int) and b == 0:
                        sp.wait_ge(L.vp.sem, L.vp.at(0, 0))
                        sp.dma_start(wqkvo1[:, 0:3], ins["wqkvo2"][:, 0:3]).then_inc(s_ld[2], 16)
                    if what == "vectors" and n == 2 and isinstance(b, int) and b == 0:
                        sp.wait_ge(hm_ok.sem, hm_ok.at(NBATCH, 0))
                        sp.dma_start(w_out[2], ins["wqkvo2"][:, 3]).then_inc(s_ld[3], 16)
                        sp.dma_start(wqkvo3, ins["wqkvo3"]).then_inc(s_ld[3], 16)
                    if what == "load" and n == 1:
                        sp.wait_ge(x1_ok.sem, x1_ok.at(b, 0))
                        sp.wait_ge(s_memset, 1)
                        sp.dma_start(x_in[:], ins["x"][b].rearrange("(t p) d -> p t d", p=P)).then_inc(x_loaded.sem, 16)
                        sp.dma_start(xt_in[:], ins["x_t"][b]).then_inc(x_loaded.sem, 16)
                    if what == "split":
                        def stack(dst, part, first, row):
                            sp.dma_start(dst[HD * row:HD * (row + 1), :, :].bitcast(F32),
                                         part[:, first:first + DC, :].bitcast(F32)).then_inc(L.stacked.sem, 16)

                        if k == 0:
                            if n == 1:
                                sp.wait_ge(L.qk_hi.sem, L.qk_hi.at(b, 1))
                            else:
                                sp.wait_ge(L.o_raw.sem, L.o_raw.at(b - 2, 2))
                            stack(qs[par], qk_hi, 0, 0)
                            stack(qs[par], qk_hi, 0, 2)
                            sp.wait_ge(L.qk_lo.sem, L.qk_lo.at(b, 1))
                            stack(qs[par], qk_lo, 0, 1)
                        else:
                            sp.wait_ge(L.qk_hi.sem, L.qk_hi.at(b, 2))
                            stack(ks[par], qk_hi, DC, 0)
                            stack(ks[par], qk_hi, DC, 1)
                            sp.wait_ge(L.qk_lo.sem, L.qk_lo.at(b, 2))
                            stack(ks[par], qk_lo, DC, 2)
                    if what == "max":
                        sp.wait_ge(L.nm.sem, L.nm.at(b, 2))
                        for r, part in enumerate((nm_hi, nm_lo)):
                            sp.dma_start(qs[par][SHIFT + r:SHIFT + r + 1, :, :].bitcast(F32),
                                         part[:, :].bitcast(F32)).then_inc(L.shifted.sem, 16)
                    if what == "resid":
                        sp.wait_ge(L3.x_new.sem, L3.x_new.at(b, 1))
                        sp.wait_ge(s_setup, 1)
                        sp.dma_start(out[b].rearrange("(t p) d -> p t d", p=P), xres[:, b, :, :]).then_inc(stored.sem, 16)

                return step

            run_layers(sp, steps_of)
            sp.wait_ge(stored.sem, 16 * NBATCH)

        @block.gpsimd
        def _(pool):
            clears = [(ones[:], 1.0), (half[:], -0.5), (guard[:], 1e-6), (cvec[:], 0.0), (cvec[C:CA, SILU, :], 1.0)]
            for i in range(2):
                clears += [(qs[i][32:64, :, :].bitcast(F32), 0.0), (qs[i][64:96, :, :].bitcast(F32), 0.0),
                           (ks[i][32:64, :, :].bitcast(F32), 0.0), (ks[i][64:96, :, :].bitcast(F32), 0.0),
                           (ks[i][96:98, :, :].bitcast(F32), 1.0), (vp[i][:, :, :, HD:HW], 0.0), (vp[i][:, :, :, HD:HD + 1], 1.0)]
            assert len(clears) == 19
            for k, (tile, value) in enumerate(clears):
                if k:
                    pool.wait_ge(s_memset, k)
                if k == len(clears) - 4:
                    pool.wait_ge(s_vch, mark["A"])
                    pool.tensor_tensor(gj_c[:, 3:4], gj_c[:, 2:3], half[0:HC, 0:1], ALU.pow).then_inc(s_pool0, 1)
                pool.memset(tile, value).then_inc(s_memset, 1)
            pool.wait_ge(s_memset, len(clears))

            pool.wait_ge(s_vch, mark["var"])
            pool.tensor_tensor(fs[:, 3:4], fs[:, 2:3], half[0:NBATCH, 0:1], ALU.pow).then_inc(s_pool0, 1)
            pool.wait_ge(s_vch, mark["C"])
            pool.tensor_tensor(gj_c[:, 3:4], gj_c[:, 2:3], half[0:HC, 0:1], ALU.pow).then_inc(s_pool0, 1)

            def steps_of(n):
                L = lay[n]

                def step(what, k, b, par):
                    if what == "squares" and n == 1:
                        rsqrt(b, stat, sq1, ms1, inv1)
                    if what == "split":
                        part = slice(DC * k, DC * (k + 1))
                        pool.wait_ge(L.qk_hi.sem, L.qk_hi.at(b, k + 1))
                        if k == 0:
                            pool.wait_ge(L.stacked.sem, L.stacked.at(b, 0))
                        pool.tensor_tensor(qk_lo[:, part, :], qk[:, part, :], qk_hi[:, part, :], ALU.subtract).then_inc(L.qk_lo.sem, 1)
                    if what == "yn":
                        rsqrt(b, statb, sq2, ms2, inv2)
                        pool.tensor_tensor(xres[:, b, :, :], xres[:, b, :, :], y[:], ALU.add).then_inc(xy_ok.sem, 1)
                    if what == "wo" and n == 2:
                        pool.wait_ge(attn2_ok.sem, attn2_ok.at(b, 1))
                        pool.tensor_tensor(xres[:, b, :, :], xres[:, b, :, :], y[:], ALU.add).then_inc(L.x_new.sem, 1)
                    if what == "resid":
                        pool.wait_ge(mod_sum.sem, mod_sum.at(b, 2))
                        pool.tensor_tensor(y[:], y[:], mod_s[:, :].rearrange("p (a d) -> p a d", a=1).to_broadcast([P, TC, D]), ALU.add)\
                            .then_inc(mod_sum.sem, 1)
                        pool.wait_ge(mod_sum.sem, mod_sum.at(b, 3))
                        pool.tensor_tensor(xres[:, b, :, :], xres[:, b, :, :], y[:], ALU.add).then_inc(L.x_new.sem, 1)
                    if what == "squares" and n == 3:
                        rsqrt(b, statb, sq3, ms3, inv3)
                    if what == "vectors" and n == 3:
                        pool.wait_ge(mod_ok.sem, mod_ok.at(b, 0))
                        pool.wait_ge(L.cur_b.sem, L.cur_b.at(b, 1))
                        pool.tensor_tensor(mod_l[:], ones[0:CA, :], cur_b[0:CA, SILU:SILU + 1].to_broadcast([CA, P]), ALU.mult).then_inc(mod_l_ok.sem, 1)

                def rsqrt(b, st, sq, ms, inv):
                    pool.wait_ge(sq.sem, sq.at(b, TC))
                    pool.tensor_tensor(st[:, 1, :], st[:, 0, :], guard[:], ALU.add).then_inc(ms.sem, 1)
                    pool.wait_ge(ms.sem, ms.at(b, 1))
                    pool.tensor_tensor(st[:, 2, :], st[:, 1, :], half[:], ALU.pow).then_inc(inv.sem, 1)

                return step

            start_layers(pool)
            run_layers(pool, steps_of)

        @block.scalar
        def _(act):
            act.wait_ge(s_ld0, 16 * (len(loads0) + 2))
            act.activation(th_c[:], cond_a[0:C, :], ACT.Tanh, scale=0.5).then_inc(s_act0, 1)
            act.wait_ge(s_vch, mark["E"])
            act.activation(fld[:, 2, :], banks[6][0:NBATCH, 0:S], ACT.Exp, bias=fs[:, 5:6],
                           accum_out=fs[:, 6:7]).then_inc(s_act0, 1)

            def steps_of(n):
                L = lay[n]
                hd, md, bk = L.head, L.middle, L.back

                def step(what, k, b, par):
                    if what == "spec":
                        t = hd.wait_filled(act, b, "spec")
                        act.wait_ge(L.cur_f.sem, L.cur_f.at(b, 1))
                        act.activation(h_spec[:], t[0:C, 0:S], ACT.Identity, scale=cur_f[0:C, SPEC:SPEC + 1]).then_inc(h_spec_ok.sem, 1)
                    if what == "rank":
                        t = hd.wait_filled(act, b, "rank")
                        act.activation(h_rank[:], t[0:C, 0:S], ACT.Identity, scale=cur_f[0:C, RANK:RANK + 1]).then_inc(h_rank_ok.sem, 1)
                    if what == "squares" and n == 1:
                        act.wait_ge(x1_ok.sem, x1_ok.at(b, 1))
                        for t in range(TC):
                            act.activation(xn[:, t, :], xres[:, b, t, :], ACT.Square, scale=D ** -0.5, accum_out=stat[:, 0, t:t + 1]).then_inc(sq1.sem, 1)
                    if what == "xT":
                        bank = hd.wait_filled(act, b, "xT")
                        for c in range(DC):
                            src = bank[:, c * S:(c + 1) * S]
                            if n == 1:
                                a = act.activation(xt[:, c, :], src, ACT.Identity, scale=cur_f[:, G1 + c:G1 + c + 1],
                                                   bias=cur_f[:, B1 + c:B1 + c + 1])
                            else:
                                a = act.copy(xt[:, c, :], src)
                            a.then_inc(L.xt.sem, 1)
                    if what == "q":
                        act.wait_ge(L.qk_lo.sem, L.qk_lo.at(b, 0))
                        bank = hd.wait_filled(act, b, "q")
                        if n == 2:
                            for c in range(DC):
                                a = act.activation(qk[:, c, :], bank[:, c * S:(c + 1) * S], ACT.Identity,
                                                   scale=HD ** -0.5, bias=bqk[:, c:c + 1])
                        else:
                            a = act.activation(qk[:, 0:DC, :], bank[:, :].rearrange("p (c s) -> p c s", c=DC), ACT.Copy, scale=HD ** -0.5)
                        a.then_inc(L.q.sem, 1)
                    if what == "v" and n != 2:
                        if not (isinstance(b, int) and b < 2 and n == 1):
                            act.wait_ge(L.pv.sem, L.pv.at(b - 1, 0))
                        if n == 3 and isinstance(b, int) and b < 2:
                            act.wait_ge(sumv_ok.sem, sumv_ok.at(NBATCH - 2 + b, 1))
                        bank = hd.wait_filled(act, b, "v")
                        act.copy(vp[par][:, :, :, 0:HD], bank[:, :].rearrange("p (t h d) -> p t h d", t=TC, h=H)).then_inc(L.vp.sem, 1)
                    if what == "coh1":
                        bank = hd.wait_filled(act, b, "coh1")
                        for c in range(DC):
                            act.activation(c1t[:, c, :], bank[:, c * S:(c + 1) * S], ACT.Tanh,
                                           bias=cur_f[:, C1 + c:C1 + c + 1]).then_inc(c1_ok.sem, 1)
                    if what == "coh2":
                        act.wait_ge(zz_ok.sem, zz_ok.at(b, 1))
                        act.wait_ge(coh_ok.sem, coh_ok.at(b, 0))
                        act.activation(ez[:], zz[:], ACT.Exp, scale=-1.0).then_inc(ez_ok.sem, 1)
                    if what == "probs":
                        bank = bk.wait_filled(act, b, f"p{k}")
                        act.wait_ge(L.pv.sem, L.pv.at(b, 0 if k < PBUF else (k - PBUF) // HG + 1))
                        act.activation(probs[:, k % PBUF, :, :], bank[:, :].rearrange("p (c s) -> p c s", c=TC), ACT.Exp)\
                            .then_inc(L.probs.sem, 1)
                    if what == "oT":
                        bank = bk.wait_filled(act, b, "oT")
                        for c in range(DC):
                            act.copy(ot[:, c, :], bank[:, c * S:(c + 1) * S]).then_inc(L.ot.sem, 1)
                    if what == "wo" and n == 1:
                        act.wait_ge(y_ok.sem, y_ok.at(b, 1))
                        for t in range(TC):
                            act.activation(yn[:, t, :], y[:, t, :], ACT.Square, scale=D ** -0.5, accum_out=statb[:, 0, t:t + 1]).then_inc(sq2.sem, 1)
                    if what == "squares" and n == 3:
                        act.wait_ge(attn3_ok.sem, attn3_ok.at(b, 1))
                        for t in range(TC):
                            act.activation(yn[:, t, :], y[:, t, :], ACT.Square, scale=D ** -0.5, accum_out=statb[:, 0, t:t + 1]).then_inc(sq3.sem, 1)
                    if what == "yT":
                        bank = bk.wait_filled(act, b, "yT")
                        for c in range(DC):
                            act.activation(yt[:, c, :], bank[:, c * S:(c + 1) * S], ACT.Identity, scale=cur_b[:, G2 + c:G2 + c + 1],
                                           bias=cur_b[:, B2 + c:B2 + c + 1]).then_inc(yt_ok.sem, 1)
                    if what == "ffn":
                        bank = bk.wait_filled(act, b, f"ffn{k}")
                        act.wait_ge(act1_ok.sem, act1_ok.at(b, max(k - 1, 0)))
                        act.activation(th[:, k % 2, :], bank[:, 0:S], ACT.Tanh, scale=0.5).then_inc(th_ok.sem, 1)

                return step

            start_layers(act)
            run_layers(act, steps_of)

        @block.tensor
        def _(pe):
            pe.wait_ge(s_first, 16 * len(loads_first))
            pe.matmul(banks[7][0:HC, 0:C], raw[:, 0:HC], raw[:], start=True, stop=True)
            pe.matmul(banks[7][0:HC, C:C + HC], raw[:, HC:C], raw[:, HC:C], start=True, stop=True).then_inc(s_pe0, 1)
            pe.wait_ge(s_ld0, 16 * (len(loads0) + 2))
            for v in range(10):
                pe.matmul(banks[4][:, v * NBATCH:(v + 1) * NBATCH], cond_w[:, v, :], cond_a[:], start=True, stop=True)
            for c in range(DC):
                m = pe.matmul(banks[5][:, c * NBATCH:(c + 1) * NBATCH], we1[:, c * P:(c + 1) * P], cond_a[:], start=True, stop=True)
            m.then_inc(s_pe0, 1)
            pe.wait_ge(s_vch, mark["inv_a"])
            pe.matmul(banks[1][0:HC, 0:HC], inv_a_t[:], cross[:], start=True, stop=True).then_inc(s_pe0, 1)
            pe.wait_ge(s_memset, 1)
            pe.wait_ge(s_vch, mark["A1"])
            for c in range(DC):
                pe.matmul(banks[6][0:NBATCH, 0:D], a1[:, c, :], we2[:, c, :], start=(c == 0), stop=False)
            pe.matmul(banks[6][0:NBATCH, 0:D], ones[0:1, 0:NBATCH], be2[:], start=False, stop=True).then_inc(s_pe0, 1)
            pe.wait_ge(s_vch, mark["Z"])
            pe.matmul(banks[2][0:HC, 0:HC], z[:], z[:], start=True, stop=True)
            pe.matmul(banks[3][0:HC, 0:HC], z[:], inv_a[:], start=True, stop=True).then_inc(s_pe0, 1)
            pe.wait_ge(s_vch, mark["F"])
            for c in range(DC):
                m = pe.transpose(banks[7][:, c * NBATCH:(c + 1) * NBATCH], fld[:, 0, c * P:(c + 1) * P], ident[0:NBATCH, 0:NBATCH])
            m.then_inc(s_pe0, 1)
            pe.wait_ge(s_vch, mark["FT"])
            for c in range(DC):
                m = pe.matmul(banks[6][0:NBATCH, 0:S], fld_t[:, c, :], pe_t[:, c, :], start=(c == 0), stop=(c == DC - 1))
            m.then_inc(s_pe0, 1)
            pe.wait_ge(s_vch, mark["FA"])
            for t in range(TC):
                m = pe.transpose(banks[7][:, t * NBATCH:(t + 1) * NBATCH], fld[:, 1, t * P:(t + 1) * P], ident[0:NBATCH, 0:NBATCH])
            m.then_inc(s_pe0, 1)
            pe.wait_ge(s_vch, mark["inv_c"])
            pe.matmul(banks[1][0:HC, 0:HC], m1[:], inv_c_t[:], start=True, stop=True).then_inc(s_pe0, 1)
            pe.wait_ge(s_vch, mark["inv_b"])
            pe.matmul(banks[2][0:C, 0:HC], raw_t[:], inv_a_t[:], start=True, stop=True)
            pe.matmul(banks[2][0:C, HC:C], raw_t[:], inv_b_t[:], start=True, stop=False)
            pe.matmul(banks[2][0:C, HC:C], raw_t2[:], inv_c_t[:], start=False, stop=True).then_inc(s_pe0, 1)
            pe.wait_ge(s_vch, mark["Q"])
            pe.matmul(banks[3][0:C, 0:C], ones[0:C, 0:C], sgn[:], start=True, stop=True).then_inc(s_pe0, 1)

            def steps_of(n):
                L = lay[n]
                hd, md, bk = L.head, L.middle, L.back
                w = wqkv[n]

                def outputs_first(bank, weights, acts):
                    for c in range(DC):
                        for i in range(DC):
                            m = pe.matmul(bank[:, c * S:(c + 1) * S], weights[:, i, c * P:(c + 1) * P], acts[:, i, :],
                                          start=(i == 0), stop=(i == DC - 1))
                    return m

                def tokens_first(bank, acts, weights, n_in=DC, width=D):
                    for t in range(TC):
                        for i in range(n_in):
                            m = pe.matmul(bank[:, t * width:(t + 1) * width], acts[:, i, t * P:(t + 1) * P], weights[:, i, :],
                                          start=(i == 0), stop=(i == n_in - 1))
                    return m

                def last_product_read(b):
                    if n == 1:
                        pe.wait_ge(L.x_new.sem, L.x_new.at(b, 0))
                    elif isinstance(b, int) and b == 0:
                        if n == 2:
                            pe.wait_ge(L.x_new.sem, L.x_new.at(0, 0))
                        else:
                            pe.wait_ge(attn2_ok.sem, attn2_ok.at(NBATCH, 0))
                    else:
                        done = attn2_ok if n == 2 else attn3_ok
                        pe.wait_ge(done.sem, done.at(b, 0))

                def transposes(bank, src):
                    for c in range(DC):
                        for t in range(TC):
                            m = pe.transpose(bank[:, c * S + t * P:c * S + (t + 1) * P], src[:, t, c * P:(c + 1) * P], ident[:])
                    return m

                def step(what, k, b, par):
                    if what == "spec":
                        pe.wait_ge(x_loaded.sem, x_loaded.at(b, 32))
                        hd.wait_free(pe, b, "spec")
                        for c in range(DC):
                            m = pe.matmul(hd.bank("spec")[0:C, 0:S], w_basis[:, c, :], xt_in[:, c, :], start=(c == 0), stop=(c == DC - 1))
                        m.then_inc(hd.full.sem, 1)
                    if what == "rank":
                        pe.wait_ge(h_spec_ok.sem, h_spec_ok.at(b, 1))
                        hd.wait_free(pe, b, "rank")
                        pe.matmul(hd.bank("rank")[:, 0:S], mtr[:], h_spec[:], start=True, stop=True).then_inc(hd.full.sem, 1)
                    if what == "cond":
                        pe.wait_ge(h_rank_ok.sem, h_rank_ok.at(b, 1))
                        hd.wait_free(pe, b, "cond")
                        for t in range(TC):
                            m = pe.matmul(hd.bank("cond")[:, t * D:(t + 1) * D], h_rank[:, t * P:(t + 1) * P], w_outb[:], start=True, stop=True)
                        m.then_inc(hd.full.sem, 1)
                    if what == "xT":
                        if n == 1:
                            pe.wait_ge(xn_ok.sem, xn_ok.at(b, 2))
                        else:
                            pe.wait_ge(L.staged.sem, L.staged.at(b, 1))
                        if n > 1 and isinstance(b, int) and b == 0:
                            pe.wait_ge(L.k.sem, L.k.at(0, 0))
                            pe.wait_ge(L.vp.sem, L.vp.at(0, 0))
                            if n == 3:
                                pe.wait_ge(zz_ok.sem, zz_ok.at(NBATCH, 0))
                        hd.wait_free(pe, b, "xT")
                        transposes(hd.bank("xT"), xn).then_inc(hd.full.sem, 1)
                    if what in ("q", "k"):
                        pe.wait_ge(L.xt.sem, L.xt.at(b, 2))
                        if n == 2 and isinstance(b, int) and b == 0:
                            pe.wait_ge(s_ld[2], 16)
                        hd.wait_free(pe, b, what)
                        outputs_first(hd.bank(what), w[:, "qk".index(what)], xt).then_inc(hd.full.sem, 1)
                    if what == "v":
                        hd.wait_free(pe, b, "v")
                        tokens_first(hd.bank("v"), xt, w[:, 2]).then_inc(hd.full.sem, 1)
                    if what == "coh1":
                        hd.wait_free(pe, b, "coh1")
                        outputs_first(hd.bank("coh1"), w_c1, xt).then_inc(hd.full.sem, 1)
                    if what == "coh2":
                        pe.wait_ge(c1_ok.sem, c1_ok.at(b, 2))
                        hd.wait_free(pe, b, "coh2")
                        tokens_first(hd.bank("coh2"), c1t, w_c2, width=H).then_inc(hd.full.sem, 1)
                    if what == "smax":
                        if k == 0:
                            pe.wait_ge(L.stacked.sem, L.stacked.at(b, 16 * 6))
                        md.wait_free(pe, b, f"s{k}")
                        bank = md.bank(f"s{k}")
                        for t in range(TC):
                            m = pe.matmul(bank[:, t * S:(t + 1) * S], qs[par][0:SCORE_ROWS, k, t * P:(t + 1) * P], ks[par][0:SCORE_ROWS, k, :],
                                          start=True, stop=True)
                        m.then_inc(md.full.sem, 1)
                    if what == "max":
                        pe.wait_ge(L.rowmax.sem, L.rowmax.at(b, H))
                        md.wait_free(pe, b, "max")
                        for t in range(TC):
                            m = pe.transpose(md.bank("max")[0:H, t * P:(t + 1) * P], rowmax[:, t, :], ident[:])
                        m.then_inc(md.full.sem, 1)
                    if what == "probs":
                        if k == 0:
                            pe.wait_ge(L.shifted.sem, L.shifted.at(b, 32))
                        bk.wait_free(pe, b, f"p{k}")
                        bank = bk.bank(f"p{k}")
                        for c in range(TC):
                            m = pe.matmul(bank[:, c * S:(c + 1) * S], ks[par][0:SHIFTED_ROWS, k, c * P:(c + 1) * P], qs[par][0:SHIFTED_ROWS, k, :],
                                          start=True, stop=(n != 3))
                            if n == 3:
                                m = pe.matmul(bank[:, c * S:(c + 1) * S], ident_bf[:], big_k[:, c, :], start=False, stop=True)
                        m.then_inc(bk.full.sem, 1)
                    if what == "pv":
                        if k == 0:
                            pe.wait_ge(L.vp.sem, L.vp.at(b, 1))
                            pe.wait_ge(L.o_raw.sem, L.o_raw.at(b, 0))
                        if k == 2 and n != 3:
                            last_product_read(b)
                        if k == 2 and n == 3:
                            pe.wait_ge(mod_ok.sem, mod_ok.at(b, 2))
                        pe.wait_ge(L.probs.sem, L.probs.at(b, HG * (k + 1)))
                        for c in range(TC):
                            for i in range(HG):
                                h = HG * k + i
                                m = pe.matmul(o_bank[k // 2][HW * i:HW * (i + 1), (k % 2) * S:(k % 2 + 1) * S], vp[par][:, c, h, :],
                                              probs[:, h % PBUF, c, :], start=(c == 0), stop=(c == TC - 1))
                        m.then_inc(L.pv.sem, 1)
                    if what == "sumv":
                        pe.wait_ge(L.o_raw.sem, L.o_raw.at(b, 1))
                        for c in range(TC):
                            m = pe.matmul(o_bank[0][:, 0:D], ones[:], vp[par][:, c, :, 0:HD], start=(c == 0), stop=(c == TC - 1))
                        m.then_inc(sumv_ok.sem, 1)
                    if what == "tok":
                        pe.wait_ge(L.o_raw.sem, L.o_raw.at(b, 2))
                        for t in range(TC):
                            bk.wait_free(pe, b, f"tok{t}")
                            for g in range(NG):
                                m = pe.transpose(bk.bank(f"tok{t}")[:, g * P:(g + 1) * P], ot_raw[:, g, t * P:(t + 1) * P], ident[:])
                            m.then_inc(bk.full.sem, 1)
                    if what == "oT":
                        done = on_field if n == 2 else L.on
                        pe.wait_ge(done.sem, done.at(b, TC))
                        bk.wait_free(pe, b, "oT")
                        transposes(bk.bank("oT"), on).then_inc(bk.full.sem, 1)
                    if what == "wo":
                        if n == 2 and isinstance(b, int) and b == 0:
                            pe.wait_ge(s_ld[3], 32)
                        for i in range(DC):
                            pe.wait_ge(L.ot.sem, L.ot.at(b, i + 1))
                            for t in range(TC):
                                m = pe.matmul(o_bank[1][:, t * D:(t + 1) * D], ot[:, i, t * P:(t + 1) * P], w_out[n][:, i, :],
                                              start=(i == 0 and t == 0), stop=(i == DC - 1 and t == TC - 1))
                        m.then_inc(L.wo.sem, 1)
                    if what == "yT":
                        pe.wait_ge(yn_ok.sem, yn_ok.at(b, 2))
                        bk.wait_free(pe, b, "yT")
                        transposes(bk.bank("yT"), yn).then_inc(bk.full.sem, 1)
                    if what == "ffn":
                        if k == 0:
                            pe.wait_ge(yt_ok.sem, yt_ok.at(b, 1))
                        bk.wait_free(pe, b, f"ffn{k}")
                        bank = bk.bank(f"ffn{k}")
                        for j, wt in enumerate((w_gate, w_hid)):
                            for c in range(DC):
                                if k == 0 and j == 0 and c == 1:
                                    pe.wait_ge(yt_ok.sem, yt_ok.at(b, 2))
                                m = pe.matmul(bank[:, j * S:(j + 1) * S], wt[:, c, k * P:(k + 1) * P], yt[:, c, :], start=(c == 0), stop=(c == DC - 1))
                        m.then_inc(bk.full.sem, 1)
                    if what == "down":
                        pe.wait_ge(y_ok.sem, y_ok.at(b, 1))
                        for f in range(FC):
                            if f >= FC - 2:
                                pe.wait_ge(hm_ok.sem, hm_ok.at(b, f + 1))
                            for t in range(TC):
                                m = pe.matmul(o_bank[1][:, t * D:(t + 1) * D], hm[:, f, t * P:(t + 1) * P], w_down[:, f, :],
                                              start=(f == 0 and t == 0), stop=(f == FC - 1 and t == TC - 1))
                        m.then_inc(down_full.sem, 1)
                    if what == "mod":
                        pe.wait_ge(mod_l_ok.sem, mod_l_ok.at(b, 1))
                        pe.wait_ge(L.o_raw.sem, L.o_raw.at(b, 0))
                        last_product_read(b)
                        pe.matmul(o_bank[1][:, :], mod_l[:], w_mod[:], start=True, stop=True).then_inc(mod_full.sem, 1)

                return step

            start_layers(pe)
            run_layers(pe, steps_of)


def chunked(a):
    return np.ascontiguousarray(a.reshape(-1, P, a.shape[1]).transpose(1, 0, 2))


def by_dim(a):
    return np.moveaxis(a.reshape(*a.shape[:-1], H // DC, DC, HD), -3, -1).reshape(a.shape)


def position_table():
    pos = np.arange(S, dtype=np.float32)
    inv = np.float32(10000.0) ** np.repeat(np.arange(0, D, 2, dtype=np.float32) / np.float32(D), 2)
    return np.sin(pos[:, None] / inv[None, :]).astype(np.float32)


def layouts(v):
    one = np.ones((1, 1), np.float32)
    with_bias = lambda w, b: np.concatenate([w.T, b[None, :]], 0)
    cond_w = np.concatenate([
        with_bias(v["L1_cond_g1w"], v["L1_cond_g1b"]), with_bias(v["L1_cond_b1w"], v["L1_cond_b1b"]),
        with_bias(v["L1_cond_g2w"], v["L1_cond_g2b"]), with_bias(v["L1_cond_b2w"], v["L1_cond_b2b"]),
        with_bias(v["L2_cond_Wc1"][:, D:], v["L2_cond_bc1"])], 1).reshape(CA, 10, P)
    qkvo = lambda q, k, vv, o: np.stack([chunked(by_dim(q.T)), chunked(by_dim(k.T)), chunked(vv.T), chunked(o.T)], 1)
    w2 = v["L2_cond_Wqkv"].reshape(3, D, D)
    b2 = v["L2_cond_bqkv"].reshape(3, D)
    mask = v["mask_SxS_bk1"]
    return {
        "x": v["x"], "x_t": v["x"].transpose(0, 2, 1).reshape(NBATCH, DC, P, S).transpose(0, 2, 1, 3),
        "ident": np.eye(P, dtype=np.float32), "below": -np.tril(np.ones((HC, HC), np.float32), -1),
        "raw": v["L0_cond_mode_to_rank"], "raw_t": v["L0_cond_mode_to_rank"].T[:HC],
        "raw_t2": v["L0_cond_mode_to_rank"].T[HC:],
        "cond_a": np.concatenate([v["cond_256"].T, np.repeat(one, NBATCH, 1)], 0), "cond_64t": v["cond_64"].T,
        "cond_w": cond_w, "we1": with_bias(v["L2_cond_We1"], v["L2_cond_be1"]), "we2": chunked(v["L2_cond_We2"].T),
        "be2": v["L2_cond_be2"][None, :],
        "ln_gb": np.broadcast_to(np.stack([v["L2_cond_ln_g"], v["L2_cond_ln_b"]])[None], (NBATCH, 2, D)),
        "pe_t": chunked(position_table().T),
        "w_basis": chunked(v["L0_cond_input_basis"].T), "w_outb": v["L0_cond_output_basis"],
        "mask_q": chunked(mask), "mask_k": chunked(mask.T),
        "bqk": np.concatenate([by_dim(b2[0]).reshape(DC, P), by_dim(b2[1]).reshape(DC, P)]).T,
        "wqkvo1": qkvo(v["L1_cond_Wq"], v["L1_cond_Wk"], v["L1_cond_Wv"], v["L1_cond_Wo"]),
        "w_gate": chunked(v["L1_cond_gate_w"].T), "w_hid": chunked(v["L1_cond_hid_w"].T), "w_down": chunked(v["L1_cond_out_w"].T),
        "wqkvo2": qkvo(w2[0], w2[1], w2[2], v["L2_cond_Wout"]),
        "w_c1": chunked(v["L2_cond_Wc1"][:, :D].T), "w_c2": chunked(v["L2_cond_Wc2"].T),
        "bv": b2[2], "bout": v["L2_cond_bout"], "bc2": v["L2_cond_bc2"],
        "wqkvo3": qkvo(v["L3_cond_Wq"], v["L3_cond_Wk"], v["L3_cond_Wv"], v["L3_cond_Wo"]),
        "w_mod": with_bias(v["L3_cond_Wc"], v["L3_cond_bc"]), "rms": v["L3_cond_rms_scale"],
    }


def kernel(**inputs):
    import concourse.bacc as bacc
    from concourse.bass_utils import run_bass_kernel_spmd

    nc = bacc.Bacc("TRN2", target_bir_lowering=False, num_devices=1)
    arrays, ins = {}, {}
    for name, a in layouts({k: np.asarray(a) for k, a in inputs.items()}).items():
        a = np.ascontiguousarray(a)
        arrays[f"in_{name}"] = a
        ins[name] = nc.dram_tensor(f"in_{name}", a.shape, mybir.dt.from_np(a.dtype), kind="ExternalInput").ap()
    out = nc.dram_tensor("out", (NBATCH, S, D), F32, kind="ExternalOutput").ap()
    cond_resid_kernel(nc, ins, out)
    r = run_bass_kernel_spmd(nc, [arrays], core_ids=[0])
    return r.results[0]["out"]
```
